# Optimizing a Trainium2 kernel written in Bass

```python
import numpy as np
import jax
import jax.numpy as jnp

def _softmax(x, axis=-1):
    return jax.nn.softmax(x, axis=axis)

def _gelu(x):
    return jax.nn.gelu(x, approximate=True)

def _silu(x):
    return jax.nn.silu(x)

def _sigmoid(x):
    return jax.nn.sigmoid(x)

def _layernorm(x, axis=-1, eps=1e-05):
    m = jnp.mean(x, axis=axis, keepdims=True)
    v = jnp.var(x, axis=axis, keepdims=True)
    return (x - m) / jnp.sqrt(v + eps)

def _scatter_add(tgt, idx, src, axis=0):
    return tgt.at[idx].add(src)

def _segment_sum(src, seg, n):
    return jax.ops.segment_sum(src, seg, n)
kernel_name = 'mk_flamingo_gated_d2_seqx_r4_8be546'

def setup_inputs(seed: int=0):
    np.random.seed(seed)
    _w = jnp.asarray

    def _rec_inputs():
        import jax
        import jax.numpy as jnp
        _rk = jax.random.key(seed)
        x = -0.0002928 + 1 * jax.random.normal(jax.random.fold_in(_rk, 1), (4, 512, 256), jnp.float32)
        _lenS = 512 - jax.random.randint(jax.random.fold_in(_rk, 7), (4,), 0, max(1, 512 // 4) + 1, jnp.int32)
        _lenS2 = 512 - jax.random.randint(jax.random.fold_in(_rk, 8), (4,), 0, max(1, 512 // 4) + 1, jnp.int32)
        _ctx_1024P = jax.random.normal(jax.random.fold_in(_rk, 11), (4, 16, 256), jnp.float32)
        _ctx_1024c = jax.random.dirichlet(jax.random.fold_in(_rk, 511), 0.3 * jnp.ones((16,), jnp.float32), (4, 512))
        _ctx_1024t = jnp.einsum('bsk,bkd->bsd', _ctx_1024c, _ctx_1024P)
        _ctx_1024t = _ctx_1024t * jax.lax.rsqrt(jnp.mean(jnp.square(_ctx_1024t)) + 1e-12) * 0.953939
        ctx_1024 = -1.39393e-06 + 0.999914 * (_ctx_1024t + 0.3 * jax.random.normal(jax.random.fold_in(_rk, 611), (4, 512, 256), jnp.float32))
        _validS = jnp.arange(512)[None, :] < _lenS[:, None]
        _validS2 = jnp.arange(512)[None, :] < _lenS2[:, None]
        _causal = jnp.tril(jnp.ones((512, 512), dtype=bool))
        mask_BxS2_bf1 = jnp.ones((4, 512), dtype=bool)
        _g = jax.random.normal(jax.random.fold_in(_rk, 9001), (2, 2), jnp.float32)
        _g = jnp.sign(_g) * jnp.maximum(jnp.abs(_g), 1.0) + (_g == 0) * 1.0
        g_xattn = _g[0]
        g_ffn = _g[1]
        return (x, ctx_1024, mask_BxS2_bf1, g_xattn, g_ffn)
    x, ctx_1024, mask_BxS2_bf1, g_xattn, g_ffn = _rec_inputs()

    def _L0_xattn_setup():
        import jax, jax.numpy as jnp
        import numpy as np
        DIM = 256
        HEADS = 16
        HEAD_DIM = DIM // HEADS
        ROPE_BASE = 10000.0

        def _rope_cos_sin(seq_len, head_dim, dtype=jnp.float32):
            inv_freq = 1.0 / ROPE_BASE ** (jnp.arange(0, head_dim, 2, dtype=jnp.float32) / head_dim)
            t = jnp.arange(seq_len, dtype=jnp.float32)
            freqs = jnp.outer(t, inv_freq)
            emb = jnp.concatenate([freqs, freqs], axis=-1)
            return (jnp.cos(emb).astype(dtype), jnp.sin(emb).astype(dtype))

        def _rotate_half(x):
            x1, x2 = jnp.split(x, 2, axis=-1)
            return jnp.concatenate([-x2, x1], axis=-1)

        def _apply_rope(x, cos, sin):
            return x * cos[None, None, :, :] + _rotate_half(x) * sin[None, None, :, :]
        key = jax.random.key(seed)
        ks = jax.random.split(key, 10)
        B, L, K = (2, 512, 512)
        s = 1.0 / np.sqrt(DIM)
        inp = {'target': jax.random.normal(ks[0], (B, L, DIM), jnp.float32), 'context': jax.random.normal(ks[1], (B, K, DIM), jnp.float32), 'target_mask': jnp.ones((B, L), dtype=bool), 'context_mask': jnp.ones((B, K), dtype=bool), 'Wq': jax.random.normal(ks[2], (DIM, DIM), jnp.float32) * s, 'bq': jnp.zeros((DIM,), jnp.float32), 'Wk': jax.random.normal(ks[3], (DIM, DIM), jnp.float32) * s, 'bk': jnp.zeros((DIM,), jnp.float32), 'Wv': jax.random.normal(ks[4], (DIM, DIM), jnp.float32) * s, 'bv': jnp.zeros((DIM,), jnp.float32), 'Wp': jax.random.normal(ks[5], (DIM, DIM), jnp.float32) * s, 'bp': jnp.zeros((DIM,), jnp.float32)}
        return inp
    _L0_xattn_all = _L0_xattn_setup()
    _L0_xattn_in = {k: v for k, v in _L0_xattn_all.items() if k in ('Wq', 'bq', 'Wk', 'bk', 'Wv', 'bv', 'Wp', 'bp')}
    del _L0_xattn_all

    def _L0_ffn_setup():
        import jax, jax.numpy as jnp
        import numpy as np
        H = 256
        I = 128
        E = 8
        K = 2
        SI = I * 2
        B, S = (2, 256)

        def _mlp(x, gw, uw, dw):
            return jax.nn.silu(x @ gw.T) * (x @ uw.T) @ dw.T
        key = jax.random.key(seed)
        ks = jax.random.split(key, 9)
        s = 0.02
        return {'x': jax.random.normal(ks[0], (B, S, H), jnp.float32), 'gate_w': jax.random.normal(ks[1], (E, H), jnp.float32) * s, 'lb_bias': jnp.zeros((E,), jnp.float32), 'expert_gate_w': jax.random.normal(ks[2], (E, I, H), jnp.float32) * s, 'expert_up_w': jax.random.normal(ks[3], (E, I, H), jnp.float32) * s, 'expert_down_w': jax.random.normal(ks[4], (E, H, I), jnp.float32) * s, 'shared_gate_w': jax.random.normal(ks[5], (SI, H), jnp.float32) * s, 'shared_up_w': jax.random.normal(ks[6], (SI, H), jnp.float32) * s, 'shared_down_w': jax.random.normal(ks[7], (H, SI), jnp.float32) * s}
    _L0_ffn_all = _L0_ffn_setup()
    _L0_ffn_in = {k: v for k, v in _L0_ffn_all.items() if k in ('gate_w', 'lb_bias', 'expert_gate_w', 'expert_up_w', 'expert_down_w', 'shared_gate_w', 'shared_up_w', 'shared_down_w')}
    del _L0_ffn_all

    def _L1_xattn_setup():
        import jax, jax.numpy as jnp
        import numpy as np
        B, L_ENC, L_DEC, D = (16, 128, 128, 256)
        key = jax.random.key(seed)
        k1, k2, k3, k4, k5, k6 = jax.random.split(key, 6)
        encoder_hc = jax.random.normal(k1, (B, L_ENC, D), dtype=jnp.float32)
        decoder_hq = jax.random.normal(k2, (B, L_DEC, D), dtype=jnp.float32)
        w_sim = jax.random.normal(k3, (3 * D,), dtype=jnp.float32) * 0.02
        b_sim = jax.random.normal(k4, (1,), dtype=jnp.float32) * 0.02
        W_qv = jax.random.normal(k5, (4 * D, D), dtype=jnp.float32) * 0.02
        b_qv = jax.random.normal(k6, (D,), dtype=jnp.float32) * 0.02
        return {'encoder_hc': encoder_hc, 'decoder_hq': decoder_hq, 'w_sim': w_sim, 'b_sim': b_sim, 'W_qv': W_qv, 'b_qv': b_qv}
    _L1_xattn_all = _L1_xattn_setup()
    _L1_xattn_in = {k: v for k, v in _L1_xattn_all.items() if k in ('w_sim', 'b_sim', 'W_qv', 'b_qv')}
    del _L1_xattn_all

    def _L1_ffn_setup():
        import jax, jax.numpy as jnp
        import numpy as np
        HIDDEN = 256
        INNER = 1024

        def _weight_quant(w):
            scale = 1.0 / jnp.clip(jnp.mean(jnp.abs(w)), 1e-05)
            wq = jnp.clip(jnp.round(w * scale), -1.0, 1.0) / scale
            return w + jax.lax.stop_gradient(wq - w)

        def _act_quant(x):
            scale = 127.0 / jnp.clip(jnp.max(jnp.abs(x), axis=-1, keepdims=True), 1e-05)
            xq = jnp.clip(jnp.round(x * scale), -128.0, 127.0) / scale
            return x + jax.lax.stop_gradient(xq - x)

        def _bitlinear(x, w):
            return jnp.einsum('bsi,oi->bso', _act_quant(x), _weight_quant(w))
        key = jax.random.key(seed)
        k0, k1, k2, k3 = jax.random.split(key, 4)
        x = jax.random.normal(k0, (4, 512, HIDDEN), dtype=jnp.float32)
        w_gate = jax.random.normal(k1, (INNER, HIDDEN), dtype=jnp.float32) / np.sqrt(HIDDEN)
        w_up = jax.random.normal(k2, (INNER, HIDDEN), dtype=jnp.float32) / np.sqrt(HIDDEN)
        w_down = jax.random.normal(k3, (HIDDEN, INNER), dtype=jnp.float32) / np.sqrt(INNER)
        return {'x': x, 'w_gate': w_gate, 'w_up': w_up, 'w_down': w_down}
    _L1_ffn_all = _L1_ffn_setup()
    _L1_ffn_in = {k: v for k, v in _L1_ffn_all.items() if k in ('w_gate', 'w_up', 'w_down')}
    del _L1_ffn_all
    return {'x': x, 'ctx_1024': ctx_1024, 'mask_BxS2_bf1': mask_BxS2_bf1, 'g_xattn': g_xattn, 'g_ffn': g_ffn, 'L0_xattn_Wq': _L0_xattn_in['Wq'], 'L0_xattn_bq': _L0_xattn_in['bq'], 'L0_xattn_Wk': _L0_xattn_in['Wk'], 'L0_xattn_bk': _L0_xattn_in['bk'], 'L0_xattn_Wv': _L0_xattn_in['Wv'], 'L0_xattn_bv': _L0_xattn_in['bv'], 'L0_xattn_Wp': _L0_xattn_in['Wp'], 'L0_xattn_bp': _L0_xattn_in['bp'], 'L0_ffn_gate_w': _L0_ffn_in['gate_w'], 'L0_ffn_lb_bias': _L0_ffn_in['lb_bias'], 'L0_ffn_expert_gate_w': _L0_ffn_in['expert_gate_w'], 'L0_ffn_expert_up_w': _L0_ffn_in['expert_up_w'], 'L0_ffn_expert_down_w': _L0_ffn_in['expert_down_w'], 'L0_ffn_shared_gate_w': _L0_ffn_in['shared_gate_w'], 'L0_ffn_shared_up_w': _L0_ffn_in['shared_up_w'], 'L0_ffn_shared_down_w': _L0_ffn_in['shared_down_w'], 'L1_xattn_w_sim': _L1_xattn_in['w_sim'], 'L1_xattn_b_sim': _L1_xattn_in['b_sim'], 'L1_xattn_W_qv': _L1_xattn_in['W_qv'], 'L1_xattn_b_qv': _L1_xattn_in['b_qv'], 'L1_ffn_w_gate': _L1_ffn_in['w_gate'], 'L1_ffn_w_up': _L1_ffn_in['w_up'], 'L1_ffn_w_down': _L1_ffn_in['w_down']}

def reference(x, ctx_1024, mask_BxS2_bf1, g_xattn, g_ffn, L0_xattn_Wq, L0_xattn_bq, L0_xattn_Wk, L0_xattn_bk, L0_xattn_Wv, L0_xattn_bv, L0_xattn_Wp, L0_xattn_bp, L0_ffn_gate_w, L0_ffn_lb_bias, L0_ffn_expert_gate_w, L0_ffn_expert_up_w, L0_ffn_expert_down_w, L0_ffn_shared_gate_w, L0_ffn_shared_up_w, L0_ffn_shared_down_w, L1_xattn_w_sim, L1_xattn_b_sim, L1_xattn_W_qv, L1_xattn_b_qv, L1_ffn_w_gate, L1_ffn_w_up, L1_ffn_w_down):
    import jax
    import jax.numpy as jnp

    def _L0_xattn_ref(target, context, target_mask, context_mask, Wq, bq, Wk, bk, Wv, bv, Wp, bp):
        import jax, jax.numpy as jnp
        import numpy as np
        DIM = 256
        HEADS = 16
        HEAD_DIM = DIM // HEADS
        ROPE_BASE = 10000.0

        def _rope_cos_sin(seq_len, head_dim, dtype=jnp.float32):
            inv_freq = 1.0 / ROPE_BASE ** (jnp.arange(0, head_dim, 2, dtype=jnp.float32) / head_dim)
            t = jnp.arange(seq_len, dtype=jnp.float32)
            freqs = jnp.outer(t, inv_freq)
            emb = jnp.concatenate([freqs, freqs], axis=-1)
            return (jnp.cos(emb).astype(dtype), jnp.sin(emb).astype(dtype))

        def _rotate_half(x):
            x1, x2 = jnp.split(x, 2, axis=-1)
            return jnp.concatenate([-x2, x1], axis=-1)

        def _apply_rope(x, cos, sin):
            return x * cos[None, None, :, :] + _rotate_half(x) * sin[None, None, :, :]
        B, L, C = target.shape
        K = context.shape[1]
        H, D = (HEADS, HEAD_DIM)
        q = (target @ Wq.T + bq).reshape(B, L, H, D).transpose(0, 2, 1, 3)
        k = (context @ Wk.T + bk).reshape(B, K, H, D).transpose(0, 2, 1, 3)
        v = (context @ Wv.T + bv).reshape(B, K, H, D).transpose(0, 2, 1, 3)
        cos_q, sin_q = _rope_cos_sin(L, D)
        cos_k, sin_k = _rope_cos_sin(K, D)
        q = _apply_rope(q, cos_q, sin_q)
        k = _apply_rope(k, cos_k, sin_k)
        scale = D ** (-0.5)
        attn = jnp.einsum('bhld,bhkd->bhlk', q, k) * scale
        attn = jnp.where(context_mask[:, None, None, :], attn, -jnp.inf)
        attn = jax.nn.softmax(attn, axis=-1)
        x = jnp.einsum('bhlk,bhkd->bhld', attn, v)
        x = x.transpose(0, 2, 1, 3).reshape(B, L, C)
        x = x @ Wp.T + bp
        x = x * target_mask[:, :, None].astype(x.dtype)
        return x

    def _L0_ffn_ref(x, gate_w, lb_bias, expert_gate_w, expert_up_w, expert_down_w, shared_gate_w, shared_up_w, shared_down_w):
        import jax, jax.numpy as jnp
        import numpy as np
        H = 256
        I = 128
        E = 8
        K = 2
        SI = I * 2
        B, S = (2, 256)

        def _mlp(x, gw, uw, dw):
            return jax.nn.silu(x @ gw.T) * (x @ uw.T) @ dw.T
        b, s, h = x.shape
        xf = x.reshape(-1, h)
        logits = xf @ gate_w.T + lb_bias
        scores = jax.nn.sigmoid(logits.astype(jnp.float32))
        topw, topi = jax.lax.top_k(scores, K)
        topw = (topw / (topw.sum(-1, keepdims=True) + 1e-08)).astype(x.dtype)
        out = jnp.zeros_like(xf)
        for e in range(E):
            m = topi == e
            sel = m.any(axis=-1)
            cnt = m.sum()
            wmean = (topw * m).sum() / jnp.maximum(cnt, 1).astype(topw.dtype)
            y = _mlp(xf, expert_gate_w[e], expert_up_w[e], expert_down_w[e])
            out = out + jnp.where(sel[:, None], y * wmean, jnp.zeros((), x.dtype))
        out = out.reshape(b, s, h)
        out = out + _mlp(x, shared_gate_w, shared_up_w, shared_down_w)
        return out

    def _L1_xattn_ref(encoder_hc, decoder_hq, w_sim, b_sim, W_qv, b_qv):
        import jax, jax.numpy as jnp
        import numpy as np
        B, L_ENC, L_DEC, D = (16, 128, 128, 256)
        d = encoder_hc.shape[-1]
        w1, w2, w3 = (w_sim[:d], w_sim[d:2 * d], w_sim[2 * d:])
        Sim = (encoder_hc @ w1)[:, :, None] + (decoder_hq @ w2)[:, None, :] + jnp.einsum('bid,bjd->bij', encoder_hc * w3, decoder_hq) + b_sim[0]
        A = jax.nn.softmax(Sim, axis=2)
        hq_hat = jnp.einsum('bij,bjd->bid', A, decoder_hq)
        Batt = jax.nn.softmax(jnp.max(Sim, axis=2), axis=1)
        hc_bar = jnp.einsum('bi,bid->bd', Batt, encoder_hc)[:, None, :]
        hc_hat = jnp.broadcast_to(hc_bar, encoder_hc.shape)
        feats = jnp.concatenate([encoder_hc, hq_hat, encoder_hc * hq_hat, encoder_hc * hc_hat], axis=-1)
        hcq = feats @ W_qv + b_qv
        return hcq

    def _L1_ffn_ref(x, w_gate, w_up, w_down):
        import jax, jax.numpy as jnp
        import numpy as np
        HIDDEN = 256
        INNER = 1024

        def _weight_quant(w):
            scale = 1.0 / jnp.clip(jnp.mean(jnp.abs(w)), 1e-05)
            wq = jnp.clip(jnp.round(w * scale), -1.0, 1.0) / scale
            return w + jax.lax.stop_gradient(wq - w)

        def _act_quant(x):
            scale = 127.0 / jnp.clip(jnp.max(jnp.abs(x), axis=-1, keepdims=True), 1e-05)
            xq = jnp.clip(jnp.round(x * scale), -128.0, 127.0) / scale
            return x + jax.lax.stop_gradient(xq - x)

        def _bitlinear(x, w):
            return jnp.einsum('bsi,oi->bso', _act_quant(x), _weight_quant(w))
        gate = jax.nn.silu(_bitlinear(x, w_gate))
        up = _bitlinear(x, w_up)
        return _bitlinear(gate * up, w_down)
    x = x + jnp.tanh(g_xattn[0]) * _L0_xattn_ref(_layernorm(x, axis=-1), ctx_1024, mask_BxS2_bf1, mask_BxS2_bf1, L0_xattn_Wq, L0_xattn_bq, L0_xattn_Wk, L0_xattn_bk, L0_xattn_Wv, L0_xattn_bv, L0_xattn_Wp, L0_xattn_bp)
    x = x + jnp.tanh(g_ffn[0]) * _L0_ffn_ref(_layernorm(x, axis=-1), L0_ffn_gate_w, L0_ffn_lb_bias, L0_ffn_expert_gate_w, L0_ffn_expert_up_w, L0_ffn_expert_down_w, L0_ffn_shared_gate_w, L0_ffn_shared_up_w, L0_ffn_shared_down_w)
    x = x + jnp.tanh(g_xattn[1]) * _L1_xattn_ref(_layernorm(x, axis=-1), ctx_1024, L1_xattn_w_sim, L1_xattn_b_sim, L1_xattn_W_qv, L1_xattn_b_qv)
    x = x + jnp.tanh(g_ffn[1]) * _L1_ffn_ref(_layernorm(x, axis=-1), L1_ffn_w_gate, L1_ffn_w_up, L1_ffn_w_down)
    return x

_drawn_inputs = setup_inputs


def setup_inputs(seed=0):
    import zlib

    import numpy as np

    out = dict(_drawn_inputs(seed))
    spreads = {'g_ffn': (-1.0, 0.6),
     'L0_xattn_bq': (0.0, 0.631),
     'L0_xattn_bk': (0.0, 0.8),
     'L0_xattn_bv': (0.0, 0.1),
     'L0_xattn_bp': (0.0, 0.1),
     'L0_ffn_lb_bias': (0.0, 0.8)}
    factors = {'L0_ffn_gate_w': 8.0,
     'L0_ffn_expert_gate_w': 8.0,
     'L0_ffn_expert_up_w': 8.0,
     'L0_ffn_expert_down_w': 8.0,
     'L0_ffn_shared_gate_w': 4.703,
     'L0_ffn_shared_up_w': 4.589,
     'L0_ffn_shared_down_w': 4.613,
     'L1_xattn_b_qv': 13.369,
     'L1_xattn_w_sim': 6.335}
    for name, (base, spread) in spreads.items():
        noise = np.random.default_rng([zlib.crc32(name.encode()), seed]).standard_normal(out[name].shape)
        drawn = base * np.exp(spread * noise) if base else spread * noise
        out[name] = jnp.asarray(drawn.astype(out[name].dtype))
    for name, factor in factors.items():
        out[name] = (out[name] * factor).astype(out[name].dtype)
    return out
```

```python
from contextlib import ExitStack

import concourse.bass as bass
from concourse import mybir
from concourse.alu_op_type import AluOpType as ALU

ACT = mybir.ActivationFunctionType
F32 = mybir.dt.float32
BF16 = mybir.dt.bfloat16
U8 = mybir.dt.uint8
U16 = mybir.dt.uint16
AX_X = mybir.AxisListType.X
ds = bass.ds

P = 128
B = 4
S = 512
D = 256
DC = D // P
QT = S // P
T = B * QT
H = 16
HD = D // H
G = 4
NG = H // G
STEPS = B * NG
E = 8
I = 128
SH = 2
NX = E + SH
INNER = 1024
IC = INNER // P
EPS = 1e-5
BIG = 1e30
HPAD = 32
XROWS = 32
MASK_ROW = 3 * G
SCALE = HD ** -0.5
MAGIC = 1.5 * 2.0 ** 23

C_ID, C_SEL, C_COS, C_SIN, C_TRI, C32 = 0, 128, 256, 320, 384, 448
B_ID, B_PRE, C16 = 0, 128, 128 + 2 * H * XROWS

Q1, Q2, Q3 = slice(0, 3), slice(3, 5), slice(5, 6)
K1, K2, K3 = slice(1, 6, 2), slice(2, 5, 2), slice(0, 1)


def wait(eng, sem, value):
    if not isinstance(value, int) or value > 0:
        eng.wait_ge(sem, value)


def row_statistics(nc, sb, sem, x_sb, tag):
    st = sb("st" + tag, [P, T, 6], F32)
    tmp = sb("lntmp" + tag, [P, 4, T], F32)
    mean = sb("mean" + tag, [P, T], F32)
    rstd = sb("rstd" + tag, [P, T], F32)
    power = sb("power" + tag, [P, T], F32)
    chain = sem("ln_chain" + tag)
    var_ready = sem("var_ready" + tag)
    rstd_ready = sem("rstd_ready" + tag)

    def vector(dve):
        for t in range(T):
            last = dve.bn_stats(st[:, t, :], x_sb[:, t, :])
        last.then_inc(chain, 1)
        dve.wait_ge(chain, 1)
        dve.tensor_tensor(tmp[:, 0, :], st[:, :, 1], st[:, :, 4], ALU.subtract)
        dve.tensor_tensor(tmp[:, 1, :], st[:, :, 1], st[:, :, 4], ALU.add)
        dve.tensor_tensor(tmp[:, 2, :], st[:, :, 2], st[:, :, 5], ALU.add).then_inc(chain, 1)
        dve.wait_ge(chain, 2)
        dve.tensor_tensor(tmp[:, 3, :], tmp[:, 0, :], tmp[:, 0, :], ALU.mult)
        dve.tensor_scalar(mean[:, :], tmp[:, 1, :], 0.5, None, ALU.mult).then_inc(chain, 1)
        dve.wait_ge(chain, 3)
        dve.tensor_scalar(tmp[:, 0, :], tmp[:, 3, :], 0.25, EPS, ALU.mult, ALU.add).then_inc(chain, 1)
        dve.wait_ge(chain, 4)
        dve.scalar_tensor_tensor(out=tmp[:, 1, :], in0=tmp[:, 2, :], scalar=1.0 / D, in1=tmp[:, 0, :],
                                 op0=ALU.mult, op1=ALU.add).then_inc(var_ready, 1)

    def pool(pool_):
        pool_.memset(power[:, :], -0.5).then_inc(rstd_ready, 1)
        pool_.wait_ge(rstd_ready, 1)
        pool_.wait_ge(var_ready, 1)
        pool_.tensor_tensor(rstd[:, :], tmp[:, 1, :], power[:, :], ALU.pow).then_inc(rstd_ready, 1)

    return mean, rstd, rstd_ready, vector, pool


def phase_load(nc, a, per):
    with ExitStack() as ctx:
        sem = lambda n: ctx.enter_context(nc.semaphore(n))
        loaded, gates = sem("loaded"), sem("gates")
        block = ctx.enter_context(nc.Block())

        @block.sync
        def _(sp):
            xv = a["x"].rearrange("b (q p) d -> p (b q) d", p=P)
            for b in range(B):
                sp.dma_start(per["x"][:, 4 * b:4 * b + 4, :], xv[:, 4 * b:4 * b + 4, :]).then_inc(loaded, 16)
            sp.wait_ge(loaded, 16 * (B + 3))

        @block.scalar
        def _(act):
            act.dma_start(per["gates_raw"][:, :], a["gates"].to_broadcast([P, 4])).then_inc(gates, 16)
            act.dma_start(per["c32"][:, :], a["c32"]).then_inc(loaded, 16)
            act.dma_start(per["c16"][:, :].bitcast(U16), a["c16"]).then_inc(loaded, 16)
            act.dma_start(per["mask_u8"][:, :], a["mask"]).then_inc(loaded, 16)
            act.wait_ge(gates, 16)
            act.activation(per["gates"][:, :], per["gates_raw"][:, :], ACT.Tanh)


def phase_prepare(nc, a, per, qs, ks, va):
    x_sb, c32, c16 = per["x"], per["c32"], per["c16"]
    id32 = c32[:, C_ID:C_ID + P]
    id16 = c16[:, B_ID:B_ID + P]
    cos = c32[:, C_COS:C_SIN].rearrange("p (q d) -> p q d", q=QT)
    sin = c32[:, C_SIN:C_TRI].rearrange("p (q d) -> p q d", q=QT)
    preset = c16[:, B_PRE:C16].rearrange("p (h r) -> p h r", r=XROWS)
    with ExitStack() as ctx:
        sb = lambda n, s, d: ctx.enter_context(nc.sbuf_tensor(n, s, d))
        ps = lambda n, s, d: ctx.enter_context(nc.psum_tensor(n, s, d))
        sem = lambda n: ctx.enter_context(nc.semaphore(n))
        wq, wk, wv = (sb(n, [P, DC, D], F32) for n in ("wq", "wk", "wv"))
        bqk = sb("bqk", [P, 2 * D], F32)
        bv = sb("bv", [P, D], F32)
        ctxT = sb("ctxT", [P, 2, DC, P], F32)
        xn = sb("xn", [P, 2, D], F32)
        xnT = sb("xnT", [P, 2, DC, P], F32)
        qkb = sb("qkb", [P, 2, 2 * H, HD], F32)
        rope2 = sb("rope2", [P, 2 * H, HD], F32)
        qkr = sb("qkr", [P, 2 * H, HD], F32)
        rest = qkb
        stack = sb("stack", [P, 2, 2 * H, P], BF16)
        mbias = sb("mbias", [P, T], F32)
        mean, rstd, rstd_ready, ln_vector, ln_pool = row_statistics(nc, sb, sem, x_sb, "A")
        ps_st = [ps(f"ps_st{i}", [P, 8, P], BF16) for i in range(4)]
        ps_T = ps("ps_T", [P, DC, P], F32)
        ps_qk = ps("ps_qk", [P, 2 * D], F32)
        ps_v = ps("ps_v", [P, D], F32)

        weights, ctx_in = sem("weights"), [sem("ctx_in0"), sem("ctx_in1")]
        xn_ready, xT_done, xT_copied = sem("xn_ready"), sem("xT_done"), sem("xT_copied")
        proj_done, qk_copied, v_copied = sem("proj_done"), sem("qk_copied"), sem("v_copied")
        vb_done, mask_done = sem("vb_done"), sem("mask_done")
        rope_half, rope_done, rest1_done = sem("rope_half"), sem("rope_done"), sem("rest1_done")
        part1_done, part2_done, part3_done = sem("part1_done"), sem("part2_done"), sem("part3_done")
        stackT_done, stackT_v, stackT_a = sem("stackT_done"), sem("stackT_v"), sem("stackT_a")
        block = ctx.enter_context(nc.Block())

        va_v = va[:, :, :].rearrange("p s (k j d) -> p s k j d", k=QT, j=G)
        parts = lambda u, first: stack[:, u, first:first + H, 0:96].rearrange("p h (s d) -> p h s d", d=HD)

        def stack_out(copy, dst, i, n):
            at = (n // QT) * H + 8 * (i % 2)
            return copy(dst[:, ds(at, 8), ds((n % QT) * P, P)], ps_st[i][:, :, :])

        @block.sync
        def _(sp):
            for w, n in ((wq, "wq"), (wk, "wk"), (wv, "wv")):
                sp.dma_start(w[:, :, :], a[n]).then_inc(weights, 16)
            sp.dma_start(bqk[:, :], a["bqk"].to_broadcast([P, 2 * D])).then_inc(weights, 16)
            sp.dma_start(bv[:, :], a["bv"].to_broadcast([P, D])).then_inc(weights, 16)

            def load(n, u):
                wait(sp, proj_done, n - 1)
                sp.dma_start(ctxT[:, u, :, :], a["ctxT"][ds(n, 1), :, :, :]).then_inc(ctx_in[u], 16)
            load(0, 0)
            load(1, 1)
            with sp.Fori(1, T // 2) as half_n0:
                n0 = 2 * half_n0
                for u in range(2):
                    load(n0 + u, u)

        @block.vector
        def _(dve):
            for u in range(2):
                dve.tensor_copy(stack[:, u, :, 96:128], preset)
            dve.tensor_copy(per["mask"][:, :], per["mask_u8"][:, :]).then_inc(mask_done, 1)
            dve.wait_ge(mask_done, 1)
            dve.tensor_scalar(mbias[:, :], per["mask"][:, :], BIG, -BIG, ALU.mult, ALU.add).then_inc(mask_done, 1)
            ln_vector(dve)
            dve.wait_ge(rstd_ready, 2)
            dve.wait_ge(mask_done, 2)
            dve.wait_ge(weights, 16 * 5)
            for k in range(QT):
                m = per["mask"][:, k:T:QT].rearrange("p (b g j) -> p b g j", g=1, j=1)
                vm = va_v[:, :, k, :, HD].rearrange("p (b g) j -> p b g j", b=B)
                dve.tensor_copy(vm, m.broadcast_to([P, B, NG, G]))

            def normalise(n, u):
                wait(dve, xT_done, n - 1)
                dve.tensor_scalar(xn[:, u, :], x_sb[:, ds(n, 1), :], mean[:, ds(n, 1)], rstd[:, ds(n, 1)],
                                  ALU.subtract, ALU.mult).then_inc(xn_ready, 1)

            def third_part(n, u):
                dve.wait_ge(part2_done, n + 1)
                for first, slot, src in ((0, Q3, Q2), (H, K3, K2)):
                    last = dve.tensor_tensor(parts(u, first)[:, :, slot.start, :], rest[:, u, first:first + H, :],
                                             parts(u, first)[:, :, src.start, :], ALU.subtract)
                dve.tensor_copy(stack[:, u, H:2 * H, 96 + MASK_ROW],
                                mbias[:, ds(n, 1)].broadcast_to([P, H])).then_inc(part3_done, 1)

            def stack_copy(n):
                dve.wait_ge(stackT_done, 4 * n + 2)
                for i in (0, 1):
                    last = stack_out(dve.tensor_copy, qs, i, n)
                last.then_inc(stackT_v, 1)

            def projections(n, u):
                dve.wait_ge(proj_done, n + 1)
                dve.tensor_tensor(qkb[:, u, :, :], ps_qk[:, :].rearrange("p (h d) -> p h d", d=HD),
                                  bqk[:, :].rearrange("p (h d) -> p h d", d=HD), ALU.add).then_inc(qk_copied, 1)
                out = va_v[:, ds((n // QT) * NG, NG), ds(n % QT, 1), :, 0:HD].rearrange("p g k j d -> p (g k) j d")
                heads = lambda v: v[:, :].rearrange("p (g j d) -> p g j d", g=NG, j=G)
                dve.tensor_tensor(out, heads(ps_v), heads(bv), ALU.add).then_inc(vb_done, 1)
                dve.wait_ge(vb_done, n + 1)
                dve.tensor_scalar(out, out, per["mask"][:, ds(n, 1)], None, ALU.mult).then_inc(v_copied, 1)

            def transposed(n, u):
                dve.wait_ge(xT_done, n + 1)
                wait(dve, proj_done, n - 1)
                dve.tensor_copy(xnT[:, u, :, :], ps_T[:, :, :]).then_inc(xT_copied, 1)

            def step(n, u, lo, hi):
                if lo:
                    third_part(n - 2, u)
                if hi:
                    normalise(n + 1, 1 - u)
                if lo:
                    stack_copy(n - 2)
                if hi:
                    transposed(n + 1, 1 - u)
            normalise(0, 0)
            transposed(0, 0)
            step(0, 0, False, True)
            projections(0, 0)
            step(1, 1, False, True)
            projections(1, 1)
            with dve.Fori(1, (T - 2) // 2) as half_n0:
                n0 = 2 * half_n0
                for u in range(2):
                    step(n0 + u, u, True, True)
                    projections(n0 + u, u)
            step(T - 2, 0, True, True)
            projections(T - 2, 0)
            step(T - 1, 1, True, False)
            projections(T - 1, 1)
            step(T, 0, True, False)
            step(T + 1, 1, True, False)

        @block.scalar
        def _(act):
            def first_part(n, u):
                act.wait_ge(rope_done, n + 1)
                wait(act, stackT_done, 4 * (n - 1))
                for first, slots in ((0, Q1), (H, K1)):
                    src = qkr[:, first:first + H, :].rearrange("p h (o d) -> p h o d", o=1)
                    last = act.copy(parts(u, first)[:, :, slots, :], src.broadcast_to([P, H, 3, HD]))
                last.then_inc(part1_done, 1)

            def second_part(n, u):
                act.wait_ge(rest1_done, n + 1)
                for first, slots in ((0, Q2), (H, K2)):
                    src = rest[:, u, first:first + H, :].rearrange("p h (o d) -> p h o d", o=1)
                    last = act.copy(parts(u, first)[:, :, slots, :], src.broadcast_to([P, H, 2, HD]))
                last.then_inc(part2_done, 1)

            def stack_copy(n):
                for i in (2, 3):
                    act.wait_ge(stackT_done, 4 * n + i + 1)
                    last = stack_out(act.copy, ks, i, n)
                last.then_inc(stackT_a, 1)

            first_part(0, 0)
            second_part(0, 0)
            first_part(1, 1)
            with act.Fori(1, T // 2) as half_n0:
                n0 = 2 * half_n0
                for u in range(2):
                    stack_copy(n0 + u - 2)
                    second_part(n0 + u - 1, 1 - u)
                    first_part(n0 + u, u)
            stack_copy(T - 2)
            second_part(T - 1, 1)
            stack_copy(T - 1)

        @block.gpsimd
        def _(pool):
            ln_pool(pool)

            def rope(n, u):
                pool.wait_ge(qk_copied, n + 1)
                wait(pool, rope_done, n)
                wait(pool, rest1_done, n)
                c = cos[:, ds(n % QT, 1), :].broadcast_to([P, 2 * H, HD])
                s = sin[:, ds(n % QT, 1), :]
                lo, hi = slice(0, HD // 2), slice(HD // 2, HD)
                pool.tensor_tensor(qkr[:, :, :], qkb[:, u, :, :], c, ALU.mult)
                pool.tensor_tensor(rope2[:, :, lo], qkb[:, u, :, hi], s[:, :, lo].broadcast_to([P, 2 * H, HD // 2]),
                                   ALU.mult)
                pool.tensor_tensor(rope2[:, :, hi], qkb[:, u, :, lo], s[:, :, hi].broadcast_to([P, 2 * H, HD // 2]),
                                   ALU.mult).then_inc(rope_half, 1)
                pool.wait_ge(rope_half, n + 1)
                pool.tensor_tensor(qkr[:, :, :], qkr[:, :, :], rope2[:, :, :], ALU.add).then_inc(rope_done, 1)

            def first_rest(n, u):
                pool.wait_ge(part1_done, n + 1)
                for first, slot in ((0, Q1), (H, K1)):
                    last = pool.tensor_tensor(rest[:, u, first:first + H, :], qkr[:, first:first + H, :],
                                              parts(u, first)[:, :, slot.start, :], ALU.subtract)
                last.then_inc(rest1_done, 1)
            rope(0, 0)
            first_rest(0, 0)
            rope(1, 1)
            with pool.Fori(1, T // 2) as half_n0:
                n0 = 2 * half_n0
                for u in range(2):
                    first_rest(n0 + u - 1, 1 - u)
                    rope(n0 + u, u)
            first_rest(T - 1, 1)

        @block.tensor
        def _(pe):
            def stack_transposes(n, u):
                pe.wait_ge(part3_done, n + 1)
                for i in range(4):
                    if i == 0:
                        wait(pe, stackT_v, n)
                    if i == 2:
                        wait(pe, stackT_a, n)
                    for h in range(8):
                        last = pe.transpose(ps_st[i][:, h, :], stack[:, u, 8 * i + h, :], id16)
                    last.then_inc(stackT_done, 1)

            def x_transposes(n, u):
                pe.wait_ge(xn_ready, n + 1)
                wait(pe, xT_copied, n)
                for c in range(DC):
                    last = pe.transpose(ps_T[:, c, :], xn[:, u, c * P:(c + 1) * P], id32)
                last.then_inc(xT_done, 1)

            def projections(n, u):
                pe.wait_ge(xT_copied, n + 1)
                wait(pe, v_copied, n)
                pe.wait_ge(ctx_in[u], (n // 2 + 1) * 16)
                for out, src, w in ((ps_qk[:, 0:D], xnT, wq), (ps_qk[:, D:2 * D], ctxT, wk), (ps_v[:, :], ctxT, wv)):
                    for c in range(DC):
                        last = pe.matmul(out, src[:, u, c, :], w[:, c, :], start=(c == 0), stop=(c == DC - 1))
                last.then_inc(proj_done, 1)

            pe.wait_ge(weights, 16 * 5)
            x_transposes(0, 0)
            x_transposes(1, 1)
            projections(0, 0)
            x_transposes(2, 0)
            projections(1, 1)
            with pe.Fori(1, (T - 2) // 2) as half_n0:
                n0 = 2 * half_n0
                for u in range(2):
                    stack_transposes(n0 + u - 2, u)
                    x_transposes(n0 + u + 1, 1 - u)
                    projections(n0 + u, u)
            stack_transposes(T - 4, 0)
            x_transposes(T - 1, 1)
            projections(T - 2, 0)
            stack_transposes(T - 3, 1)
            projections(T - 1, 1)
            stack_transposes(T - 2, 0)
            stack_transposes(T - 1, 1)


def phase_attend(nc, per, qs, ks, va):
    id16 = per["c16"][:, B_ID:B_ID + P]
    with ExitStack() as ctx:
        sb = lambda n, s, d: ctx.enter_context(nc.sbuf_tensor(n, s, d))
        ps = lambda n, s, d: ctx.enter_context(nc.psum_tensor(n, s, d))
        sem = lambda n: ctx.enter_context(nc.semaphore(n))
        prob = sb("prob", [P, 2, G, S], F32)
        vst = sb("vst", [P, 2, QT, G * HPAD], F32)
        mx = sb("mx", [P, 2, QT, G], F32)
        minus = sb("minus", [P, QT, G], F32)
        mrest = sb("mrest", [P, 2, QT, G], F32)
        mparts = sb("mparts", [P, 2, QT, XROWS], BF16)
        ps_f = [ps(f"ps_f{i}", [P, S], F32) for i in range(2)]
        ps_s = [ps(f"ps_s{i}", [P, 2, S], F32) for i in range(2)]
        ps_o = ps("ps_o", [P, S], F32)
        ps_m = ps("ps_m", [P, QT, P], BF16)
        scored, max_done = sem("scored"), sem("max_done")
        mpreset, split1, split_done = sem("mpreset"), sem("split1"), sem("split_done")
        mT_done, m_ready = sem("mT_done"), sem("m_ready")
        v_ready = sem("v_ready")
        s_done, exp_done, pv_done, o_copied = sem("s_done"), sem("exp_done"), sem("pv_done"), sem("o_copied")
        block = ctx.enter_context(nc.Block())
        o32 = qs[:, :, :].rearrange("p h s -> p (h s)").bitcast(F32).rearrange("p (s c) -> p s c", s=STEPS)

        @block.tensor
        def _(pe):
            def first_scores(f, idx):
                qt, j = divmod(idx, G)
                wait(pe, max_done, f * 16 + idx - 1)
                pe.matmul(ps_f[idx % 2][:, :], qs[:, ds(f * G + j, 1), qt * P:(qt + 1) * P],
                          ks[:, ds(f * G + j, 1), :], start=True, stop=True).then_inc(scored, 1)

            def scores(s, kt, half):
                wait(pe, exp_done, s * 8 + kt * 2 + half - 1)
                for j in (2 * half, 2 * half + 1):
                    last = pe.matmul(ps_s[half][:, j % 2, :], ks[:, ds(s * G + j, 1), kt * P:(kt + 1) * P],
                                     qs[:, ds(s * G + j, 1), :], start=True, stop=True)
                last.then_inc(s_done, 1)

            def values(s, u, kt):
                pe.wait_ge(exp_done, s * 8 + kt * 2 + 2)
                if kt == 0:
                    pe.wait_ge(v_ready, s + 1)
                    wait(pe, o_copied, s)
                for j in range(G):
                    last = pe.matmul(ps_o[HPAD * j:HPAD * (j + 1), :], vst[:, u, kt, HPAD * j:HPAD * (j + 1)],
                                     prob[:, kt % 2, j, :], start=(kt == 0), stop=(kt == QT - 1))
                last.then_inc(pv_done, 1)

            def maxima(s, u):
                pe.wait_ge(split_done, s + 1)
                wait(pe, m_ready, s)
                for qt in range(QT):
                    last = pe.transpose(ps_m[96:128, qt, :], mparts[:, u, qt, :], id16)
                last.then_inc(mT_done, 1)

            def step(s, u, before, ahead, next_):
                for kt in range(QT):
                    if ahead:
                        first_scores(s + 2, 4 * kt)
                    if kt == 0:
                        pe.wait_ge(m_ready, s + 1)
                    scores(s, kt, 0)
                    if ahead:
                        first_scores(s + 2, 4 * kt + 1)
                    scores(s, kt, 1)
                    if ahead:
                        first_scores(s + 2, 4 * kt + 2)
                    if kt:
                        values(s, u, kt - 1)
                    elif before:
                        values(s - 1, 1 - u, QT - 1)
                    if ahead:
                        first_scores(s + 2, 4 * kt + 3)
                    if kt == 2 and next_:
                        maxima(s + 1, 1 - u)

            for f in range(2):
                for idx in range(16):
                    first_scores(f, idx)
            maxima(0, 0)
            step(0, 0, False, True, True)
            step(1, 1, True, True, True)
            with pe.Fori(1, (STEPS - 2) // 2) as half_s0:
                s0 = 2 * half_s0
                for u in range(2):
                    step(s0 + u, u, True, True, True)
            step(STEPS - 2, 0, True, False, True)
            step(STEPS - 1, 1, True, False, False)
            values(STEPS - 1, 1, QT - 1)

        @block.vector
        def _(dve):
            def maxima(f, u):
                wait(dve, split_done, f - 1)
                for idx in range(16):
                    dve.wait_ge(scored, f * 16 + idx + 1)
                    dve.tensor_reduce(mx[:, u, idx // G, idx % G:idx % G + 1], ps_f[idx % 2][:, :], AX_X,
                                      ALU.max).then_inc(max_done, 1)
            maxima(0, 0)
            maxima(1, 1)
            with dve.Fori(1, STEPS // 2) as half_f0:
                f0 = 2 * half_f0
                for u in range(2):
                    maxima(f0 + u, u)

        @block.gpsimd
        def _(pool):
            pool.memset(vst[:, :, :, :], 0.0)
            pool.memset(minus[:, :, :], -1.0)
            pool.memset(mparts[:, :, :, :], 0.0).then_inc(mpreset, 1)
            pool.wait_ge(mpreset, 1)
            pool.memset(mparts[:, :, :, MASK_ROW:MASK_ROW + 1], 1.0).then_inc(mpreset, 1)
            pool.wait_ge(mpreset, 2)

            def split(s, u):
                out = mparts[:, u, :, 0:3 * G].rearrange("p q (j i) -> p q j i", i=3)
                pool.wait_ge(max_done, 16 * (s + 1))
                wait(pool, mT_done, s - 1)
                pool.tensor_tensor(out[:, :, :, 0], mx[:, u, :, :], minus[:, :, :], ALU.mult).then_inc(split1, 1)
                pool.wait_ge(split1, s * 4 + 1)
                pool.tensor_tensor(mrest[:, 0, :, :], mx[:, u, :, :], out[:, :, :, 0], ALU.add).then_inc(split1, 1)
                pool.wait_ge(split1, s * 4 + 2)
                pool.tensor_tensor(out[:, :, :, 1], mrest[:, 0, :, :], minus[:, :, :], ALU.mult).then_inc(split1, 1)
                pool.wait_ge(split1, s * 4 + 3)
                pool.tensor_tensor(mrest[:, 1, :, :], mrest[:, 0, :, :], out[:, :, :, 1], ALU.add).then_inc(split1, 1)
                pool.wait_ge(split1, s * 4 + 4)
                pool.tensor_tensor(out[:, :, :, 2], mrest[:, 1, :, :], minus[:, :, :], ALU.mult)\
                    .then_inc(split_done, 1)

            def stage_values(s, u):
                wait(pool, pv_done, QT * (s - 1))
                pool.tensor_copy(vst[:, u, :, :].rearrange("p k (j c) -> p (k j) c", c=HPAD)[:, :, 0:HD + 1],
                                 va[:, ds(s, 1), :].rearrange("p o (k d) -> p (o k) d", d=HD + 1)).then_inc(v_ready, 1)

            for s in range(2):
                split(s, s)
                stage_values(s, s)
            with pool.Fori(1, STEPS // 2) as half_s0:
                s0 = 2 * half_s0
                for u in range(2):
                    split(s0 + u, u)
                    stage_values(s0 + u, u)

        @block.scalar
        def _(act):
            def exps(s, kt):
                for half in range(2):
                    act.wait_ge(s_done, s * 8 + kt * 2 + half + 1)
                    if half == 0:
                        wait(act, pv_done, s * QT + kt - 1)
                    act.activation(prob[:, kt % 2, 2 * half:2 * half + 2, :], ps_s[half][:, :, :], ACT.Exp,
                                   scale=SCALE).then_inc(exp_done, 1)

            def spread_maxima(s):
                act.wait_ge(mT_done, s + 1)
                act.copy(qs[96:128, ds(s * G, G), :],
                         ps_m[96:128, :, :].rearrange("p q (o c) -> p o (q c)", o=1).broadcast_to([32, G, S]))\
                    .then_inc(m_ready, 1)

            def sums_out(s):
                act.wait_ge(pv_done, QT * (s + 1))
                act.copy(o32[:, ds(s, 1), 0:S], ps_o[:, :]).then_inc(o_copied, 1)

            def step(s, before, next_):
                for kt in range(QT):
                    exps(s, kt)
                    if kt == 0 and before:
                        sums_out(s - 1)
                    if kt == 3 and next_:
                        spread_maxima(s + 1)
            spread_maxima(0)
            step(0, False, True)
            with act.Fori(1, STEPS - 1) as s:
                step(s, True, True)
            step(STEPS - 1, True, False)
            sums_out(STEPS - 1)


def phase_project(nc, a, per, qs):
    x_sb, c32 = per["x"], per["c32"]
    sel = c32[:, C_SEL:C_SEL + P]
    o32 = qs[:, :, :].rearrange("p h s -> p (h s)").bitcast(F32).rearrange("p (s c) -> p s c", s=STEPS)
    with ExitStack() as ctx:
        sb = lambda n, s, d: ctx.enter_context(nc.sbuf_tensor(n, s, d))
        ps = lambda n, s, d: ctx.enter_context(nc.psum_tensor(n, s, d))
        sem = lambda n: ctx.enter_context(nc.semaphore(n))
        wp = sb("wp", [P, NG, D], F32)
        bp = sb("bp", [P, D], F32)
        recip = sb("recip", [P, 2, S], F32)
        on = sb("on", [P, NG, S], F32)
        yb = sb("yb", [P, 2, D], F32)
        coef = sb("coef", [P, T], F32)
        ps_l = [ps(f"ps_l{i}", [P, S], F32) for i in range(2)]
        ps_y = [ps(f"ps_y{i}", [P, 2, D], F32) for i in range(2)]
        wp_in, bp_in, l_done, r_done, on_ready = sem("wp_in"), sem("bp_in"), sem("l_done"), sem("r_done"), sem("on_ready")
        g_used, y_done, y_biased, y_used = sem("g_used"), sem("y_done"), sem("y_biased"), sem("y_used")
        wp_zero, coef_done = sem("wp_zero"), sem("coef_done")
        block = ctx.enter_context(nc.Block())

        @block.sync
        def _(sp):
            sp.dma_start(bp[:, :], a["bp"].to_broadcast([P, D])).then_inc(bp_in, 16)
            sp.wait_ge(wp_zero, 1)
            for j in range(G):
                sp.dma_start(wp[HPAD * j:HPAD * j + HD, :, :], a["wp"][j]).then_inc(wp_in, 16)

        @block.gpsimd
        def _(pool):
            pool.memset(wp[:, :, :], 0.0).then_inc(wp_zero, 1)

        @block.tensor
        def _(pe):
            pe.wait_ge(wp_in, 16 * G)

            def sums(s, slot):
                pe.matmul(ps_l[slot][:, :], sel, o32[:, ds(s, 1), 0:S], start=True, stop=True).then_inc(l_done, 1)

            def project(b, g):
                pe.wait_ge(on_ready, b * NG + g + 1)
                for qt in range(QT):
                    last = pe.matmul(ps_y[qt // 2][:, qt % 2, :], on[:, g, qt * P:(qt + 1) * P], wp[:, g, :],
                                     start=(g == 0 and qt % 2 == 0), stop=(g == NG - 1), skip_group_check=True)
                last.then_inc(g_used, 1)
            sums(0, 0)
            with pe.Fori(0, B - 1) as b:
                for g in range(NG):
                    sums(b * NG + g + 1, (g + 1) % 2)
                    project(b, g)
            for g in range(NG):
                if g < NG - 1:
                    sums((B - 1) * NG + g + 1, (g + 1) % 2)
                project(B - 1, g)

        @block.vector
        def _(dve):
            dve.tensor_scalar(coef[:, :], per["mask"][:, :], per["gates"][:, 0:1], None, ALU.mult)\
               .then_inc(coef_done, 1)
            dve.wait_ge(coef_done, 1)
            dve.wait_ge(bp_in, 16)
            with dve.Fori(0, B) as b:
                for g in range(NG):
                    s = b * NG + g
                    dve.wait_ge(l_done, s + 1)
                    dve.reciprocal(recip[:, g % 2, :], ps_l[g % 2][:, :]).then_inc(r_done, 1)
                    dve.wait_ge(r_done, s + 1)
                    dve.tensor_tensor(on[:, g, :].rearrange("p (o c) -> p o c", o=1), o32[:, ds(s, 1), 0:S],
                                      recip[:, g % 2, :].rearrange("p (o c) -> p o c", o=1),
                                      ALU.mult).then_inc(on_ready, 1)
                dve.wait_ge(g_used, (b + 1) * NG)
                for h in range(2):
                    for q in range(2):
                        dve.tensor_tensor(yb[:, q, :], ps_y[h][:, q, :], bp[:, :], ALU.add)\
                           .then_inc(y_biased, 1)
                    for q in range(2):
                        t = b * QT + 2 * h + q
                        dve.wait_ge(y_biased, t + 2 - q)
                        last = dve.scalar_tensor_tensor(out=x_sb[:, ds(t, 1), :].rearrange("p o d -> p (o d)"),
                                                        in0=yb[:, q, :], scalar=coef[:, ds(t, 1)],
                                                        in1=x_sb[:, ds(t, 1), :].rearrange("p o d -> p (o d)"),
                                                        op0=ALU.mult, op1=ALU.add)
                    last.then_inc(y_used, 1)
                    dve.wait_ge(y_used, b * 2 + h + 1)


def phase_route(nc, a, per, xT_all, nselT, down):
    x_sb, c32, c16 = per["x"], per["c32"], per["c16"]
    id32 = c32[:, C_ID:C_ID + P]
    id16 = c16[:, B_ID:B_ID + P]
    tri = c32[:, C_TRI:C_TRI + E * E].rearrange("p (o e f) -> p o e f", o=1, f=E)
    with ExitStack() as ctx:
        sb = lambda n, s, d: ctx.enter_context(nc.sbuf_tensor(n, s, d))
        ps = lambda n, s, d: ctx.enter_context(nc.psum_tensor(n, s, d))
        sem = lambda n: ctx.enter_context(nc.semaphore(n))
        gw = sb("gw", [P, DC, E], F32)
        lb = sb("lb", [P, E], F32)
        xn = sb("xnB", [P, 2, D], F32)
        xt = sb("xtB", [P, 2, DC, P], F32)
        logits = sb("logits", [P, T, E], F32)
        score = sb("score", [P, T, E], F32)
        beats = sb("beats", [P, T, E, E], F32)
        ties = sb("ties", [P, T, E, E], F32)
        rank = sb("rank", [P, T, E], F32)
        total = sb("total", [P, 2, T], F32)
        both = sb("both", [P, 2, E, T], F32)
        sums = sb("sums", [P, 2, E], F32)
        ones = sb("ones", [P, P], F32)
        most = sb("most", [P, 3, E], F32)
        nsel = sb("nsel", [P, T, P], BF16)
        mean, rstd, rstd_ready, ln_vector, ln_pool = row_statistics(nc, sb, sem, x_sb, "B")
        ps_T = [ps(f"ps_TB{i}", [P, DC, P], F32) for i in range(2)]
        ps_lg = ps("ps_lg", [P, T, E], F32)
        ps_sum = ps("ps_sum", [P, 2 * E], F32)
        ps_n = [ps(f"ps_n{i}", [P, 8, P], BF16) for i in range(2)]
        small_in, down_in = sem("small_in"), sem("down_in")
        xn_ready, xT_done, xt_ready, lg_done = sem("xn_readyB"), sem("xT_doneB"), sem("xt_readyB"), sem("lg_done")
        kept = sem("kept")
        lg_copied, score_done, step_done = sem("lg_copied"), sem("score_done"), sem("step_done")
        sums_ready, sums_done, nsel_ready, nT_done = sem("sums_ready"), sem("sums_done"), sem("nsel_ready"), sem("nT_done")
        consts = sem("constsB")
        block = ctx.enter_context(nc.Block())

        @block.sync
        def _(sp):
            sp.dma_start(gw[:, :, :], a["gate_w"]).then_inc(small_in, 16)
            sp.dma_start(lb[:, :], a["lb"].to_broadcast([P, E])).then_inc(small_in, 16)
            sp.dma_start(down[:, :, :], a["down"]).then_inc(down_in, 16)

        @block.vector
        def _(dve):
            ln_vector(dve)
            dve.wait_ge(rstd_ready, 2)

            def normalise(n, u):
                wait(dve, xT_done, n - 1)
                dve.tensor_scalar(xn[:, u, :], x_sb[:, ds(n, 1), :], mean[:, ds(n, 1)], rstd[:, ds(n, 1)],
                                  ALU.subtract, ALU.mult).then_inc(xn_ready, 1)

            def transposed(n, u):
                dve.wait_ge(xT_done, n + 1)
                wait(dve, lg_done, n - 1)
                wait(dve, kept, n - 1)
                dve.tensor_copy(xt[:, u, :, :], ps_T[u][:, :, :]).then_inc(xt_ready, 1)
            normalise(0, 0)
            normalise(1, 1)
            transposed(0, 0)
            transposed(1, 1)
            with dve.Fori(1, T // 2) as half_n0:
                n0 = 2 * half_n0
                for u in range(2):
                    normalise(n0 + u, u)
                for u in range(2):
                    transposed(n0 + u, u)

            count = [0]

            def link(ins):
                count[0] += 1
                ins.then_inc(step_done, 1)
                dve.wait_ge(step_done, count[0])
            dve.wait_ge(lg_done, T)
            dve.wait_ge(small_in, 32)
            dve.tensor_tensor(logits[:, :, :], ps_lg[:, :, :],
                              lb[:, :].rearrange("p (o e) -> p o e", o=1).broadcast_to([P, T, E]), ALU.add)\
               .then_inc(lg_copied, 1)
            dve.wait_ge(score_done, 1)
            other = score[:, :, :].rearrange("p t (o f) -> p t o f", o=1).broadcast_to([P, T, E, E])
            own = score[:, :, :].rearrange("p t (e o) -> p t e o", o=1).broadcast_to([P, T, E, E])
            dve.tensor_tensor(beats[:, :, :, :], other, own, ALU.is_gt)
            link(dve.tensor_tensor(ties[:, :, :, :], other, own, ALU.is_equal))
            link(dve.tensor_tensor(ties[:, :, :, :], ties[:, :, :, :], tri.broadcast_to([P, T, E, E]), ALU.mult))
            link(dve.tensor_tensor(beats[:, :, :, :], beats[:, :, :, :], ties[:, :, :, :], ALU.add))
            link(dve.tensor_reduce(rank[:, :, :], beats[:, :, :, :], AX_X, ALU.add))
            chosen = both[:, 1, :, :].rearrange("p e t -> p t e")
            weight = both[:, 0, :, :].rearrange("p e t -> p t e")
            link(dve.tensor_scalar(chosen, rank[:, :, :], 1.5, None, ALU.is_lt))
            dve.tensor_scalar(nsel[:, :, 0:E], rank[:, :, :], 1.5, None, ALU.is_gt).then_inc(nsel_ready, 1)
            link(dve.tensor_tensor(weight, score[:, :, :], chosen, ALU.mult))
            link(dve.tensor_reduce(total[:, 0, :], weight, AX_X, ALU.add))
            link(dve.tensor_scalar(total[:, 1, :], total[:, 0, :], 1e-8, None, ALU.add))
            link(dve.reciprocal(total[:, 0, :], total[:, 1, :]))
            link(dve.tensor_tensor(both[:, 0, :, :], both[:, 0, :, :],
                                   total[:, 0, :].rearrange("p (o t) -> p o t", o=1).broadcast_to([P, E, T]),
                                   ALU.mult))
            dve.tensor_reduce(sums[:, :, :], both[:, :, :, :], AX_X, ALU.add).then_inc(sums_ready, 1)
            for i in range(2):
                dve.wait_ge(nT_done, i + 1)
                dve.tensor_copy(nselT[:, i * 8 * P:(i + 1) * 8 * P].rearrange("p (t c) -> p t c", c=P), ps_n[i][:, :, :])
            dve.wait_ge(sums_done, 1)
            link(dve.tensor_scalar(most[:, 0, :], ps_sum[:, E:2 * E], 1.0, None, ALU.max))
            link(dve.reciprocal(most[:, 1, :], most[:, 0, :]))
            link(dve.tensor_tensor(most[:, 2, :], ps_sum[:, 0:E], most[:, 1, :], ALU.mult))
            dve.wait_ge(down_in, 16)
            for e in range(E):
                dve.tensor_scalar(down[:, e, :], down[:, e, :], most[:, 2, e:e + 1], None, ALU.mult)

        @block.scalar
        def _(act):
            act.wait_ge(lg_copied, 1)
            act.activation(score[:, :, :], logits[:, :, :], ACT.Sigmoid).then_inc(score_done, 1)

        @block.gpsimd
        def _(pool):
            pool.memset(ones[:, :], 1.0).then_inc(consts, 1)
            pool.memset(nsel[:, :, E:P], 0.0).then_inc(consts, 1)
            ln_pool(pool)
            with pool.Fori(0, T // 2) as half_n0:
                n0 = 2 * half_n0
                for u in range(2):
                    n = n0 + u
                    pool.wait_ge(xt_ready, n + 1)
                    pool.tensor_copy(xT_all[:, :, ds(n * P, P)], xt[:, u, :, :]).then_inc(kept, 1)

        @block.tensor
        def _(pe):
            def transposes(n, u):
                pe.wait_ge(xn_ready, n + 1)
                for c in range(DC):
                    last = pe.transpose(ps_T[u][:, c, :], xn[:, u, c * P:(c + 1) * P], id32)
                last.then_inc(xT_done, 1)

            def scores(n, u):
                pe.wait_ge(xt_ready, n + 1)
                for c in range(DC):
                    last = pe.matmul(ps_lg[:, ds(n, 1), :], xt[:, u, c, :], gw[:, c, :],
                                     start=(c == 0), stop=(c == DC - 1))
                last.then_inc(lg_done, 1)
            pe.wait_ge(small_in, 32)
            with pe.Fori(0, T // 2) as half_n0:
                n0 = 2 * half_n0
                for u in range(2):
                    transposes(n0 + u, u)
                for u in range(2):
                    scores(n0 + u, u)
            pe.wait_ge(nsel_ready, 1)
            pe.wait_ge(consts, 2)
            for i in range(2):
                for k in range(8):
                    last = pe.transpose(ps_n[i][:, k, :], nsel[:, 8 * i + k, :], id16)
                last.then_inc(nT_done, 1)
            pe.wait_ge(sums_ready, 1)
            pe.wait_ge(consts, 1)
            pe.matmul(ps_sum[:, :], ones[:, :], sums[:, :, :].rearrange("p a e -> p (a e)"), start=True, stop=True)\
              .then_inc(sums_done, 1)


def phase_experts(nc, a, per, xT_all, nselT, down):
    x_sb = per["x"]
    with ExitStack() as ctx:
        sb = lambda n, s, d: ctx.enter_context(nc.sbuf_tensor(n, s, d))
        ps = lambda n, s, d: ctx.enter_context(nc.psum_tensor(n, s, d))
        sem = lambda n: ctx.enter_context(nc.semaphore(n))
        up = sb("up", [P, NX, 2, DC, P], F32)
        skip = sb("skip", [P, E, P], BF16)
        sg = sb("sg", [P, 2, S], F32)
        h = sb("h", [P, 2, S], F32)
        ps_g = [ps(f"ps_g{i}", [P, S], F32) for i in range(2)]
        ps_u = [ps(f"ps_u{i}", [P, S], F32) for i in range(2)]
        ps_y = [ps(f"ps_yE{i}", [P, 2, D], F32) for i in range(2)]
        up_in, gu_done, silu_done = sem("up_in"), sem("gu_done"), sem("silu_done")
        h_ready, h_used, y_used = sem("h_ready"), sem("h_used"), sem("y_usedE")
        block = ctx.enter_context(nc.Block())

        @block.sync
        def _(sp):
            sp.dma_start(skip[:, :, :].bitcast(U16), a["skip"]).then_inc(up_in, 16)
            for e in range(NX):
                sp.dma_start(up[:, e, :, :, :], a["up"][e]).then_inc(up_in, 16)

        @block.tensor
        def _(pe):
            def gate_up(c, e, first):
                k, u = c * NX + e, e % 2
                if first:
                    pe.wait_ge(up_in, 16 * (NX + 1))
                cols = ds(c * S, S)
                for i, out in ((0, ps_g[u]), (1, ps_u[u])):
                    masked = i == 0 and e < E
                    for d in range(DC):
                        last = pe.matmul(out[:, :], up[:, e, i, d, :], xT_all[:, d, cols], start=(d == 0),
                                         stop=(d == DC - 1 and not masked))
                    if masked:
                        pe.matmul(out[:, :], skip[:, e, :], nselT[:, cols], start=False, stop=True)
                last.then_inc(gu_done, 1)

            def project(c, e):
                k, u = c * NX + e, e % 2
                pe.wait_ge(h_ready, k + 1)
                for q in range(QT):
                    last = pe.matmul(ps_y[q // 2][:, q % 2, :], h[:, u, q * P:(q + 1) * P], down[:, e, :],
                                     start=(e == 0 and q % 2 == 0), stop=(e == NX - 1), skip_group_check=True)
                last.then_inc(h_used, 1)

            def chunk(c, edge):
                for e in range(1, NX):
                    gate_up(c, e, False)
                    project(c, e - 1)
                if not edge:
                    gate_up(c + 1, 0, False)
                project(c, NX - 1)
            gate_up(0, 0, True)
            with pe.Fori(0, B - 1) as c:
                chunk(c, False)
            chunk(B - 1, True)

        @block.scalar
        def _(act):
            with act.Fori(0, B) as c:
                for e in range(NX):
                    k, u = c * NX + e, e % 2
                    act.wait_ge(gu_done, k + 1)
                    act.activation(sg[:, u, :], ps_g[u][:, :], ACT.Silu).then_inc(silu_done, 1)

        @block.vector
        def _(dve):
            def residual(c):
                dve.wait_ge(h_used, (c + 1) * NX)
                for i in range(2):
                    xs = x_sb[:, ds(c * QT + 2 * i, 2), :]
                    dve.scalar_tensor_tensor(out=xs, in0=ps_y[i][:, :, :], scalar=per["gates"][:, 2:3], in1=xs,
                                             op0=ALU.mult, op1=ALU.add).then_inc(y_used, 1)

            def hidden(c, e, edge):
                k, u = c * NX + e, e % 2
                dve.wait_ge(silu_done, k + 1)
                if not edge:
                    dve.wait_ge(h_used, k - 1)
                dve.tensor_tensor(h[:, u, :], sg[:, u, :], ps_u[u][:, :], ALU.mult).then_inc(h_ready, 1)
            for e in range(NX):
                hidden(0, e, e < 2)
            with dve.Fori(1, B) as c:
                residual(c - 1)
                for e in range(NX):
                    hidden(c, e, False)
            residual(B - 1)


def phase_coattend(nc, a, per, w32, wq16, wstat):
    x_sb, c32 = per["x"], per["c32"]
    id32 = c32[:, C_ID:C_ID + P]
    with ExitStack() as ctx:
        sb = lambda n, s, d: ctx.enter_context(nc.sbuf_tensor(n, s, d))
        ps = lambda n, s, d: ctx.enter_context(nc.psum_tensor(n, s, d))
        sem = lambda n: ctx.enter_context(nc.semaphore(n))
        ctok = sb("ctok", [P, T, D], F32)
        ctxT = sb("ctxTC", [P, DC, T * P], F32)
        wqv = sb("wqv", [P, 4, DC, D], F32)
        wsim = sb("wsim", [P, 2, DC], F32)
        w1 = sb("w1", [P, D], F32)
        bsim = sb("bsim", [P, 1], F32)
        bqv = sb("bqv", [P, D], F32)
        e = sb("e", [P, 2, QT, D], F32)
        eT = sb("eT", [P, 2, DC, S], F32)
        sT = sb("sT", [P, DC, S], F32)
        hqT = sb("hqT", [P, DC, S], F32)
        ehT = sb("ehT", [P, DC, S], F32)
        junk = sb("junk", [P, QT, D], F32)
        att = sb("att", [P, QT, S], F32)
        attT = sb("attT", [P, 2, QT, P], F32)
        hq = sb("hq", [P, 2, D], F32)
        wx = sb("wx", [P, DC, D], F32)
        yb = sb("ybC", [P, 2, D], F32)
        nmax = sb("nmax", [P, QT], F32)
        lsum = sb("lsum", [P, QT], F32)
        lrec = sb("lrec", [P, QT], F32)
        own = sb("own", [P, QT], F32)
        z = sb("z", [P, 3, QT], F32)
        nz = sb("nz", [P, 1], F32)
        ez = sb("ez", [P, QT], F32)
        ezs = sb("ezs", [P, 1], F32)
        rz = sb("rz", [P, 1], F32)
        hc = sb("hc", [P, DC], F32)
        ones = sb("onesC", [P, P], F32)
        wabs = sb("wabs", [P, 3], F32)
        wjunk = sb("wjunk", [P, 2 * INNER], F32)
        mean, rstd, rstd_ready, ln_vector, ln_pool = row_statistics(nc, sb, sem, x_sb, "C")
        ps_T = [ps(f"ps_TC{i}", [P, DC, 2 * P], F32) for i in range(2)]
        ps_S = [ps(f"ps_SC{i}", [P, S], F32) for i in range(2)]
        ps_A = ps("ps_A", [P, QT, P], F32)
        ps_q = ps("ps_q", [P, D], F32)
        ps_qT = ps("ps_qT", [P, DC, P], F32)
        ps_h = ps("ps_h", [P, 8], F32)
        w_in, wts_in, ctx_in = sem("w_inC"), sem("wts_inC"), sem("ctx_inC")
        e_ready, eT_done, eT_ready, sT_ready = sem("e_readyC"), sem("eT_done"), sem("eT_ready"), sem("sT_ready")
        S_done, max_ready, exp_done = sem("S_doneC"), sem("max_readyC"), sem("exp_doneC")
        own_done, z_half, z_ready, zmax_ready, nz_ready = (sem("own_done"), sem("z_half"), sem("z_ready"),
                                                           sem("zmax_ready"), sem("nz_ready"))
        ez_ready, hc_done, hc_step, wx_ready = sem("ez_ready"), sem("hc_done"), sem("hc_step"), sem("wx_ready")
        attT_done, attT_ready, q_done, q_ready = sem("attT_done"), sem("attT_ready"), sem("q_done"), sem("q_ready")
        l_ready = sem("l_ready")
        qT_done, qT_ready, eh_ready = sem("qT_done"), sem("qT_ready"), sem("eh_ready")
        out_done, biased, out_used = sem("out_doneC"), sem("biasedC"), sem("out_usedC")
        ones_ready, abs_done, wsum_done, wstat_step, quant = (sem("ones_ready"), sem("abs_done"), sem("wsum_done"),
                                                              sem("wstat_step"), sem("quant"))
        block = ctx.enter_context(nc.Block())

        @block.sync
        def _(sp):
            sp.dma_start(wsim[:, :, :], a["wsim"]).then_inc(w_in, 16)
            sp.dma_start(w1[:, :], a["w1"].to_broadcast([P, D])).then_inc(w_in, 16)
            sp.dma_start(bsim[:, :], a["bsim"].to_broadcast([P, 1])).then_inc(w_in, 16)
            sp.dma_start(bqv[:, :], a["bqv"].to_broadcast([P, D])).then_inc(w_in, 16)
            sp.dma_start(ctxT[:, :, :], a["ctxTC"]).then_inc(ctx_in, 16)
            sp.dma_start(ctok[:, :, :], a["ctx"].rearrange("b (q p) d -> p (b q) d", p=P)).then_inc(ctx_in, 16)
            sp.dma_start(wqv[:, :, :, :], a["wqv"]).then_inc(w_in, 16)
            for i, n in enumerate(("wg", "wu", "wd")):
                sp.dma_start(w32[:, i, :], a[n]).then_inc(wts_in, 16)

        @block.tensor
        def _(pe):
            def transposes(b, v):
                for i in range(2):
                    for q in range(2):
                        pe.wait_ge(e_ready, b * QT + 2 * i + q + 1)
                        for c in range(DC):
                            last = pe.transpose(ps_T[i][:, c, q * P:(q + 1) * P],
                                                e[:, v, 2 * i + q, c * P:(c + 1) * P], id32)
                    last.then_inc(eT_done, 1)

            def similarity(b, q):
                n = b * QT + q
                if q == 0:
                    pe.wait_ge(sT_ready, b + 1)
                if q > 1:
                    pe.wait_ge(exp_done, n - 1)
                for c in range(DC):
                    last = pe.matmul(ps_S[q % 2][:, :], sT[:, c, q * P:(q + 1) * P], ctxT[:, c, ds(b * S, S)],
                                     start=(c == 0), stop=(c == DC - 1))
                last.then_inc(S_done, 1)

            def attended(b, q):
                n = b * QT + q
                pe.wait_ge(exp_done, n + 1)
                if q:
                    pe.wait_ge(attT_ready, n)
                for k in range(QT):
                    last = pe.transpose(ps_A[:, k, :], att[:, q, k * P:(k + 1) * P], id32)
                last.then_inc(attT_done, 1)

            def context(b, q):
                n = b * QT + q
                pe.wait_ge(attT_ready, n + 1)
                if q:
                    pe.wait_ge(q_ready, n)
                for k in range(QT):
                    last = pe.matmul(ps_q[:, :], attT[:, q % 2, k, :], ctok[:, ds(b * QT + k, 1), :],
                                     start=(k == 0), stop=(k == QT - 1))
                last.then_inc(q_done, 1)

            def context_transposes(b, q):
                n = b * QT + q
                pe.wait_ge(q_ready, n + 1)
                if q:
                    pe.wait_ge(qT_ready, n)
                for c in range(DC):
                    last = pe.transpose(ps_qT[:, c, :], hq[:, q % 2, c * P:(c + 1) * P], id32)
                last.then_inc(qT_done, 1)

            def pooled(b, v):
                pe.wait_ge(ez_ready, b + 1)
                pe.matmul(ps_h[:, 2:3], ones[:, :], ezs[:, :], start=True, stop=True)
                for c in range(DC):
                    for q in range(QT):
                        last = pe.matmul(ps_h[:, c:c + 1], e[:, v, q, c * P:(c + 1) * P], ez[:, q:q + 1],
                                         start=(q == 0), stop=(q == QT - 1))
                last.then_inc(hc_done, 1)

            def features(b, v, q):
                n = b * QT + q
                if q == 0:
                    pe.wait_ge(wx_ready, b + 1)
                pe.wait_ge(eh_ready, n + 1)
                if q > 1:
                    pe.wait_ge(out_used, n - 1)
                cols = slice(q * P, (q + 1) * P)
                terms = [(eT[:, v, c, cols], wx[:, c, :]) for c in range(DC)]
                terms += [(hqT[:, c, cols], wqv[:, 1, c, :]) for c in range(DC)]
                terms += [(ehT[:, c, cols], wqv[:, 2, c, :]) for c in range(DC)]
                for i, (l, r) in enumerate(terms):
                    last = pe.matmul(ps_T[q % 2][:, 0, :], l, r, start=(i == 0), stop=(i == len(terms) - 1))
                last.then_inc(out_done, 1)

            pe.wait_ge(w_in, 16 * 5)
            pe.wait_ge(ctx_in, 32)
            pe.wait_ge(ones_ready, 1)
            pe.wait_ge(abs_done, 3)
            pe.matmul(ps_h[:, 4:7], ones[:, :], wabs[:, :], start=True, stop=True).then_inc(wsum_done, 1)
            pe.wait_ge(wstat_step, 1)
            with pe.Fori(0, B // 2) as half_b0:
                b0 = 2 * half_b0
                for v in range(2):
                    b = b0 + v
                    transposes(b, v)
                    for q in range(QT):
                        similarity(b, q)
                    for q in range(QT):
                        attended(b, q)
                        if q:
                            context(b, q - 1)
                        if q > 1:
                            context_transposes(b, q - 2)
                    context(b, QT - 1)
                    context_transposes(b, QT - 2)
                    pooled(b, v)
                    context_transposes(b, QT - 1)
                    for q in range(QT):
                        features(b, v, q)

        @block.vector
        def _(dve):
            ln_vector(dve)
            dve.wait_ge(rstd_ready, 2)
            dve.wait_ge(w_in, 16 * 5)
            dve.wait_ge(wsum_done, 1)
            dve.tensor_scalar(wstat[:, 0:3], ps_h[:, 4:7], 1.0 / (D * INNER), 1e-5, ALU.mult, ALU.max)\
               .then_inc(wstat_step, 1)
            dve.wait_ge(wstat_step, 1)
            dve.reciprocal(wstat[:, 3:6], wstat[:, 0:3]).then_inc(wstat_step, 1)

            with dve.Fori(0, B // 2) as half_b0:
                b0 = 2 * half_b0
                for v in range(2):
                    b = b0 + v
                    for q in range(QT):
                        n = b * QT + q
                        dve.tensor_scalar(e[:, v, q, :], x_sb[:, ds(n, 1), :].rearrange("p o d -> p (o d)"),
                                          mean[:, ds(n, 1)], rstd[:, ds(n, 1)], ALU.subtract, ALU.mult)\
                           .then_inc(e_ready, 1)
                    for i in range(2):
                        dve.wait_ge(eT_done, b * 2 + i + 1)
                        last = dve.tensor_copy(eT[:, v, :, i * 2 * P:(i + 1) * 2 * P], ps_T[i][:, :, :])
                    last.then_inc(eT_ready, 1)
                    dve.wait_ge(eT_ready, b + 1)
                    for c in range(DC):
                        last = dve.tensor_scalar(sT[:, c, :], eT[:, v, c, :], wsim[:, 1, c:c + 1],
                                                 wsim[:, 0, c:c + 1], ALU.mult, ALU.add)
                    last.then_inc(sT_ready, 1)
                    for q in range(QT):
                        last = dve.tensor_tensor_reduce(out=junk[:, q, :], in0=e[:, v, q, :], in1=w1[:, :], scale=1.0,
                                                        scalar=0.0, op0=ALU.mult, op1=ALU.add,
                                                        accum_out=own[:, q:q + 1])
                    last.then_inc(own_done, 1)
                    for q in range(QT):
                        dve.wait_ge(S_done, b * QT + q + 1)
                        dve.tensor_reduce(nmax[:, q:q + 1], ps_S[q % 2][:, :], AX_X, ALU.max, negate=True)\
                           .then_inc(max_ready, 1)
                    dve.wait_ge(max_ready, (b + 1) * QT)
                    dve.wait_ge(own_done, b + 1)
                    dve.tensor_tensor(z[:, 0, :], own[:, :], nmax[:, :], ALU.subtract).then_inc(z_half, 1)
                    dve.wait_ge(z_half, b + 1)
                    dve.tensor_scalar(z[:, 1, :], z[:, 0, :], bsim[:, 0:1], None, ALU.add).then_inc(z_ready, 1)
                    dve.wait_ge(exp_done, (b + 1) * QT)
                    dve.reciprocal(lrec[:, :], lsum[:, :]).then_inc(l_ready, 1)
                    dve.wait_ge(l_ready, b + 1)
                    dve.wait_ge(zmax_ready, b + 1)
                    dve.tensor_reduce(nz[:, :], z[:, 2, :], AX_X, ALU.max, negate=True).then_inc(nz_ready, 1)

                    def context(q):
                        n = b * QT + q
                        dve.wait_ge(q_done, n + 1)
                        dve.tensor_scalar(hq[:, q % 2, :], ps_q[:, :], lrec[:, q:q + 1], None, ALU.mult)\
                           .then_inc(q_ready, 1)

                    def context_transposed(q):
                        n = b * QT + q
                        dve.wait_ge(qT_done, n + 1)
                        dve.tensor_copy(hqT[:, :, q * P:(q + 1) * P], ps_qT[:, :, :]).then_inc(qT_ready, 1)
                    for q in range(QT):
                        context(q)
                        if q:
                            context_transposed(q - 1)
                    dve.wait_ge(hc_done, b + 1)
                    dve.reciprocal(rz[:, :], ps_h[:, 2:3]).then_inc(hc_step, 1)
                    dve.wait_ge(hc_step, b * 2 + 1)
                    dve.tensor_scalar(hc[:, :], ps_h[:, 0:2], rz[:, 0:1], None, ALU.mult).then_inc(hc_step, 1)
                    dve.wait_ge(hc_step, b * 2 + 2)
                    for c in range(DC):
                        last = dve.scalar_tensor_tensor(out=wx[:, c, :], in0=wqv[:, 3, c, :], scalar=hc[:, c:c + 1],
                                                        in1=wqv[:, 0, c, :], op0=ALU.mult, op1=ALU.add)
                    last.then_inc(wx_ready, 1)
                    context_transposed(QT - 1)
                    for q in range(QT):
                        n = b * QT + q
                        dve.wait_ge(out_done, n + 1)
                        dve.tensor_tensor(yb[:, q % 2, :], ps_T[q % 2][:, 0, :], bqv[:, :], ALU.add).then_inc(biased, 1)
                        dve.wait_ge(biased, n + 1)
                        xs = x_sb[:, ds(n, 1), :].rearrange("p o d -> p (o d)")
                        dve.scalar_tensor_tensor(out=xs, in0=yb[:, q % 2, :], scalar=per["gates"][:, 1:2], in1=xs,
                                                 op0=ALU.mult, op1=ALU.add).then_inc(out_used, 1)

        @block.scalar
        def _(act):
            act.wait_ge(wts_in, 16 * 3)
            for i in range(3):
                wait(act, abs_done, i)
                act.activation(wjunk[:, :], w32[:, i, :], ACT.Abs, accum_out=wabs[:, i:i + 1]).then_inc(abs_done, 1)
            with act.Fori(0, B) as b:
                for q in range(QT):
                    n = b * QT + q
                    act.wait_ge(max_ready, n + 1)
                    act.activation(att[:, q, :], ps_S[q % 2][:, :], ACT.Exp, bias=nmax[:, q:q + 1],
                                   accum_out=lsum[:, q:q + 1]).then_inc(exp_done, 1)
                for q in range(QT):
                    n = b * QT + q
                    act.wait_ge(attT_done, n + 1)
                    if q > 1:
                        act.wait_ge(q_done, n - 1)
                    act.copy(attT[:, q % 2, :, :], ps_A[:, :, :]).then_inc(attT_ready, 1)
                    if q == 0:
                        act.wait_ge(nz_ready, b + 1)
                        act.activation(ez[:, :], z[:, 1, :], ACT.Exp, bias=nz[:, 0:1], accum_out=ezs[:, 0:1])\
                           .then_inc(ez_ready, 1)

        @block.gpsimd
        def _(pool):
            pool.memset(ones[:, :], 1.0).then_inc(ones_ready, 1)
            ln_pool(pool)
            pool.wait_ge(wstat_step, 2)
            for i in range(3):
                pool.tensor_scalar(w32[:, i, :], w32[:, i, :], wstat[:, 3 + i:4 + i], MAGIC, ALU.mult, ALU.add)\
                    .then_inc(quant, 1)
                pool.wait_ge(quant, 3 * i + 1)
                pool.tensor_scalar(w32[:, i, :], w32[:, i, :], MAGIC + 1.0, MAGIC - 1.0, ALU.min, ALU.max)\
                    .then_inc(quant, 1)
                pool.wait_ge(quant, 3 * i + 2)
                pool.tensor_scalar(wq16[:, i, :], w32[:, i, :], 1.0, -MAGIC, ALU.mult, ALU.add).then_inc(quant, 1)
            for b in range(B):
                pool.wait_ge(z_ready, b + 1)
                pool.partition_all_reduce(z[:, 2, :], z[:, 1, :], P, bass.bass_isa.ReduceOp.max)\
                    .then_inc(zmax_ready, 1)
                for q in range(QT):
                    pool.wait_ge(qT_ready, b * QT + q + 1)
                    cols = slice(q * P, (q + 1) * P)
                    pool.tensor_tensor(ehT[:, :, cols], eT[:, b % 2, :, cols], hqT[:, :, cols], ALU.mult)\
                        .then_inc(eh_ready, 1)


def phase_bitffn(nc, per, wq16, wstat, out):
    x_sb, c16 = per["x"], per["c16"]
    id16 = c16[:, B_ID:B_ID + P]
    wg, wu = (wq16[:, i, :].rearrange("p (c n) -> p c n", c=DC) for i in range(2))
    wd = wq16[:, 2, :].rearrange("p (c n) -> p c n", c=IC)
    with ExitStack() as ctx:
        sb = lambda n, s, d: ctx.enter_context(nc.sbuf_tensor(n, s, d))
        ps = lambda n, s, d: ctx.enter_context(nc.psum_tensor(n, s, d))
        sem = lambda n: ctx.enter_context(nc.semaphore(n))
        xn = sb("xnD", [P, T, D], F32)
        amax = sb("amax", [P, 6, T], F32)
        gd = sb("gd", [P, 2], F32)
        xr = sb("xr", [P, 2, D], F32)
        xq = sb("xq", [P, 2, D], BF16)
        xqT = sb("xqT", [P, 2, DC, P], BF16)
        sg = sb("sgD", [P, 2, INNER], F32)
        t = sb("tD", [P, 2, INNER], F32)
        r = sb("rD", [P, 2, INNER], F32)
        hq = sb("hqD", [P, 2, INNER], BF16)
        hqT = sb("hqTD", [P, 2, IC, P], BF16)
        hs = sb("hs", [P, 2, 5], F32)
        mean, rstd, rstd_ready, ln_vector, ln_pool = row_statistics(nc, sb, sem, x_sb, "D")
        ps_x = ps("ps_x", [P, DC, P], BF16)
        ps_g = ps("ps_gD", [P, INNER], F32)
        ps_u = ps("ps_uD", [P, INNER], F32)
        ps_h = ps("ps_hD", [P, IC, P], BF16)
        ps_y = [ps(f"ps_yD{i}", [P, D], F32) for i in range(2)]
        lnd, small = sem("lnd"), sem("smallD")
        xr_done, xq_ready, xT_done, xT_ready = sem("xr_done"), sem("xq_readyD"), sem("xT_doneD"), sem("xT_readyD")
        gate_done, up_done, silu_done, t_ready = sem("gate_done"), sem("up_done"), sem("silu_doneD"), sem("t_ready")
        hstep, f_ready, r_ready, hq_ready = sem("hstep"), sem("f_ready"), sem("r_ready"), sem("hq_readyD")
        hT_done, hT_ready, y_done, y_used, stored = (sem("hT_done"), sem("hT_readyD"), sem("y_doneD"), sem("y_usedD"),
                                                     sem("stored"))
        block = ctx.enter_context(nc.Block())
        AMAX, INV, SX, AG, AU = range(5)

        @block.sync
        def _(sp):
            ov = out.rearrange("b (q p) d -> p (b q) d", p=P)
            with sp.Fori(0, T) as n:
                sp.wait_ge(y_used, n + 1)
                sp.dma_start(ov[:, ds(n, 1), :], x_sb[:, ds(n, 1), :]).then_inc(stored, 16)
            sp.wait_ge(stored, 16 * T)

        @block.gpsimd
        def _(pool):
            ln_pool(pool)

        @block.vector
        def _(dve):
            ln_vector(dve)
            dve.wait_ge(rstd_ready, 2)
            with dve.Fori(0, T) as n:
                dve.tensor_scalar(xn[:, ds(n, 1), :], x_sb[:, ds(n, 1), :], mean[:, ds(n, 1)], rstd[:, ds(n, 1)],
                                  ALU.subtract, ALU.mult).then_inc(lnd, 1)
                dve.wait_ge(lnd, n + 1)
                dve.tensor_reduce(amax[:, 5, ds(n, 1)], xn[:, ds(n, 1), :], AX_X, ALU.max,
                                  apply_absolute_value=True).then_inc(small, 1)
            dve.wait_ge(small, T)
            dve.tensor_scalar(amax[:, AMAX, :], amax[:, 5, :], 1e-5, None, ALU.max).then_inc(small, 1)
            dve.wait_ge(small, T + 1)
            dve.reciprocal(amax[:, INV, :], amax[:, AMAX, :])
            dve.tensor_scalar(amax[:, AG, :], amax[:, AMAX, :], wstat[:, 0:1], 1.0 / 127.0, ALU.mult, ALU.mult)
            dve.tensor_scalar(amax[:, AU, :], amax[:, AMAX, :], wstat[:, 1:2], 1.0 / 127.0, ALU.mult, ALU.mult)
            dve.tensor_scalar(gd[:, 0:1], wstat[:, 2:3], per["gates"][:, 3:4], 1.0 / 127.0, ALU.mult, ALU.mult)\
               .then_inc(small, 1)
            dve.wait_ge(small, T + 2)
            dve.tensor_scalar(amax[:, SX, :], amax[:, INV, :], 127.0, None, ALU.mult).then_inc(small, 1)
            dve.wait_ge(small, T + 3)

            def quantise(n, u):
                dve.tensor_scalar(xr[:, u, :], xn[:, ds(n, 1), :].rearrange("p o d -> p (o d)"),
                                  amax[:, SX, ds(n, 1)], MAGIC, ALU.mult, ALU.add).then_inc(xr_done, 1)
                dve.wait_ge(xr_done, n + 1)
                wait(dve, xT_done, n - 1)
                dve.tensor_scalar(xq[:, u, :], xr[:, u, :], -MAGIC, 127.0, ALU.add, ALU.min).then_inc(xq_ready, 1)

            def transposed(n, u):
                dve.wait_ge(xT_done, n + 1)
                wait(dve, up_done, n - 1)
                dve.tensor_copy(xqT[:, u, :, :], ps_x[:, :, :]).then_inc(xT_ready, 1)

            def hidden(n, u):
                dve.wait_ge(up_done, n + 1)
                dve.wait_ge(silu_done, n + 1)
                wait(dve, r_ready, n - 1)
                dve.tensor_tensor(t[:, u, :], sg[:, u, :], ps_u[:, :], ALU.mult).then_inc(t_ready, 1)
                dve.wait_ge(t_ready, n + 1)
                dve.tensor_reduce(hs[:, u, 0:1], t[:, u, :], AX_X, ALU.max, apply_absolute_value=True)\
                   .then_inc(hstep, 1)
                dve.wait_ge(hstep, 3 * n + 1)
                dve.tensor_scalar(hs[:, u, 1:2], hs[:, u, 0:1], amax[:, AU, ds(n, 1)], 1e-5, ALU.mult, ALU.max)\
                   .then_inc(hstep, 1)
                dve.wait_ge(hstep, 3 * n + 2)
                dve.reciprocal(hs[:, u, 2:3], hs[:, u, 1:2]).then_inc(hstep, 1)
                dve.wait_ge(hstep, 3 * n + 3)
                dve.tensor_scalar(hs[:, u, 4:5], hs[:, u, 1:2], gd[:, 0:1], None, ALU.mult)
                dve.tensor_scalar(hs[:, u, 3:4], hs[:, u, 2:3], amax[:, AU, ds(n, 1)], 127.0, ALU.mult, ALU.mult)\
                   .then_inc(f_ready, 1)

            def rounded(n, u):
                dve.wait_ge(r_ready, n + 1)
                wait(dve, hT_done, n - 1)
                dve.tensor_scalar(hq[:, u, :], r[:, u, :], -MAGIC, 127.0, ALU.add, ALU.min).then_inc(hq_ready, 1)

            def residual(n, u):
                dve.wait_ge(y_done, n + 1)
                xs = x_sb[:, ds(n, 1), :].rearrange("p o d -> p (o d)")
                dve.scalar_tensor_tensor(out=xs, in0=ps_y[u][:, :], scalar=hs[:, u, 4:5], in1=xs,
                                         op0=ALU.mult, op1=ALU.add).then_inc(y_used, 1)

            def step(n, u, lo2, lo1, hi):
                if lo2:
                    residual(n - 2, u)
                if hi:
                    quantise(n + 1, 1 - u)
                    transposed(n + 1, 1 - u)
                if lo1:
                    rounded(n - 1, 1 - u)
            quantise(0, 0)
            transposed(0, 0)
            step(0, 0, False, False, True)
            hidden(0, 0)
            step(1, 1, False, True, True)
            hidden(1, 1)
            with dve.Fori(1, (T - 2) // 2) as half_n0:
                n0 = 2 * half_n0
                for u in range(2):
                    step(n0 + u, u, True, True, True)
                    hidden(n0 + u, u)
            step(T - 2, 0, True, True, True)
            hidden(T - 2, 0)
            step(T - 1, 1, True, True, False)
            hidden(T - 1, 1)
            step(T, 0, True, True, False)
            residual(T - 1, 1)

        @block.scalar
        def _(act):
            def silu(n, u):
                act.wait_ge(gate_done, n + 1)
                wait(act, t_ready, n - 1)
                act.activation(sg[:, u, :], ps_g[:, :], ACT.Silu, scale=amax[:, AG, ds(n, 1)]).then_inc(silu_done, 1)

            def rounding(n, u):
                act.wait_ge(f_ready, n + 1)
                wait(act, hq_ready, n - 1)
                act.activation(r[:, u, :], t[:, u, :], ACT.Copy, scale=hs[:, u, 3:4], bias=MAGIC).then_inc(r_ready, 1)

            def transposed(n, u):
                act.wait_ge(hT_done, n + 1)
                wait(act, y_done, n - 1)
                act.copy(hqT[:, u, :, :], ps_h[:, :, :]).then_inc(hT_ready, 1)
            act.wait_ge(small, T + 3)
            silu(0, 0)
            rounding(0, 0)
            silu(1, 1)
            transposed(0, 0)
            rounding(1, 1)
            with act.Fori(1, T // 2) as half_n0:
                n0 = 2 * half_n0
                for u in range(2):
                    silu(n0 + u, u)
                    transposed(n0 + u - 1, 1 - u)
                    rounding(n0 + u, u)
            transposed(T - 1, 1)

        @block.tensor
        def _(pe):
            def x_transposes(n, u):
                pe.wait_ge(xq_ready, n + 1)
                wait(pe, xT_ready, n)
                for c in range(DC):
                    last = pe.transpose(ps_x[:, c, :], xq[:, u, c * P:(c + 1) * P], id16)
                last.then_inc(xT_done, 1)

            def gate_up(n, u):
                pe.wait_ge(xT_ready, n + 1)
                for out_, w, used, done in ((ps_g, wg, silu_done, gate_done), (ps_u, wu, t_ready, up_done)):
                    wait(pe, used, n)
                    for half in range(2):
                        cols = slice(half * 512, half * 512 + 512)
                        for c in range(DC):
                            last = pe.matmul(out_[:, cols], xqT[:, u, c, :], w[:, c, cols], start=(c == 0),
                                             stop=(c == DC - 1))
                    last.then_inc(done, 1)

            def h_transposes(n, u):
                pe.wait_ge(hq_ready, n + 1)
                wait(pe, hT_ready, n)
                for c in range(IC):
                    last = pe.transpose(ps_h[:, c, :], hq[:, u, c * P:(c + 1) * P], id16)
                last.then_inc(hT_done, 1)

            def down(n, u):
                pe.wait_ge(hT_ready, n + 1)
                wait(pe, y_used, n - 1)
                for c in range(IC):
                    last = pe.matmul(ps_y[u][:, :], hqT[:, u, c, :], wd[:, c, :], start=(c == 0), stop=(c == IC - 1))
                last.then_inc(y_done, 1)
            x_transposes(0, 0)
            x_transposes(1, 1)
            gate_up(0, 0)
            x_transposes(2, 0)
            gate_up(1, 1)
            h_transposes(0, 0)
            down(0, 0)
            with pe.Fori(1, (T - 2) // 2) as half_n0:
                n0 = 2 * half_n0
                for u in range(2):
                    x_transposes(n0 + u + 1, 1 - u)
                    gate_up(n0 + u, u)
                    h_transposes(n0 + u - 1, 1 - u)
                    down(n0 + u - 1, 1 - u)
            x_transposes(T - 1, 1)
            gate_up(T - 2, 0)
            h_transposes(T - 3, 1)
            down(T - 3, 1)
            gate_up(T - 1, 1)
            h_transposes(T - 2, 0)
            down(T - 2, 0)
            h_transposes(T - 1, 1)
            down(T - 1, 1)


def build(nc, a, out, stop=99):
    outer = ExitStack()
    with outer:
        sb = lambda n, s, d: outer.enter_context(nc.sbuf_tensor(n, s, d))
        per = {
            "x": sb("x", [P, T, D], F32), "c32": sb("c32", [P, C32], F32), "c16": sb("c16", [P, C16], BF16),
            "mask_u8": sb("mask_u8", [P, T], U8), "mask": sb("mask", [P, T], F32),
            "gates_raw": sb("gates_raw", [P, 4], F32), "gates": sb("gates", [P, 4], F32),
        }
        phase_load(nc, a, per)
        with ExitStack() as ctx:
            sba = lambda n, s, d: ctx.enter_context(nc.sbuf_tensor(n, s, d))
            qs = sba("qs", [P, B * H, S], BF16)
            ks = sba("ks", [P, B * H, S], BF16)
            with ExitStack() as inner:
                va = inner.enter_context(nc.sbuf_tensor("va", [P, STEPS, QT * G * (HD + 1)], F32))
                phase_prepare(nc, a, per, qs, ks, va)
                phase_attend(nc, per, qs, ks, va)
            phase_project(nc, a, per, qs)
        if stop > 1:
            with ExitStack() as ctx:
                sbb = lambda n, s, d: ctx.enter_context(nc.sbuf_tensor(n, s, d))
                xT_all = sbb("xT_all", [P, DC, T * P], F32)
                nselT = sbb("nselT", [P, T * P], BF16)
                down = sbb("down", [P, NX, D], F32)
                phase_route(nc, a, per, xT_all, nselT, down)
                phase_experts(nc, a, per, xT_all, nselT, down)
        if stop > 2:
            with ExitStack() as ctx:
                sbc = lambda n, s, d: ctx.enter_context(nc.sbuf_tensor(n, s, d))
                w32 = sbc("w32", [P, 3, 2 * INNER], F32)
                wq16 = sbc("wq16", [P, 3, 2 * INNER], BF16)
                wstat = sbc("wstat", [P, 6], F32)
                phase_coattend(nc, a, per, w32, wq16, wstat)
                if stop > 3:
                    phase_bitffn(nc, per, wq16, wstat, out)
        if stop <= 3:
            with ExitStack() as ctx:
                st = ctx.enter_context(nc.semaphore("st"))
                block = ctx.enter_context(nc.Block())

                @block.sync
                def _(sp):
                    sp.dma_start(out.rearrange("b (q p) d -> p (b q) d", p=P), per["x"][:, :, :]).then_inc(st, 16)
                    sp.wait_ge(st, 16)


def constants():
    import numpy as np

    c32 = np.zeros((P, C32), np.float32)
    c32[:, C_ID:C_ID + P] = np.eye(P)
    for m in range(P):
        c32[HPAD * (m // HPAD) + HD, C_SEL + m] = 1.0
    inv = (np.float32(1.0) / np.float32(10000.0) ** (np.arange(0, HD, 2, dtype=np.float32) / np.float32(HD)))
    f = np.outer(np.arange(S, dtype=np.float32), inv.astype(np.float32)).astype(np.float32)
    cos = np.cos(f.astype(np.float64)).astype(np.float32)
    sin = np.sin(f.astype(np.float64)).astype(np.float32)
    cos, sin = np.concatenate([cos, cos], -1), np.concatenate([-sin, sin], -1)
    c32[:, C_COS:C_SIN] = cos.reshape(QT, P, HD).transpose(1, 0, 2).reshape(P, -1)
    c32[:, C_SIN:C_TRI] = sin.reshape(QT, P, HD).transpose(1, 0, 2).reshape(P, -1)
    c32[:, C_TRI:C_TRI + E * E] = np.tril(np.ones((E, E)), -1).reshape(1, -1)
    c16 = np.zeros((P, C16), np.float32)
    c16[:, B_ID:B_ID + P] = np.eye(P)
    pre = np.zeros((2, H, XROWS), np.float32)
    pre[0, :, MASK_ROW] = 1.0
    for h in range(H):
        pre[1, h, 3 * (h % G):3 * (h % G) + 3] = 1.0
    c16[:, B_PRE:C16] = pre.reshape(1, -1)
    skip = np.zeros((P, E, P), np.float32)
    for e in range(E):
        skip[e, e, :] = -BIG
    bits = lambda v: (v.view(np.uint32) >> 16).astype(np.uint16)
    return c32, bits(c16), bits(skip)


def layout(inputs):
    import numpy as np

    i = {k: np.asarray(v) for k, v in inputs.items()}
    row = lambda v: np.ascontiguousarray(v).reshape(1, -1)
    chunks = lambda w: np.ascontiguousarray(w.reshape(-1, P, w.shape[-1]).transpose(1, 0, 2))
    a = {"x": i["x"], "ctx": i["ctx_1024"]}
    ctxT = i["ctx_1024"].reshape(T * P, D).T
    a["ctxTC"] = chunks(ctxT)
    a["ctxT"] = np.ascontiguousarray(ctxT.reshape(DC, P, T, P).transpose(2, 1, 0, 3))
    a["mask"] = np.ascontiguousarray(i["mask_BxS2_bf1"].reshape(T, P).T).view(np.uint8)
    a["gates"] = row(np.concatenate([i["g_xattn"], i["g_ffn"]]))
    a["wq"], a["wk"], a["wv"] = (chunks(i[f"L0_xattn_W{n}"].T) for n in "qkv")
    a["bqk"] = row(np.concatenate([i["L0_xattn_bq"], i["L0_xattn_bk"]]))
    a["bv"], a["bp"] = row(i["L0_xattn_bv"]), row(i["L0_xattn_bp"])
    a["wp"] = np.ascontiguousarray(i["L0_xattn_Wp"].T.reshape(NG, G, HD, D).transpose(1, 2, 0, 3))
    a["gate_w"] = chunks(i["L0_ffn_gate_w"].T)
    a["lb"] = row(i["L0_ffn_lb_bias"])
    gate = np.concatenate([i["L0_ffn_expert_gate_w"], i["L0_ffn_shared_gate_w"].reshape(SH, I, D)])
    up = np.concatenate([i["L0_ffn_expert_up_w"], i["L0_ffn_shared_up_w"].reshape(SH, I, D)])
    a["up"] = np.ascontiguousarray(np.stack([gate, up], 1).reshape(NX, 2, I, DC, P).transpose(0, 4, 1, 3, 2))
    down = np.concatenate([i["L0_ffn_expert_down_w"].transpose(2, 0, 1),
                           i["L0_ffn_shared_down_w"].T.reshape(SH, I, D).transpose(1, 0, 2)], 1)
    a["down"] = np.ascontiguousarray(down)
    ws = i["L1_xattn_w_sim"].reshape(3, DC, P)
    a["wsim"] = np.ascontiguousarray(ws[1:].transpose(2, 0, 1))
    a["w1"] = row(i["L1_xattn_w_sim"][:D])
    a["bsim"], a["bqv"] = row(i["L1_xattn_b_sim"]), row(i["L1_xattn_b_qv"])
    a["wqv"] = np.ascontiguousarray(i["L1_xattn_W_qv"].reshape(4, DC, P, D).transpose(2, 0, 1, 3))
    a["wg"], a["wu"], a["wd"] = (chunks(i[f"L1_ffn_w_{n}"].T).reshape(P, -1) for n in ("gate", "up", "down"))
    a["c32"], a["c16"], a["skip"] = constants()
    return a


def kernel(**inputs):
    import numpy as np
    import concourse.bacc as bacc
    from concourse.bass_utils import run_bass_kernel_spmd as run

    nc = bacc.Bacc("TRN2", target_bir_lowering=False, num_devices=1)
    arrays, args = {}, {}
    for name, v in layout(inputs).items():
        v = np.ascontiguousarray(v)
        arrays[f"in_{name}"] = v
        args[name] = nc.dram_tensor(f"in_{name}", v.shape, mybir.dt.from_np(v.dtype), kind="ExternalInput").ap()
    out = nc.dram_tensor("out", (B, S, D), F32, kind="ExternalOutput").ap()
    build(nc, args, out)
    return run(nc, [arrays], core_ids=[0]).results[0]["out"]
```

```python
from contextlib import ExitStack

import concourse.bass as bass
from concourse import mybir
from concourse.alu_op_type import AluOpType as ALU

ACT = mybir.ActivationFunctionType
F32 = mybir.dt.float32
BF16 = mybir.dt.bfloat16
U8 = mybir.dt.uint8
U16 = mybir.dt.uint16
AX_X = mybir.AxisListType.X
ds = bass.ds

P = 128
B = 4
S = 512
D = 256
DC = D // P
QT = S // P
T = B * QT
H = 16
HD = D // H
G = 4
NG = H // G
STEPS = B * NG
E = 8
I = 128
SH = 2
NX = E + SH
INNER = 1024
IC = INNER // P
EPS = 1e-5
BIG = 1e30
HPAD = 32
XROWS = 32
MASK_ROW = 3 * G
SCALE = HD ** -0.5
MAGIC = 1.5 * 2.0 ** 23

C_ID, C_COS, C_SIN, C_TRI, C32 = 0, 128, 192, 256, 320
B_ID, B_PRE, C16 = 0, 128, 128 + 2 * H * XROWS

Q1, Q2, Q3 = slice(0, 3), slice(3, 5), slice(5, 6)
K1, K2, K3 = slice(1, 6, 2), slice(2, 5, 2), slice(0, 1)


def wait(eng, sem, value):
    if not isinstance(value, int) or value > 0:
        eng.wait_ge(sem, value)


def carve(region, sizes):
    views, lo = [], 0
    for shape in sizes:
        size = 1
        for n in shape:
            size *= n
        v = region[:, lo:lo + size]
        lo += size
        if len(shape) == 2:
            v = v.rearrange("p (a b) -> p a b", a=shape[0])
        if len(shape) == 3:
            v = v.rearrange("p (a b c) -> p a b c", a=shape[0], b=shape[1])
        views.append(v)
    return views


def row_statistics(nc, sb, sem, per, tag, halves=False):
    st, x_sb = per["st"], per["x"]
    tmp = sb("lntmp" + tag, [P, 4, T], F32)
    mean = sb("mean" + tag, [P, T], F32)
    rstd = sb("rstd" + tag, [P, T], F32)
    power = sb("power" + tag, [P, T], F32)
    chain = sem("ln_chain" + tag)
    var_ready = sem("var_ready" + tag)
    rstd_ready = sem("rstd_ready" + tag)

    def vector(dve):
        if halves:
            for t in range(T):
                last = dve.bn_stats(st[:, t, :], x_sb[:, t, :])
            last.then_inc(chain, 1)
            dve.wait_ge(chain, 1)
        n = int(halves)
        dve.tensor_tensor(tmp[:, 0, :], st[:, :, 1], st[:, :, 4], ALU.subtract)
        dve.tensor_tensor(tmp[:, 1, :], st[:, :, 1], st[:, :, 4], ALU.add)
        dve.tensor_tensor(tmp[:, 2, :], st[:, :, 2], st[:, :, 5], ALU.add).then_inc(chain, 1)
        dve.wait_ge(chain, n + 1)
        dve.tensor_tensor(tmp[:, 3, :], tmp[:, 0, :], tmp[:, 0, :], ALU.mult)
        dve.tensor_scalar(mean[:, :], tmp[:, 1, :], 0.5, None, ALU.mult).then_inc(chain, 1)
        dve.wait_ge(chain, n + 2)
        dve.tensor_scalar(tmp[:, 0, :], tmp[:, 3, :], 0.25, EPS, ALU.mult, ALU.add).then_inc(chain, 1)
        dve.wait_ge(chain, n + 3)
        dve.scalar_tensor_tensor(out=tmp[:, 1, :], in0=tmp[:, 2, :], scalar=1.0 / D, in1=tmp[:, 0, :],
                                 op0=ALU.mult, op1=ALU.add).then_inc(var_ready, 1)

    def pool(pool_):
        pool_.memset(power[:, :], -0.5).then_inc(rstd_ready, 1)
        pool_.wait_ge(rstd_ready, 1)
        pool_.wait_ge(var_ready, 1)
        pool_.tensor_tensor(rstd[:, :], tmp[:, 1, :], power[:, :], ALU.pow).then_inc(rstd_ready, 1)

    return mean, rstd, rstd_ready, vector, pool


def normalise_batch(pool, per, ffn, b):
    st, x_sb, tmp, steps = per["st"], per["x"], ffn["tmp"], ffn["steps"]
    own = slice(b * QT, (b + 1) * QT)
    ready = 5 * b
    if b == 0:
        pool.memset(ffn["power"][:, :], -0.5).then_inc(ffn["power_ready"], 1)
        pool.wait_ge(ffn["power_ready"], 1)
    pool.wait_ge(ffn["stats_done"], (b + 1) * QT)
    pool.tensor_tensor(tmp[:, 0, own], st[:, own, 1], st[:, own, 4], ALU.subtract)
    pool.tensor_tensor(tmp[:, 1, own], st[:, own, 1], st[:, own, 4], ALU.add)
    pool.tensor_tensor(tmp[:, 2, own], st[:, own, 2], st[:, own, 5], ALU.add).then_inc(steps, 1)
    pool.wait_ge(steps, ready + 1)
    pool.tensor_tensor(tmp[:, 3, own], tmp[:, 0, own], tmp[:, 0, own], ALU.mult)
    pool.tensor_scalar(tmp[:, 4, own], tmp[:, 1, own], 0.5, None, ALU.mult)
    pool.tensor_scalar(tmp[:, 5, own], tmp[:, 2, own], 1.0 / D, None, ALU.mult).then_inc(steps, 1)
    pool.wait_ge(steps, ready + 2)
    pool.tensor_scalar(tmp[:, 6, own], tmp[:, 3, own], 0.25, EPS, ALU.mult, ALU.add).then_inc(steps, 1)
    pool.wait_ge(steps, ready + 3)
    pool.tensor_tensor(tmp[:, 7, own], tmp[:, 5, own], tmp[:, 6, own], ALU.add).then_inc(steps, 1)
    pool.wait_ge(steps, ready + 4)
    pool.tensor_tensor(tmp[:, 8, own], tmp[:, 7, own], ffn["power"][:, 0:QT], ALU.pow).then_inc(steps, 1)
    pool.wait_ge(steps, ready + 5)
    for t in range(b * QT, (b + 1) * QT):
        last = pool.tensor_scalar(ffn["xn"][:, t, :], x_sb[:, t, :], tmp[:, 4, t:t + 1], tmp[:, 8, t:t + 1],
                                  ALU.subtract, ALU.mult)
    last.then_inc(ffn["normed"], 1)


def phase_load(nc, a, per):
    with ExitStack() as ctx:
        sem = lambda n: ctx.enter_context(nc.semaphore(n))
        loaded, gates = sem("loaded"), sem("gates")
        block = ctx.enter_context(nc.Block())

        @block.sync
        def _(sp):
            xv = a["x"].rearrange("b (q p) d -> p (b q) d", p=P)
            for b in range(B):
                sp.dma_start(per["x"][:, 4 * b:4 * b + 4, :], xv[:, 4 * b:4 * b + 4, :]).then_inc(loaded, 16)
            sp.wait_ge(loaded, 16 * (B + 3))

        @block.scalar
        def _(act):
            act.dma_start(per["gates_raw"][:, :], a["gates"].to_broadcast([P, 4])).then_inc(gates, 16)
            act.dma_start(per["c32"][:, :], a["c32"]).then_inc(loaded, 16)
            act.dma_start(per["c16"][:, :].bitcast(U16), a["c16"]).then_inc(loaded, 16)
            act.dma_start(per["mask_u8"][:, :], a["mask"]).then_inc(loaded, 16)
            act.wait_ge(gates, 16)
            act.activation(per["gates"][:, :], per["gates_raw"][:, :], ACT.Tanh)


def phase_prepare(nc, a, per, qs, ks, va):
    x_sb, c32, c16 = per["x"], per["c32"], per["c16"]
    id32 = c32[:, C_ID:C_ID + P]
    id16 = c16[:, B_ID:B_ID + P]
    cos = c32[:, C_COS:C_SIN].rearrange("p (q d) -> p q d", q=QT)
    sin = c32[:, C_SIN:C_TRI].rearrange("p (q d) -> p q d", q=QT)
    preset = c16[:, B_PRE:C16].rearrange("p (h r) -> p h r", r=XROWS)
    with ExitStack() as ctx:
        sb = lambda n, s, d: ctx.enter_context(nc.sbuf_tensor(n, s, d))
        ps = lambda n, s, d: ctx.enter_context(nc.psum_tensor(n, s, d))
        sem = lambda n: ctx.enter_context(nc.semaphore(n))
        wq, wk, wv = (sb(n, [P, DC, D], F32) for n in ("wq", "wk", "wv"))
        bqk = sb("bqk", [P, 2 * D], F32)
        bv = sb("bv", [P, D], F32)
        ctxT = sb("ctxT", [P, 2, DC, P], F32)
        xn = sb("xn", [P, 2, D], F32)
        xnT = sb("xnT", [P, 2, DC, P], F32)
        qkb = sb("qkb", [P, 2, 2 * H, HD], F32)
        rope2 = sb("rope2", [P, 2 * H, HD], F32)
        qkr = sb("qkr", [P, 2 * H, HD], F32)
        rest = qkb
        stack = sb("stack", [P, 2, 2 * H, P], BF16)
        mbias = sb("mbias", [P, T], F32)
        mean, rstd, rstd_ready, ln_vector, ln_pool = row_statistics(nc, sb, sem, per, "A", halves=True)
        ps_st = [ps(f"ps_st{i}", [P, 8, P], BF16) for i in range(4)]
        ps_T = ps("ps_T", [P, DC, P], F32)
        ps_qk = ps("ps_qk", [P, 2 * D], F32)
        ps_v = ps("ps_v", [P, D], F32)

        weights, ctx_in = sem("weights"), [sem("ctx_in0"), sem("ctx_in1")]
        xn_ready, xT_done, xT_copied = sem("xn_ready"), sem("xT_done"), sem("xT_copied")
        proj_done, qk_copied, v_copied = sem("proj_done"), sem("qk_copied"), sem("v_copied")
        vb_done, mask_done = sem("vb_done"), sem("mask_done")
        rope_half, rope_done, rest1_done = sem("rope_half"), sem("rope_done"), sem("rest1_done")
        part1_done, part2_done, part3_done = sem("part1_done"), sem("part2_done"), sem("part3_done")
        stackT_done, stackT_v, stackT_a = sem("stackT_done"), sem("stackT_v"), sem("stackT_a")
        block = ctx.enter_context(nc.Block())

        va_v = va[:, :, :].rearrange("p s (k j d) -> p s k j d", k=QT, j=G)
        parts = lambda u, first: stack[:, u, first:first + H, 0:96].rearrange("p h (s d) -> p h s d", d=HD)

        def stack_out(copy, dst, i, n):
            at = (n // QT) * H + 8 * (i % 2)
            return copy(dst[:, ds(at, 8), ds((n % QT) * P, P)], ps_st[i][:, :, :])

        @block.sync
        def _(sp):
            for w, n in ((wq, "wq"), (wk, "wk"), (wv, "wv")):
                sp.dma_start(w[:, :, :], a[n]).then_inc(weights, 16)
            sp.dma_start(bqk[:, :], a["bqk"].to_broadcast([P, 2 * D])).then_inc(weights, 16)
            sp.dma_start(bv[:, :], a["bv"].to_broadcast([P, D])).then_inc(weights, 16)

            def load(n, u):
                wait(sp, proj_done, n - 1)
                sp.dma_start(ctxT[:, u, :, :], a["ctxT"][ds(n, 1), :, :, :]).then_inc(ctx_in[u], 16)
            load(0, 0)
            load(1, 1)
            with sp.Fori(1, T // 2) as half_n0:
                n0 = 2 * half_n0
                for u in range(2):
                    load(n0 + u, u)

        @block.vector
        def _(dve):
            for u in range(2):
                dve.tensor_copy(stack[:, u, :, 96:128], preset)
            dve.tensor_copy(per["mask"][:, :], per["mask_u8"][:, :]).then_inc(mask_done, 1)
            dve.wait_ge(mask_done, 1)
            dve.tensor_scalar(mbias[:, :], per["mask"][:, :], BIG, -BIG, ALU.mult, ALU.add).then_inc(mask_done, 1)
            ln_vector(dve)
            dve.wait_ge(rstd_ready, 2)
            dve.wait_ge(mask_done, 2)
            dve.wait_ge(weights, 16 * 5)
            for k in range(QT):
                m = per["mask"][:, k:T:QT].rearrange("p (b g j) -> p b g j", g=1, j=1)
                vm = va_v[:, :, k, :, HD].rearrange("p (b g) j -> p b g j", b=B)
                dve.tensor_copy(vm, m.broadcast_to([P, B, NG, G]))

            def normalise(n, u):
                wait(dve, xT_done, n - 1)
                dve.tensor_scalar(xn[:, u, :], x_sb[:, ds(n, 1), :], mean[:, ds(n, 1)], rstd[:, ds(n, 1)],
                                  ALU.subtract, ALU.mult).then_inc(xn_ready, 1)

            def third_part(n, u):
                dve.wait_ge(part2_done, n + 1)
                for first, slot, src in ((0, Q3, Q2), (H, K3, K2)):
                    last = dve.tensor_tensor(parts(u, first)[:, :, slot.start, :], rest[:, u, first:first + H, :],
                                             parts(u, first)[:, :, src.start, :], ALU.subtract)
                dve.tensor_copy(stack[:, u, H:2 * H, 96 + MASK_ROW],
                                mbias[:, ds(n, 1)].broadcast_to([P, H])).then_inc(part3_done, 1)

            def stack_copy(n):
                dve.wait_ge(stackT_done, 4 * n + 2)
                for i in (0, 1):
                    last = stack_out(dve.tensor_copy, qs, i, n)
                last.then_inc(stackT_v, 1)

            def projections(n, u):
                dve.wait_ge(proj_done, n + 1)
                dve.tensor_tensor(qkb[:, u, :, :], ps_qk[:, :].rearrange("p (h d) -> p h d", d=HD),
                                  bqk[:, :].rearrange("p (h d) -> p h d", d=HD), ALU.add).then_inc(qk_copied, 1)
                out = va_v[:, ds((n // QT) * NG, NG), ds(n % QT, 1), :, 0:HD].rearrange("p g k j d -> p (g k) j d")
                heads = lambda v: v[:, :].rearrange("p (g j d) -> p g j d", g=NG, j=G)
                dve.tensor_tensor(out, heads(ps_v), heads(bv), ALU.add).then_inc(vb_done, 1)
                dve.wait_ge(vb_done, n + 1)
                dve.tensor_scalar(out, out, per["mask"][:, ds(n, 1)], None, ALU.mult).then_inc(v_copied, 1)

            def transposed(n, u):
                dve.wait_ge(xT_done, n + 1)
                wait(dve, proj_done, n - 1)
                dve.tensor_copy(xnT[:, u, :, :], ps_T[:, :, :]).then_inc(xT_copied, 1)

            def step(n, u, lo, hi):
                if lo:
                    third_part(n - 2, u)
                if hi:
                    normalise(n + 1, 1 - u)
                if lo:
                    stack_copy(n - 2)
                if hi:
                    transposed(n + 1, 1 - u)
            normalise(0, 0)
            transposed(0, 0)
            step(0, 0, False, True)
            projections(0, 0)
            step(1, 1, False, True)
            projections(1, 1)
            with dve.Fori(1, (T - 2) // 2) as half_n0:
                n0 = 2 * half_n0
                for u in range(2):
                    step(n0 + u, u, True, True)
                    projections(n0 + u, u)
            step(T - 2, 0, True, True)
            projections(T - 2, 0)
            step(T - 1, 1, True, False)
            projections(T - 1, 1)
            step(T, 0, True, False)
            step(T + 1, 1, True, False)

        @block.scalar
        def _(act):
            def first_part(n, u):
                act.wait_ge(rope_done, n + 1)
                wait(act, stackT_done, 4 * (n - 1))
                for first, slots in ((0, Q1), (H, K1)):
                    src = qkr[:, first:first + H, :].rearrange("p h (o d) -> p h o d", o=1)
                    last = act.copy(parts(u, first)[:, :, slots, :], src.broadcast_to([P, H, 3, HD]))
                last.then_inc(part1_done, 1)

            def second_part(n, u):
                act.wait_ge(rest1_done, n + 1)
                for first, slots in ((0, Q2), (H, K2)):
                    src = rest[:, u, first:first + H, :].rearrange("p h (o d) -> p h o d", o=1)
                    last = act.copy(parts(u, first)[:, :, slots, :], src.broadcast_to([P, H, 2, HD]))
                last.then_inc(part2_done, 1)

            def stack_copy(n):
                for i in (2, 3):
                    act.wait_ge(stackT_done, 4 * n + i + 1)
                    last = stack_out(act.copy, ks, i, n)
                last.then_inc(stackT_a, 1)

            first_part(0, 0)
            second_part(0, 0)
            first_part(1, 1)
            with act.Fori(1, T // 2) as half_n0:
                n0 = 2 * half_n0
                for u in range(2):
                    stack_copy(n0 + u - 2)
                    second_part(n0 + u - 1, 1 - u)
                    first_part(n0 + u, u)
            stack_copy(T - 2)
            second_part(T - 1, 1)
            stack_copy(T - 1)

        @block.gpsimd
        def _(pool):
            ln_pool(pool)

            def rope(n, u):
                pool.wait_ge(qk_copied, n + 1)
                wait(pool, rope_done, n)
                wait(pool, rest1_done, n)
                c = cos[:, ds(n % QT, 1), :].broadcast_to([P, 2 * H, HD])
                s = sin[:, ds(n % QT, 1), :]
                lo, hi = slice(0, HD // 2), slice(HD // 2, HD)
                pool.tensor_tensor(qkr[:, :, :], qkb[:, u, :, :], c, ALU.mult)
                pool.tensor_tensor(rope2[:, :, lo], qkb[:, u, :, hi], s[:, :, lo].broadcast_to([P, 2 * H, HD // 2]),
                                   ALU.mult)
                pool.tensor_tensor(rope2[:, :, hi], qkb[:, u, :, lo], s[:, :, hi].broadcast_to([P, 2 * H, HD // 2]),
                                   ALU.mult).then_inc(rope_half, 1)
                pool.wait_ge(rope_half, n + 1)
                pool.tensor_tensor(qkr[:, :, :], qkr[:, :, :], rope2[:, :, :], ALU.add).then_inc(rope_done, 1)

            def first_rest(n, u):
                pool.wait_ge(part1_done, n + 1)
                for first, slot in ((0, Q1), (H, K1)):
                    last = pool.tensor_tensor(rest[:, u, first:first + H, :], qkr[:, first:first + H, :],
                                              parts(u, first)[:, :, slot.start, :], ALU.subtract)
                last.then_inc(rest1_done, 1)
            rope(0, 0)
            first_rest(0, 0)
            rope(1, 1)
            with pool.Fori(1, T // 2) as half_n0:
                n0 = 2 * half_n0
                for u in range(2):
                    first_rest(n0 + u - 1, 1 - u)
                    rope(n0 + u, u)
            first_rest(T - 1, 1)

        @block.tensor
        def _(pe):
            def stack_transposes(n, u):
                pe.wait_ge(part3_done, n + 1)
                for i in range(4):
                    if i == 0:
                        wait(pe, stackT_v, n)
                    if i == 2:
                        wait(pe, stackT_a, n)
                    for h in range(8):
                        last = pe.transpose(ps_st[i][:, h, :], stack[:, u, 8 * i + h, :], id16)
                    last.then_inc(stackT_done, 1)

            def x_transposes(n, u):
                pe.wait_ge(xn_ready, n + 1)
                wait(pe, xT_copied, n)
                for c in range(DC):
                    last = pe.transpose(ps_T[:, c, :], xn[:, u, c * P:(c + 1) * P], id32)
                last.then_inc(xT_done, 1)

            def projections(n, u):
                pe.wait_ge(xT_copied, n + 1)
                wait(pe, v_copied, n)
                pe.wait_ge(ctx_in[u], (n // 2 + 1) * 16)
                for out, src, w in ((ps_qk[:, 0:D], xnT, wq), (ps_qk[:, D:2 * D], ctxT, wk), (ps_v[:, :], ctxT, wv)):
                    for c in range(DC):
                        last = pe.matmul(out, src[:, u, c, :], w[:, c, :], start=(c == 0), stop=(c == DC - 1))
                last.then_inc(proj_done, 1)

            pe.wait_ge(weights, 16 * 5)
            x_transposes(0, 0)
            x_transposes(1, 1)
            projections(0, 0)
            x_transposes(2, 0)
            projections(1, 1)
            with pe.Fori(1, (T - 2) // 2) as half_n0:
                n0 = 2 * half_n0
                for u in range(2):
                    stack_transposes(n0 + u - 2, u)
                    x_transposes(n0 + u + 1, 1 - u)
                    projections(n0 + u, u)
            stack_transposes(T - 4, 0)
            x_transposes(T - 1, 1)
            projections(T - 2, 0)
            stack_transposes(T - 3, 1)
            projections(T - 1, 1)
            stack_transposes(T - 2, 0)
            stack_transposes(T - 1, 1)


def phase_attend(nc, per, qs, ks, va):
    id16 = per["c16"][:, B_ID:B_ID + P]
    with ExitStack() as ctx:
        sb = lambda n, s, d: ctx.enter_context(nc.sbuf_tensor(n, s, d))
        ps = lambda n, s, d: ctx.enter_context(nc.psum_tensor(n, s, d))
        sem = lambda n: ctx.enter_context(nc.semaphore(n))
        prob = sb("prob", [P, 2, G, S], F32)
        vst = sb("vst", [P, 2, QT, G * HPAD], F32)
        mx = sb("mx", [P, 2, QT, G], F32)
        minus = sb("minus", [P, QT, G], F32)
        mrest = sb("mrest", [P, 2, QT, G], F32)
        mparts = sb("mparts", [P, 2, QT, XROWS], BF16)
        ps_f = [ps(f"ps_f{i}", [P, S], F32) for i in range(2)]
        ps_s = [ps(f"ps_s{i}", [P, 2, S], F32) for i in range(2)]
        ps_o = ps("ps_o", [P, S], F32)
        ps_m = ps("ps_m", [P, QT, P], BF16)
        scored, max_done = sem("scored"), sem("max_done")
        mpreset, split1, split_done = sem("mpreset"), sem("split1"), sem("split_done")
        mT_done, m_ready = sem("mT_done"), sem("m_ready")
        v_ready = sem("v_ready")
        s_done, exp_done, pv_done, o_copied = sem("s_done"), sem("exp_done"), sem("pv_done"), sem("o_copied")
        block = ctx.enter_context(nc.Block())
        o32 = qs[:, :, :].rearrange("p h s -> p (h s)").bitcast(F32).rearrange("p (s c) -> p s c", s=STEPS)

        @block.tensor
        def _(pe):
            def first_scores(f, idx):
                qt, j = divmod(idx, G)
                wait(pe, max_done, f * 16 + idx - 1)
                pe.matmul(ps_f[idx % 2][:, :], qs[:, ds(f * G + j, 1), qt * P:(qt + 1) * P],
                          ks[:, ds(f * G + j, 1), :], start=True, stop=True).then_inc(scored, 1)

            def scores(s, kt, half):
                wait(pe, exp_done, s * 8 + kt * 2 + half - 1)
                for j in (2 * half, 2 * half + 1):
                    last = pe.matmul(ps_s[half][:, j % 2, :], ks[:, ds(s * G + j, 1), kt * P:(kt + 1) * P],
                                     qs[:, ds(s * G + j, 1), :], start=True, stop=True)
                last.then_inc(s_done, 1)

            def values(s, u, kt):
                pe.wait_ge(exp_done, s * 8 + kt * 2 + 2)
                if kt == 0:
                    pe.wait_ge(v_ready, s + 1)
                    wait(pe, o_copied, s)
                for j in range(G):
                    last = pe.matmul(ps_o[HPAD * j:HPAD * (j + 1), :], vst[:, u, kt, HPAD * j:HPAD * (j + 1)],
                                     prob[:, kt % 2, j, :], start=(kt == 0), stop=(kt == QT - 1))
                last.then_inc(pv_done, 1)

            def maxima(s, u):
                pe.wait_ge(split_done, s + 1)
                wait(pe, m_ready, s)
                for qt in range(QT):
                    last = pe.transpose(ps_m[96:128, qt, :], mparts[:, u, qt, :], id16)
                last.then_inc(mT_done, 1)

            def step(s, u, before, ahead, next_):
                for kt in range(QT):
                    if ahead:
                        first_scores(s + 2, 4 * kt)
                    if kt == 0:
                        pe.wait_ge(m_ready, s + 1)
                    scores(s, kt, 0)
                    if ahead:
                        first_scores(s + 2, 4 * kt + 1)
                    scores(s, kt, 1)
                    if ahead:
                        first_scores(s + 2, 4 * kt + 2)
                        first_scores(s + 2, 4 * kt + 3)
                    if kt:
                        values(s, u, kt - 1)
                    elif before:
                        values(s - 1, 1 - u, QT - 1)
                    if kt == 2 and next_:
                        maxima(s + 1, 1 - u)

            for f in range(2):
                for idx in range(16):
                    first_scores(f, idx)
            maxima(0, 0)
            step(0, 0, False, True, True)
            step(1, 1, True, True, True)
            with pe.Fori(1, (STEPS - 2) // 2) as half_s0:
                s0 = 2 * half_s0
                for u in range(2):
                    step(s0 + u, u, True, True, True)
            step(STEPS - 2, 0, True, False, True)
            step(STEPS - 1, 1, True, False, False)
            values(STEPS - 1, 1, QT - 1)

        @block.vector
        def _(dve):
            def maxima(f, u):
                wait(dve, split_done, f - 1)
                for idx in range(16):
                    dve.wait_ge(scored, f * 16 + idx + 1)
                    dve.tensor_reduce(mx[:, u, idx // G, idx % G:idx % G + 1], ps_f[idx % 2][:, :], AX_X,
                                      ALU.max).then_inc(max_done, 1)
            maxima(0, 0)
            maxima(1, 1)
            with dve.Fori(1, STEPS // 2) as half_f0:
                f0 = 2 * half_f0
                for u in range(2):
                    maxima(f0 + u, u)

        @block.gpsimd
        def _(pool):
            pool.memset(vst[:, :, :, :], 0.0)
            pool.memset(minus[:, :, :], -1.0)
            pool.memset(mparts[:, :, :, :], 0.0).then_inc(mpreset, 1)
            pool.wait_ge(mpreset, 1)
            pool.memset(mparts[:, :, :, MASK_ROW:MASK_ROW + 1], 1.0).then_inc(mpreset, 1)
            pool.wait_ge(mpreset, 2)

            def split(s, u):
                out = mparts[:, u, :, 0:3 * G].rearrange("p q (j i) -> p q j i", i=3)
                pool.wait_ge(max_done, 16 * (s + 1))
                wait(pool, mT_done, s - 1)
                pool.tensor_tensor(out[:, :, :, 0], mx[:, u, :, :], minus[:, :, :], ALU.mult).then_inc(split1, 1)
                pool.wait_ge(split1, s * 4 + 1)
                pool.tensor_tensor(mrest[:, 0, :, :], mx[:, u, :, :], out[:, :, :, 0], ALU.add).then_inc(split1, 1)
                pool.wait_ge(split1, s * 4 + 2)
                pool.tensor_tensor(out[:, :, :, 1], mrest[:, 0, :, :], minus[:, :, :], ALU.mult).then_inc(split1, 1)
                pool.wait_ge(split1, s * 4 + 3)
                pool.tensor_tensor(mrest[:, 1, :, :], mrest[:, 0, :, :], out[:, :, :, 1], ALU.add).then_inc(split1, 1)
                pool.wait_ge(split1, s * 4 + 4)
                pool.tensor_tensor(out[:, :, :, 2], mrest[:, 1, :, :], minus[:, :, :], ALU.mult)\
                    .then_inc(split_done, 1)

            def stage_values(s, u):
                wait(pool, pv_done, QT * (s - 1))
                pool.tensor_copy(vst[:, u, :, :].rearrange("p k (j c) -> p (k j) c", c=HPAD)[:, :, 0:HD + 1],
                                 va[:, ds(s, 1), :].rearrange("p o (k d) -> p (o k) d", d=HD + 1)).then_inc(v_ready, 1)

            for s in range(2):
                split(s, s)
                stage_values(s, s)
            with pool.Fori(1, STEPS // 2) as half_s0:
                s0 = 2 * half_s0
                for u in range(2):
                    split(s0 + u, u)
                    stage_values(s0 + u, u)

        @block.scalar
        def _(act):
            def exps(s, kt):
                for half in range(2):
                    act.wait_ge(s_done, s * 8 + kt * 2 + half + 1)
                    if half == 0:
                        wait(act, pv_done, s * QT + kt - 1)
                    act.activation(prob[:, kt % 2, 2 * half:2 * half + 2, :], ps_s[half][:, :, :], ACT.Exp,
                                   scale=SCALE).then_inc(exp_done, 1)

            def spread_maxima(s):
                act.wait_ge(mT_done, s + 1)
                act.copy(qs[96:128, ds(s * G, G), :],
                         ps_m[96:128, :, :].rearrange("p q (o c) -> p o (q c)", o=1).broadcast_to([32, G, S]))\
                    .then_inc(m_ready, 1)

            def sums_out(s):
                act.wait_ge(pv_done, QT * (s + 1))
                act.copy(o32[:, ds(s, 1), 0:S], ps_o[:, :]).then_inc(o_copied, 1)

            def step(s, before, next_):
                for kt in range(QT):
                    exps(s, kt)
                    if kt == 0 and before:
                        sums_out(s - 1)
                    if kt == 3 and next_:
                        spread_maxima(s + 1)
            spread_maxima(0)
            step(0, False, True)
            with act.Fori(1, STEPS - 1) as s:
                step(s, True, True)
            step(STEPS - 1, True, False)
            sums_out(STEPS - 1)


def phase_project(nc, a, per, qs, loads):
    x_sb, st = per["x"], per["st"]
    id32 = per["c32"][:, C_ID:C_ID + P]
    o32 = qs[:, :, :].rearrange("p h s -> p (h s)").bitcast(F32).rearrange("p (s c) -> p s c", s=STEPS)
    with ExitStack() as ctx:
        sb = lambda n, s, d: ctx.enter_context(nc.sbuf_tensor(n, s, d))
        ps = lambda n, s, d: ctx.enter_context(nc.psum_tensor(n, s, d))
        sem = lambda n: ctx.enter_context(nc.semaphore(n))
        wp = sb("wp", [P, DC, D], F32)
        bp = sb("bp", [P, D], F32)
        stage = sb("stage", [P, 2, S], F32)
        recip = sb("recip", [P, NG, QT, G], F32)
        on = sb("on", [P, QT, D], F32)
        onT = sb("onT", [P, DC, S], F32)
        yb = sb("yb", [P, 2, D], F32)
        coef = sb("coef", [P, T], F32)
        ps_t = [ps(f"ps_t{i}", [P, QT, G, HPAD], F32) for i in range(2)]
        ps_o = [ps(f"ps_oT{i}", [P, DC, 2 * P], F32) for i in range(2)]
        ps_y = [ps(f"ps_y{i}", [P, 2, D], F32) for i in range(2)]
        wp_in, bp_in, staged, t_done, r_done, on_done = (sem("wp_in"), sem("bp_in"), sem("staged"), sem("t_done"),
                                                         sem("r_done"), sem("on_done"))
        oT_done, oT_ready, y_done, y_biased, y_used = (sem("oT_done"), sem("oT_ready"), sem("y_done"),
                                                       sem("y_biased"), sem("y_used"))
        coef_done, st_done = sem("coef_done"), sem("st_doneP")
        block = ctx.enter_context(nc.Block())

        @block.sync
        def _(sp):
            sp.dma_start(wp[:, :, :], a["wp"]).then_inc(wp_in, 16)
            sp.dma_start(bp[:, :], a["bp"].to_broadcast([P, D])).then_inc(bp_in, 16)
            for dst, src, arrived in loads:
                sp.dma_start(dst, src).then_inc(arrived, 16)

        @block.scalar
        def _(act):
            def stage_sums(s, u):
                wait(act, t_done, s - 1)
                act.copy(stage[:, u, :], o32[:, ds(s, 1), 0:S].rearrange("p o c -> p (o c)")).then_inc(staged, 1)

            def transposed(b):
                for i in range(2):
                    act.wait_ge(oT_done, b * 2 + i + 1)
                    last = act.copy(onT[:, :, i * 2 * P:(i + 1) * 2 * P], ps_o[i][:, :, :])
                last.then_inc(oT_ready, 1)
            for g in range(NG):
                stage_sums(g, g % 2)
            stage_sums(NG, 0)
            stage_sums(NG + 1, 1)
            transposed(0)
            with act.Fori(1, B - 1) as b:
                stage_sums(b * NG + 2, 0)
                stage_sums(b * NG + 3, 1)
                stage_sums(b * NG + 4, 0)
                stage_sums(b * NG + 5, 1)
                transposed(b)
            stage_sums(STEPS - 2, 0)
            stage_sums(STEPS - 1, 1)
            transposed(B - 1)

        @block.tensor
        def _(pe):
            def sums(b, g):
                s = b * NG + g
                pe.wait_ge(staged, s + 1)
                wait(pe, on_done, s - 1)
                for qt in range(QT):
                    last = pe.transpose(ps_t[g % 2][:, qt, :, :].rearrange("p j c -> p (j c)"),
                                        stage[:, g % 2, qt * P:(qt + 1) * P], id32)
                last.then_inc(t_done, 1)

            def transposes(b):
                pe.wait_ge(on_done, (b + 1) * NG)
                for qt in range(QT):
                    for c in range(DC):
                        last = pe.transpose(ps_o[qt // 2][:, c, (qt % 2) * P:(qt % 2 + 1) * P],
                                            on[:, qt, c * P:(c + 1) * P], id32)
                    if qt % 2:
                        last.then_inc(oT_done, 1)

            def project(b):
                pe.wait_ge(oT_ready, b + 1)
                for qt in range(QT):
                    wait(pe, y_used, b * 2 - 1 + qt // 2)
                    for c in range(DC):
                        last = pe.matmul(ps_y[qt // 2][:, qt % 2, :], onT[:, c, qt * P:(qt + 1) * P], wp[:, c, :],
                                         start=(c == 0), stop=(c == DC - 1))
                    if qt % 2:
                        last.then_inc(y_done, 1)
            pe.wait_ge(wp_in, 16)
            for g in range(NG):
                sums(0, g)
            transposes(0)
            for g in range(NG):
                sums(1, g)
            project(0)
            transposes(1)
            with pe.Fori(2, B) as b:
                for g in range(NG):
                    sums(b, g)
                project(b - 1)
                transposes(b)
            project(B - 1)

        @block.vector
        def _(dve):
            dve.tensor_scalar(coef[:, :], per["mask"][:, :], per["gates"][:, 0:1], None, ALU.mult)\
               .then_inc(coef_done, 1)

            def normalise(b, g):
                s = b * NG + g
                dve.wait_ge(t_done, s + 1)
                wait(dve, on_done, s - NG + 1)
                dve.reciprocal(recip[:, g, :, :], ps_t[g % 2][:, :, :, HD]).then_inc(r_done, 1)
                dve.wait_ge(r_done, s + 1)
                dve.tensor_tensor(on[:, :, g * G * HD:(g + 1) * G * HD].rearrange("p q (j d) -> p q j d", d=HD),
                                  ps_t[g % 2][:, :, :, 0:HD],
                                  recip[:, g, :, :].rearrange("p q (j o) -> p q j o", o=1)
                                  .broadcast_to([P, QT, G, HD]), ALU.mult).then_inc(on_done, 1)

            def residual(b):
                for h in range(2):
                    k = b * 2 + h
                    dve.wait_ge(y_done, k + 1)
                    for q in range(2):
                        last = dve.tensor_tensor(yb[:, q, :], ps_y[h][:, q, :], bp[:, :], ALU.add)
                    last.then_inc(y_biased, 1)
                    dve.wait_ge(y_biased, k + 1)
                    for q in range(2):
                        xs = x_sb[:, ds(b * QT + 2 * h + q, 1), :].rearrange("p o d -> p (o d)")
                        last = dve.scalar_tensor_tensor(out=xs, in0=yb[:, q, :],
                                                        scalar=coef[:, ds(b * QT + 2 * h + q, 1)],
                                                        in1=xs, op0=ALU.mult, op1=ALU.add)
                    last.then_inc(y_used, 1)
                    dve.wait_ge(y_used, k + 1)
                    for q in range(2):
                        last = dve.bn_stats(st[:, ds(b * QT + 2 * h + q, 1), :].rearrange("p o d -> p (o d)"),
                                            x_sb[:, ds(b * QT + 2 * h + q, 1), :].rearrange("p o d -> p (o d)"))
            for g in range(NG):
                normalise(0, g)
            dve.wait_ge(coef_done, 1)
            dve.wait_ge(bp_in, 16)
            with dve.Fori(1, B) as b:
                for g in range(NG):
                    normalise(b, g)
                residual(b - 1)
            residual(B - 1)


def phase_route(nc, a, per, xT_all, nselT, down, down_in):
    x_sb, c32, c16 = per["x"], per["c32"], per["c16"]
    id32 = c32[:, C_ID:C_ID + P]
    id16 = c16[:, B_ID:B_ID + P]
    tri = c32[:, C_TRI:C_TRI + E * E].rearrange("p (o e f) -> p o e f", o=1, f=E)
    with ExitStack() as ctx:
        sb = lambda n, s, d: ctx.enter_context(nc.sbuf_tensor(n, s, d))
        ps = lambda n, s, d: ctx.enter_context(nc.psum_tensor(n, s, d))
        sem = lambda n: ctx.enter_context(nc.semaphore(n))
        gw = sb("gw", [P, DC, E], F32)
        lb = sb("lb", [P, E], F32)
        xn = sb("xnB", [P, 2, D], F32)
        xt = sb("xtB", [P, 2, DC, P], F32)
        logits = sb("logits", [P, T, E], F32)
        score = sb("score", [P, T, E], F32)
        beats = sb("beats", [P, T, E, E], F32)
        ties = sb("ties", [P, T, E, E], F32)
        rank = sb("rank", [P, T, E], F32)
        total = sb("total", [P, 2, T], F32)
        both = sb("both", [P, 2, E, T], F32)
        sums = sb("sums", [P, 2, E], F32)
        ones = sb("ones", [P, P], F32)
        most = sb("most", [P, 3, E], F32)
        nsel = sb("nsel", [P, T, P], BF16)
        mean, rstd, rstd_ready, ln_vector, ln_pool = row_statistics(nc, sb, sem, per, "B")
        ps_T = [ps(f"ps_TB{i}", [P, DC, P], F32) for i in range(2)]
        ps_lg = ps("ps_lg", [P, T, E], F32)
        ps_sum = ps("ps_sum", [P, 2 * E], F32)
        ps_n = [ps(f"ps_n{i}", [P, 8, P], BF16) for i in range(2)]
        small_in = sem("small_in")
        xn_ready, xT_done, xt_ready, lg_done = sem("xn_readyB"), sem("xT_doneB"), sem("xt_readyB"), sem("lg_done")
        kept = sem("kept")
        lg_copied, score_done, step_done = sem("lg_copied"), sem("score_done"), sem("step_done")
        sums_ready, sums_done, nsel_ready, nT_done = sem("sums_ready"), sem("sums_done"), sem("nsel_ready"), sem("nT_done")
        consts = sem("constsB")
        block = ctx.enter_context(nc.Block())

        @block.sync
        def _(sp):
            sp.dma_start(gw[:, :, :], a["gate_w"]).then_inc(small_in, 16)
            sp.dma_start(lb[:, :], a["lb"].to_broadcast([P, E])).then_inc(small_in, 16)

        @block.vector
        def _(dve):
            ln_vector(dve)
            dve.wait_ge(rstd_ready, 2)

            def normalise(n, u):
                wait(dve, xT_done, n - 1)
                dve.tensor_scalar(xn[:, u, :], x_sb[:, ds(n, 1), :], mean[:, ds(n, 1)], rstd[:, ds(n, 1)],
                                  ALU.subtract, ALU.mult).then_inc(xn_ready, 1)

            def transposed(n, u):
                dve.wait_ge(xT_done, n + 1)
                wait(dve, lg_done, n - 1)
                wait(dve, kept, n - 1)
                dve.tensor_copy(xt[:, u, :, :], ps_T[u][:, :, :]).then_inc(xt_ready, 1)
            normalise(0, 0)
            normalise(1, 1)
            transposed(0, 0)
            transposed(1, 1)
            with dve.Fori(1, T // 2) as half_n0:
                n0 = 2 * half_n0
                for u in range(2):
                    normalise(n0 + u, u)
                for u in range(2):
                    transposed(n0 + u, u)

            count = [0]

            def link(ins):
                count[0] += 1
                ins.then_inc(step_done, 1)
                dve.wait_ge(step_done, count[0])
            dve.wait_ge(lg_done, T)
            dve.wait_ge(small_in, 32)
            dve.tensor_tensor(logits[:, :, :], ps_lg[:, :, :],
                              lb[:, :].rearrange("p (o e) -> p o e", o=1).broadcast_to([P, T, E]), ALU.add)\
               .then_inc(lg_copied, 1)
            dve.wait_ge(score_done, 1)
            other = score[:, :, :].rearrange("p t (o f) -> p t o f", o=1).broadcast_to([P, T, E, E])
            own = score[:, :, :].rearrange("p t (e o) -> p t e o", o=1).broadcast_to([P, T, E, E])
            dve.tensor_tensor(beats[:, :, :, :], other, own, ALU.is_gt)
            link(dve.tensor_tensor(ties[:, :, :, :], other, own, ALU.is_equal))
            link(dve.tensor_tensor(ties[:, :, :, :], ties[:, :, :, :], tri.broadcast_to([P, T, E, E]), ALU.mult))
            link(dve.tensor_tensor(beats[:, :, :, :], beats[:, :, :, :], ties[:, :, :, :], ALU.add))
            link(dve.tensor_reduce(rank[:, :, :], beats[:, :, :, :], AX_X, ALU.add))
            chosen = both[:, 1, :, :].rearrange("p e t -> p t e")
            weight = both[:, 0, :, :].rearrange("p e t -> p t e")
            link(dve.tensor_scalar(chosen, rank[:, :, :], 1.5, None, ALU.is_lt))
            dve.tensor_scalar(nsel[:, :, 0:E], rank[:, :, :], 1.5, None, ALU.is_gt).then_inc(nsel_ready, 1)
            link(dve.tensor_tensor(weight, score[:, :, :], chosen, ALU.mult))
            link(dve.tensor_reduce(total[:, 0, :], weight, AX_X, ALU.add))
            link(dve.tensor_scalar(total[:, 1, :], total[:, 0, :], 1e-8, None, ALU.add))
            link(dve.reciprocal(total[:, 0, :], total[:, 1, :]))
            link(dve.tensor_tensor(both[:, 0, :, :], both[:, 0, :, :],
                                   total[:, 0, :].rearrange("p (o t) -> p o t", o=1).broadcast_to([P, E, T]),
                                   ALU.mult))
            dve.tensor_reduce(sums[:, :, :], both[:, :, :, :], AX_X, ALU.add).then_inc(sums_ready, 1)
            for i in range(2):
                dve.wait_ge(nT_done, i + 1)
                dve.tensor_copy(nselT[:, i * 8 * P:(i + 1) * 8 * P].rearrange("p (t c) -> p t c", c=P), ps_n[i][:, :, :])
            dve.wait_ge(sums_done, 1)
            link(dve.tensor_scalar(most[:, 0, :], ps_sum[:, E:2 * E], 1.0, None, ALU.max))
            link(dve.reciprocal(most[:, 1, :], most[:, 0, :]))
            link(dve.tensor_tensor(most[:, 2, :], ps_sum[:, 0:E], most[:, 1, :], ALU.mult))
            dve.wait_ge(down_in, 16 * (NX + 1))
            for e in range(E):
                dve.tensor_scalar(down[:, e, :], down[:, e, :], most[:, 2, e:e + 1], None, ALU.mult)

        @block.scalar
        def _(act):
            act.wait_ge(lg_copied, 1)
            act.activation(score[:, :, :], logits[:, :, :], ACT.Sigmoid).then_inc(score_done, 1)

        @block.gpsimd
        def _(pool):
            pool.memset(ones[:, :], 1.0).then_inc(consts, 1)
            pool.memset(nsel[:, :, E:P], 0.0).then_inc(consts, 1)
            ln_pool(pool)
            with pool.Fori(0, T // 2) as half_n0:
                n0 = 2 * half_n0
                for u in range(2):
                    n = n0 + u
                    pool.wait_ge(xt_ready, n + 1)
                    pool.tensor_copy(xT_all[:, :, ds(n * P, P)], xt[:, u, :, :]).then_inc(kept, 1)

        @block.tensor
        def _(pe):
            def transposes(n, u):
                pe.wait_ge(xn_ready, n + 1)
                for c in range(DC):
                    last = pe.transpose(ps_T[u][:, c, :], xn[:, u, c * P:(c + 1) * P], id32)
                last.then_inc(xT_done, 1)

            def scores(n, u):
                pe.wait_ge(xt_ready, n + 1)
                for c in range(DC):
                    last = pe.matmul(ps_lg[:, ds(n, 1), :], xt[:, u, c, :], gw[:, c, :],
                                     start=(c == 0), stop=(c == DC - 1))
                last.then_inc(lg_done, 1)
            pe.wait_ge(small_in, 32)
            with pe.Fori(0, T // 2) as half_n0:
                n0 = 2 * half_n0
                for u in range(2):
                    transposes(n0 + u, u)
                for u in range(2):
                    scores(n0 + u, u)
            pe.wait_ge(nsel_ready, 1)
            pe.wait_ge(consts, 2)
            for i in range(2):
                for k in range(8):
                    last = pe.transpose(ps_n[i][:, k, :], nsel[:, 8 * i + k, :], id16)
                last.then_inc(nT_done, 1)
            pe.wait_ge(sums_ready, 1)
            pe.wait_ge(consts, 1)
            pe.matmul(ps_sum[:, :], ones[:, :], sums[:, :, :].rearrange("p a e -> p (a e)"), start=True, stop=True)\
              .then_inc(sums_done, 1)


def phase_experts(nc, a, per, xT_all, nselT, up, down, w32, wjunk, wabs, up_in, w32_in):
    x_sb = per["x"]
    with ExitStack() as ctx:
        sb = lambda n, s, d: ctx.enter_context(nc.sbuf_tensor(n, s, d))
        ps = lambda n, s, d: ctx.enter_context(nc.psum_tensor(n, s, d))
        sem = lambda n: ctx.enter_context(nc.semaphore(n))
        skip = sb("skip", [P, E, P], BF16)
        sg = sb("sg", [P, 2, S], F32)
        h = sb("h", [P, 2, S], F32)
        ps_g = [ps(f"ps_g{i}", [P, S], F32) for i in range(2)]
        ps_u = [ps(f"ps_u{i}", [P, S], F32) for i in range(2)]
        ps_y = [ps(f"ps_yE{i}", [P, 2, D], F32) for i in range(2)]
        skip_in, gu_done, silu_done = sem("skip_in"), sem("gu_done"), sem("silu_done")
        h_ready, h_used, y_used, abs_done = sem("h_ready"), sem("h_used"), sem("y_usedE"), sem("abs_done")
        block = ctx.enter_context(nc.Block())

        @block.sync
        def _(sp):
            sp.dma_start(skip[:, :, :].bitcast(U16), a["skip"]).then_inc(skip_in, 16)

        @block.tensor
        def _(pe):
            def gate_up(c, e, first):
                k, u = c * NX + e, e % 2
                if first:
                    pe.wait_ge(up_in, 16 * (NX + 1))
                    pe.wait_ge(skip_in, 16)
                cols = ds(c * S, S)
                for i, out in ((0, ps_g[u]), (1, ps_u[u])):
                    masked = i == 0 and e < E
                    for d in range(DC):
                        last = pe.matmul(out[:, :], up[:, e, i, d, :], xT_all[:, d, cols], start=(d == 0),
                                         stop=(d == DC - 1 and not masked))
                    if masked:
                        pe.matmul(out[:, :], skip[:, e, :], nselT[:, cols], start=False, stop=True)
                last.then_inc(gu_done, 1)

            def project(c, e):
                k, u = c * NX + e, e % 2
                pe.wait_ge(h_ready, k + 1)
                for q in range(QT):
                    last = pe.matmul(ps_y[q // 2][:, q % 2, :], h[:, u, q * P:(q + 1) * P], down[:, e, :],
                                     start=(e == 0 and q % 2 == 0), stop=(e == NX - 1), skip_group_check=True)
                last.then_inc(h_used, 1)

            def chunk(c, edge):
                for e in range(1, NX):
                    gate_up(c, e, False)
                    project(c, e - 1)
                if not edge:
                    gate_up(c + 1, 0, False)
                project(c, NX - 1)
            gate_up(0, 0, True)
            with pe.Fori(0, B - 1) as c:
                chunk(c, False)
            chunk(B - 1, True)

        @block.scalar
        def _(act):
            def silu(c, e):
                k, u = c * NX + e, e % 2
                act.wait_ge(gu_done, k + 1)
                act.activation(sg[:, u, :], ps_g[u][:, :], ACT.Silu).then_inc(silu_done, 1)
            with act.Fori(0, B - 1) as c:
                for e in range(NX):
                    silu(c, e)
            act.wait_ge(w32_in, 16 * 3)
            for e in range(NX):
                silu(B - 1, e)
                if 1 <= e <= 3:
                    wait(act, abs_done, e - 1)
                    act.activation(wjunk[:, :], w32[:, e - 1, :], ACT.Abs, accum_out=wabs[:, e - 1:e])\
                       .then_inc(abs_done, 1)

        @block.vector
        def _(dve):
            def residual(c):
                dve.wait_ge(h_used, (c + 1) * NX)
                for i in range(2):
                    xs = x_sb[:, ds(c * QT + 2 * i, 2), :]
                    dve.scalar_tensor_tensor(out=xs, in0=ps_y[i][:, :, :], scalar=per["gates"][:, 2:3], in1=xs,
                                             op0=ALU.mult, op1=ALU.add).then_inc(y_used, 1)
                dve.wait_ge(y_used, 2 * c + 2)
                for i in range(QT):
                    dve.bn_stats(per["st"][:, ds(c * QT + i, 1), :].rearrange("p o d -> p (o d)"),
                                 x_sb[:, ds(c * QT + i, 1), :].rearrange("p o d -> p (o d)"))

            def hidden(c, e, edge):
                k, u = c * NX + e, e % 2
                dve.wait_ge(silu_done, k + 1)
                if not edge:
                    dve.wait_ge(h_used, k - 1)
                dve.tensor_tensor(h[:, u, :], sg[:, u, :], ps_u[u][:, :], ALU.mult).then_inc(h_ready, 1)
            for e in range(NX):
                hidden(0, e, e < 2)
            with dve.Fori(1, B) as c:
                residual(c - 1)
                for e in range(NX):
                    hidden(c, e, False)
            residual(B - 1)


def phase_coattend(nc, a, per, ffn, free, ctok, ctxT, wqv, w32, wabs, wq16, wstat, ctx_in):
    x_sb, c32 = per["x"], per["c32"]
    id32 = c32[:, C_ID:C_ID + P]
    with ExitStack() as ctx:
        sb = lambda n, s, d: ctx.enter_context(nc.sbuf_tensor(n, s, d))
        ps = lambda n, s, d: ctx.enter_context(nc.psum_tensor(n, s, d))
        sem = lambda n: ctx.enter_context(nc.semaphore(n))
        wsim = sb("wsim", [P, 2, DC], F32)
        w1 = sb("w1", [P, D], F32)
        bsim = sb("bsim", [P, 1], F32)
        bqv = sb("bqv", [P, D], F32)
        e, eT, sT, junk, att, attT = carve(free, [(2, QT, D), (2, DC, S), (DC, S), (QT, D), (QT, S), (2, QT, P)])
        hqT = sb("hqT", [P, 2, DC, S], F32)
        ehT = sb("ehT", [P, 2, DC, S], F32)
        hq = sb("hq", [P, 2, D], F32)
        wx = sb("wx", [P, DC, D], F32)
        yb = sb("ybC", [P, 2, D], F32)
        nmax = sb("nmax", [P, QT], F32)
        lsum = sb("lsum", [P, QT], F32)
        lrec = sb("lrec", [P, QT], F32)
        own = sb("own", [P, QT], F32)
        z = sb("z", [P, 3, QT], F32)
        nz = sb("nz", [P, 1], F32)
        ez = sb("ez", [P, QT], F32)
        ezs = sb("ezs", [P, 1], F32)
        rz = sb("rz", [P, 1], F32)
        hc = sb("hc", [P, DC], F32)
        ones = sb("onesC", [P, P], F32)
        mean, rstd, rstd_ready, ln_vector, ln_pool = row_statistics(nc, sb, sem, per, "C")
        ps_T = [ps(f"ps_TC{i}", [P, DC, 2 * P], F32) for i in range(2)]
        ps_S = [ps(f"ps_SC{i}", [P, S], F32) for i in range(2)]
        ps_A = ps("ps_A", [P, QT, P], F32)
        ps_q = ps("ps_q", [P, D], F32)
        ps_qT = ps("ps_qT", [P, DC, P], F32)
        ps_h = ps("ps_h", [P, 8], F32)
        w_in = sem("w_inC")
        e_ready, eT_done, eT_ready, sT_ready = sem("e_readyC"), sem("eT_done"), sem("eT_ready"), sem("sT_ready")
        S_done, max_ready, exp_done = sem("S_doneC"), sem("max_readyC"), sem("exp_doneC")
        own_done, z_half, z_ready, zmax_ready, nz_ready = (sem("own_done"), sem("z_half"), sem("z_ready"),
                                                           sem("zmax_ready"), sem("nz_ready"))
        ez_ready, hc_done, hc_step, wx_ready = sem("ez_ready"), sem("hc_done"), sem("hc_step"), sem("wx_ready")
        attT_done, attT_ready, q_done, q_ready = sem("attT_done"), sem("attT_ready"), sem("q_done"), sem("q_ready")
        l_ready = sem("l_ready")
        qT_done, qT_ready, eh_ready = sem("qT_done"), sem("qT_ready"), sem("eh_ready")
        out_done, biased, out_used = sem("out_doneC"), sem("biasedC"), sem("out_usedC")
        ones_ready, wsum_done, wstat_step, quant = sem("ones_ready"), sem("wsum_done"), sem("wstat_step"), sem("quant")
        block = ctx.enter_context(nc.Block())

        @block.sync
        def _(sp):
            sp.dma_start(wsim[:, :, :], a["wsim"]).then_inc(w_in, 16)
            sp.dma_start(w1[:, :], a["w1"].to_broadcast([P, D])).then_inc(w_in, 16)
            sp.dma_start(bsim[:, :], a["bsim"].to_broadcast([P, 1])).then_inc(w_in, 16)
            sp.dma_start(bqv[:, :], a["bqv"].to_broadcast([P, D])).then_inc(w_in, 16)

        def schedule(eng, batch):
            batch(0, 0, False, False)
            with eng.Fori(0, (B - 2) // 2) as pair:
                for v in range(2):
                    batch(2 * pair + v + 1, (v + 1) % 2, True, False)
            batch(B - 1, (B - 1) % 2, True, True)

        @block.tensor
        def _(pe):
            def transposes(b, v):
                for i in range(2):
                    pe.wait_ge(e_ready, b * QT + 2 * i + 2)
                    for q in range(2):
                        for c in range(DC):
                            last = pe.transpose(ps_T[i][:, c, q * P:(q + 1) * P],
                                                e[:, v, 2 * i + q, c * P:(c + 1) * P], id32)
                    last.then_inc(eT_done, 1)

            def similarity(b, q):
                n = b * QT + q
                if q == 0:
                    pe.wait_ge(sT_ready, b + 1)
                if q > 1:
                    pe.wait_ge(exp_done, n - 1)
                for c in range(DC):
                    last = pe.matmul(ps_S[q % 2][:, :], sT[:, c, q * P:(q + 1) * P], ctxT[:, c, ds(b * S, S)],
                                     start=(c == 0), stop=(c == DC - 1))
                last.then_inc(S_done, 1)

            def attended(b, q):
                n = b * QT + q
                pe.wait_ge(exp_done, n + 1)
                if q:
                    pe.wait_ge(attT_ready, n)
                for k in range(QT):
                    last = pe.transpose(ps_A[:, k, :], att[:, q, k * P:(k + 1) * P], id32)
                last.then_inc(attT_done, 1)

            def context(b, q):
                n = b * QT + q
                pe.wait_ge(attT_ready, n + 1)
                wait(pe, q_ready, n)
                for k in range(QT):
                    last = pe.matmul(ps_q[:, :], attT[:, q % 2, k, :], ctok[:, ds(b * QT + k, 1), :],
                                     start=(k == 0), stop=(k == QT - 1))
                last.then_inc(q_done, 1)

            def context_transposes(b, q):
                n = b * QT + q
                pe.wait_ge(q_ready, n + 1)
                wait(pe, qT_ready, n)
                for c in range(DC):
                    last = pe.transpose(ps_qT[:, c, :], hq[:, q % 2, c * P:(c + 1) * P], id32)
                last.then_inc(qT_done, 1)

            def pooled(b, v):
                pe.wait_ge(ez_ready, b + 1)
                pe.matmul(ps_h[:, 2:3], ones[:, :], ezs[:, :], start=True, stop=True)
                for c in range(DC):
                    for q in range(QT):
                        last = pe.matmul(ps_h[:, c:c + 1], e[:, v, q, c * P:(c + 1) * P], ez[:, q:q + 1],
                                         start=(q == 0), stop=(q == QT - 1))
                last.then_inc(hc_done, 1)

            def features(b, v, q):
                n = b * QT + q
                if q == 0:
                    pe.wait_ge(wx_ready, b + 1)
                pe.wait_ge(eh_ready, n + 1)
                wait(pe, out_used, n - 1)
                cols = slice(q * P, (q + 1) * P)
                terms = [(eT[:, v, c, cols], wx[:, c, :]) for c in range(DC)]
                terms += [(hqT[:, v, c, cols], wqv[:, 1, c, :]) for c in range(DC)]
                terms += [(ehT[:, v, c, cols], wqv[:, 2, c, :]) for c in range(DC)]
                for i, (l, r) in enumerate(terms):
                    last = pe.matmul(ps_T[q % 2][:, 0, :], l, r, start=(i == 0), stop=(i == len(terms) - 1))
                last.then_inc(out_done, 1)

            def batch(b, v, before, last):
                feature = lambda q: features(b - 1, 1 - v, q) if before else None
                transposes(b, v)
                if before:
                    pe.wait_ge(eT_ready, 2 * b + 1)
                feature(0)
                for q in range(QT):
                    similarity(b, q)
                attended(b, 0)
                feature(1)
                attended(b, 1)
                context(b, 0)
                attended(b, 2)
                context(b, 1)
                context_transposes(b, 0)
                attended(b, 3)
                context(b, 2)
                context_transposes(b, 1)
                feature(2)
                context(b, 3)
                context_transposes(b, 2)
                feature(3)
                pooled(b, v)
                context_transposes(b, 3)

            pe.wait_ge(w_in, 16 * 4)
            pe.wait_ge(ctx_in, 16 * 3)
            pe.wait_ge(ones_ready, 1)
            pe.matmul(ps_h[:, 4:7], ones[:, :], wabs[:, :], start=True, stop=True).then_inc(wsum_done, 1)
            pe.wait_ge(wstat_step, 1)
            schedule(pe, batch)
            for q in range(QT):
                features(B - 1, (B - 1) % 2, q)

        @block.vector
        def _(dve):
            def normalise(b, v):
                for q in range(QT):
                    n = b * QT + q
                    dve.tensor_scalar(e[:, v, q, :], x_sb[:, ds(n, 1), :].rearrange("p o d -> p (o d)"),
                                      mean[:, ds(n, 1)], rstd[:, ds(n, 1)], ALU.subtract, ALU.mult)\
                       .then_inc(e_ready, 1)

            def transposed(b, v):
                for i in range(2):
                    dve.wait_ge(eT_done, b * 2 + i + 1)
                    dve.tensor_copy(eT[:, v, :, i * 2 * P:(i + 1) * 2 * P], ps_T[i][:, :, :]).then_inc(eT_ready, 1)
                dve.wait_ge(eT_ready, 2 * b + 2)
                for c in range(DC):
                    last = dve.tensor_scalar(sT[:, c, :], eT[:, v, c, :], wsim[:, 1, c:c + 1],
                                             wsim[:, 0, c:c + 1], ALU.mult, ALU.add)
                last.then_inc(sT_ready, 1)

            def maximum(b, q):
                dve.wait_ge(S_done, b * QT + q + 1)
                dve.tensor_reduce(nmax[:, q:q + 1], ps_S[q % 2][:, :], AX_X, ALU.max, negate=True)\
                   .then_inc(max_ready, 1)

            def own_part(b, v):
                for q in range(QT):
                    last = dve.tensor_tensor_reduce(out=junk[:, q, :], in0=e[:, v, q, :], in1=w1[:, :], scale=1.0,
                                                    scalar=0.0, op0=ALU.mult, op1=ALU.add,
                                                    accum_out=own[:, q:q + 1])
                last.then_inc(own_done, 1)

            def sim_maxima(b):
                dve.wait_ge(max_ready, (b + 1) * QT)
                dve.wait_ge(own_done, b + 1)
                dve.tensor_tensor(z[:, 0, :], own[:, :], nmax[:, :], ALU.subtract).then_inc(z_half, 1)
                dve.wait_ge(z_half, b + 1)
                dve.tensor_scalar(z[:, 1, :], z[:, 0, :], bsim[:, 0:1], None, ALU.add).then_inc(z_ready, 1)

            def sum_inverses(b):
                dve.wait_ge(exp_done, (b + 1) * QT)
                dve.reciprocal(lrec[:, :], lsum[:, :]).then_inc(l_ready, 1)
                dve.wait_ge(l_ready, b + 1)

            def batch_maximum(b):
                dve.wait_ge(zmax_ready, b + 1)
                dve.tensor_reduce(nz[:, :], z[:, 2, :], AX_X, ALU.max, negate=True).then_inc(nz_ready, 1)

            def context(b, q):
                dve.wait_ge(q_done, b * QT + q + 1)
                dve.tensor_scalar(hq[:, q % 2, :], ps_q[:, :], lrec[:, q:q + 1], None, ALU.mult).then_inc(q_ready, 1)

            def context_transposed(b, v, q):
                dve.wait_ge(qT_done, b * QT + q + 1)
                dve.tensor_copy(hqT[:, v, :, q * P:(q + 1) * P], ps_qT[:, :, :]).then_inc(qT_ready, 1)

            def pooled_weights(b):
                dve.wait_ge(hc_done, b + 1)
                dve.reciprocal(rz[:, :], ps_h[:, 2:3]).then_inc(hc_step, 1)
                dve.wait_ge(hc_step, b * 2 + 1)
                dve.tensor_scalar(hc[:, :], ps_h[:, 0:2], rz[:, 0:1], None, ALU.mult).then_inc(hc_step, 1)
                dve.wait_ge(hc_step, b * 2 + 2)
                for c in range(DC):
                    last = dve.scalar_tensor_tensor(out=wx[:, c, :], in0=wqv[:, 3, c, :], scalar=hc[:, c:c + 1],
                                                    in1=wqv[:, 0, c, :], op0=ALU.mult, op1=ALU.add)
                last.then_inc(wx_ready, 1)

            def residual(b, q):
                n = b * QT + q
                dve.wait_ge(out_done, n + 1)
                dve.tensor_tensor(yb[:, q % 2, :], ps_T[q % 2][:, 0, :], bqv[:, :], ALU.add).then_inc(biased, 1)
                dve.wait_ge(biased, n + 1)
                xs = x_sb[:, ds(n, 1), :].rearrange("p o d -> p (o d)")
                dve.scalar_tensor_tensor(out=xs, in0=yb[:, q % 2, :], scalar=per["gates"][:, 1:2], in1=xs,
                                         op0=ALU.mult, op1=ALU.add).then_inc(out_used, 1)
                dve.wait_ge(out_used, n + 1)
                dve.bn_stats(per["st"][:, ds(n, 1), :].rearrange("p o d -> p (o d)"), xs)\
                   .then_inc(ffn["stats_done"], 1)

            def batch(b, v, before, last):
                updated = lambda q: residual(b - 1, q) if before else None
                transposed(b, v)
                own_part(b, v)
                maximum(b, 0)
                updated(0)
                for q in range(1, QT):
                    maximum(b, q)
                sim_maxima(b)
                sum_inverses(b)
                updated(1)
                context(b, 0)
                context(b, 1)
                batch_maximum(b)
                context_transposed(b, v, 0)
                context(b, 2)
                context_transposed(b, v, 1)
                updated(2)
                context(b, 3)
                context_transposed(b, v, 2)
                updated(3)
                if not last:
                    normalise(b + 1, 1 - v)
                pooled_weights(b)
                context_transposed(b, v, 3)
            ln_vector(dve)
            dve.wait_ge(rstd_ready, 2)
            normalise(0, 0)
            dve.wait_ge(w_in, 16 * 4)
            dve.wait_ge(ctx_in, 16 * 3)
            dve.wait_ge(wsum_done, 1)
            dve.tensor_scalar(wstat[:, 0:3], ps_h[:, 4:7], 1.0 / (D * INNER), 1e-5, ALU.mult, ALU.max)\
               .then_inc(wstat_step, 1)
            dve.wait_ge(wstat_step, 1)
            dve.reciprocal(wstat[:, 3:6], wstat[:, 0:3]).then_inc(wstat_step, 1)
            schedule(dve, batch)
            for q in range(QT):
                residual(B - 1, q)

        @block.scalar
        def _(act):
            with act.Fori(0, B) as b:
                for q in range(QT):
                    n = b * QT + q
                    act.wait_ge(max_ready, n + 1)
                    act.activation(att[:, q, :], ps_S[q % 2][:, :], ACT.Exp, bias=nmax[:, q:q + 1],
                                   accum_out=lsum[:, q:q + 1]).then_inc(exp_done, 1)
                for q in range(QT):
                    n = b * QT + q
                    act.wait_ge(attT_done, n + 1)
                    if q > 1:
                        act.wait_ge(q_done, n - 1)
                    act.copy(attT[:, q % 2, :, :], ps_A[:, :, :]).then_inc(attT_ready, 1)
                act.wait_ge(nz_ready, b + 1)
                act.activation(ez[:, :], z[:, 1, :], ACT.Exp, bias=nz[:, 0:1], accum_out=ezs[:, 0:1])\
                   .then_inc(ez_ready, 1)

        @block.gpsimd
        def _(pool):
            pool.memset(ones[:, :], 1.0).then_inc(ones_ready, 1)
            ln_pool(pool)

            def quantise_weights(i):
                pool.tensor_scalar(w32[:, i, :], w32[:, i, :], wstat[:, 3 + i:4 + i], MAGIC, ALU.mult, ALU.add)\
                    .then_inc(quant, 1)
                pool.wait_ge(quant, 3 * i + 1)
                pool.tensor_scalar(w32[:, i, :], w32[:, i, :], MAGIC + 1.0, MAGIC - 1.0, ALU.min, ALU.max)\
                    .then_inc(quant, 1)
                pool.wait_ge(quant, 3 * i + 2)
                pool.tensor_scalar(wq16[:, i, :], w32[:, i, :], 1.0, -MAGIC, ALU.mult, ALU.add).then_inc(quant, 1)
            for b in range(B):
                pool.wait_ge(z_ready, b + 1)
                pool.partition_all_reduce(z[:, 2, :], z[:, 1, :], P, bass.bass_isa.ReduceOp.max)\
                    .then_inc(zmax_ready, 1)
                for q in range(QT):
                    pool.wait_ge(qT_ready, b * QT + q + 1)
                    cols = slice(q * P, (q + 1) * P)
                    pool.tensor_tensor(ehT[:, b % 2, :, cols], eT[:, b % 2, :, cols], hqT[:, b % 2, :, cols],
                                       ALU.mult).then_inc(eh_ready, 1)
                if b:
                    normalise_batch(pool, per, ffn, b - 1)
                if b == 0:
                    pool.wait_ge(wstat_step, 2)
                if b < 3:
                    quantise_weights(b)


def phase_bitffn(nc, per, ffn, free, wq16, wstat, out):
    x_sb, c16, xn = per["x"], per["c16"], ffn["xn"]
    id16 = c16[:, B_ID:B_ID + P]
    wg, wu = (wq16[:, i, :].rearrange("p (c n) -> p c n", c=DC) for i in range(2))
    wd = wq16[:, 2, :].rearrange("p (c n) -> p c n", c=IC)
    with ExitStack() as ctx:
        sb = lambda n, s, d: ctx.enter_context(nc.sbuf_tensor(n, s, d))
        ps = lambda n, s, d: ctx.enter_context(nc.psum_tensor(n, s, d))
        sem = lambda n: ctx.enter_context(nc.semaphore(n))
        sg, t, r = carve(free, [(2, INNER), (2, INNER), (2, INNER)])
        amax = sb("amax", [P, 6, T], F32)
        gd = sb("gd", [P, 2], F32)
        xr = sb("xr", [P, 2, D], F32)
        xq = sb("xq", [P, 2, D], BF16)
        xqT = sb("xqT", [P, 2, DC, P], BF16)
        hq = sb("hqD", [P, 2, INNER], BF16)
        hqT = sb("hqTD", [P, 2, IC, P], BF16)
        hs = sb("hs", [P, 2, 4], F32)
        ys = sb("ys", [P, T], F32)
        ps_x = ps("ps_x", [P, DC, P], BF16)
        ps_g = ps("ps_gD", [P, INNER], F32)
        ps_u = ps("ps_uD", [P, INNER], F32)
        ps_h = ps("ps_hD", [P, IC, P], BF16)
        ps_y = [ps(f"ps_yD{i}", [P, D], F32) for i in range(2)]
        scale_step, scales_ready = sem("scale_step"), sem("scales_ready")
        xr_done, xq_ready, xT_done, xT_ready = sem("xr_done"), sem("xq_readyD"), sem("xT_doneD"), sem("xT_readyD")
        gate_done, up_done, silu_done, t_ready = sem("gate_done"), sem("up_done"), sem("silu_doneD"), sem("t_ready")
        hstep, f_ready, r_ready, hq_ready = sem("hstep"), sem("f_ready"), sem("r_ready"), sem("hq_readyD")
        hT_done, hT_ready, y_done, y_used, stored = (sem("hT_done"), sem("hT_readyD"), sem("y_doneD"), sem("y_usedD"),
                                                     sem("stored"))
        block = ctx.enter_context(nc.Block())
        ABS, AMAX, INV, SX, AG, AU = range(6)

        def live(k):
            return not isinstance(k, int) or 0 <= k < T

        def schedule(eng, step):
            for n in range(4):
                step(n, n % 2)
            with eng.Fori(2, (T - 2) // 2) as half_n0:
                for u in range(2):
                    step(2 * half_n0 + u, u)
            for n in range(T - 2, T + 3):
                step(n, n % 2)

        @block.sync
        def _(sp):
            ov = out.rearrange("b (q p) d -> p (b q) d", p=P)
            with sp.Fori(0, T) as n:
                sp.wait_ge(y_used, n + 1)
                sp.dma_start(ov[:, ds(n, 1), :], x_sb[:, ds(n, 1), :]).then_inc(stored, 16)
            sp.wait_ge(stored, 16 * T)

        @block.gpsimd
        def _(pool):
            def quantise(n, u):
                if n % QT == 0:
                    pool.wait_ge(scales_ready, n // QT + 1)
                pool.tensor_scalar(xr[:, u, :], xn[:, n, :], amax[:, SX, n:n + 1], MAGIC, ALU.mult, ALU.add)\
                    .then_inc(xr_done, 1)
                pool.wait_ge(xr_done, n + 1)
                wait(pool, xT_done, n - 1)
                pool.tensor_scalar(xq[:, u, :], xr[:, u, :], 1.0, -MAGIC, ALU.mult, ALU.add).then_inc(xq_ready, 1)

            def rounded(n, u):
                pool.wait_ge(r_ready, n + 1)
                wait(pool, hT_done, n - 1)
                pool.tensor_scalar(hq[:, u, :], r[:, u, :], 1.0, -MAGIC, ALU.mult, ALU.add).then_inc(hq_ready, 1)
            quantise(0, 0)
            quantise(1, 1)
            normalise_batch(pool, per, ffn, B - 1)
            for n in range(T + 1):
                if n + 2 < T:
                    quantise(n + 2, n % 2)
                if n:
                    rounded(n - 1, 1 - n % 2)

        @block.vector
        def _(dve):
            def scales(b):
                own = slice(b * QT, (b + 1) * QT)
                dve.wait_ge(ffn["normed"], b + 1)
                dve.tensor_reduce(amax[:, ABS, own], xn[:, own, :], AX_X, ALU.max, apply_absolute_value=True)\
                   .then_inc(scale_step, 1)
                dve.wait_ge(scale_step, 3 * b + 1)
                dve.tensor_scalar(amax[:, AMAX, own], amax[:, ABS, own], 1e-5, None, ALU.max).then_inc(scale_step, 1)
                dve.wait_ge(scale_step, 3 * b + 2)
                dve.reciprocal(amax[:, INV, own], amax[:, AMAX, own])
                dve.tensor_scalar(amax[:, AG, own], amax[:, AMAX, own], wstat[:, 0:1], 1.0 / 127.0, ALU.mult, ALU.mult)
                dve.tensor_scalar(amax[:, AU, own], amax[:, AMAX, own], wstat[:, 1:2], 1.0 / 127.0, ALU.mult, ALU.mult)\
                   .then_inc(scale_step, 1)
                dve.wait_ge(scale_step, 3 * b + 3)
                dve.tensor_scalar(amax[:, SX, own], amax[:, INV, own], 127.0, None, ALU.mult).then_inc(scales_ready, 1)

            def transposed(n, u):
                dve.wait_ge(xT_done, n + 1)
                wait(dve, up_done, n - 1)
                dve.tensor_copy(xqT[:, u, :, :], ps_x[:, :, :]).then_inc(xT_ready, 1)

            def hidden(n, u):
                dve.wait_ge(up_done, n + 1)
                dve.wait_ge(silu_done, n + 1)
                wait(dve, r_ready, n - 1)
                dve.tensor_tensor(t[:, u, :], sg[:, u, :], ps_u[:, :], ALU.mult).then_inc(t_ready, 1)
                dve.wait_ge(t_ready, n + 1)
                dve.tensor_reduce(hs[:, u, 0:1], t[:, u, :], AX_X, ALU.max, apply_absolute_value=True)\
                   .then_inc(hstep, 1)
                dve.wait_ge(hstep, 3 * n + 1)
                dve.tensor_scalar(hs[:, u, 1:2], hs[:, u, 0:1], amax[:, AU, ds(n, 1)], 1e-5, ALU.mult, ALU.max)\
                   .then_inc(hstep, 1)
                dve.wait_ge(hstep, 3 * n + 2)
                dve.reciprocal(hs[:, u, 2:3], hs[:, u, 1:2]).then_inc(hstep, 1)
                dve.wait_ge(hstep, 3 * n + 3)
                dve.tensor_scalar(hs[:, u, 3:4], hs[:, u, 2:3], amax[:, AU, ds(n, 1)], 127.0, ALU.mult, ALU.mult)\
                   .then_inc(f_ready, 1)
                dve.tensor_scalar(ys[:, ds(n, 1)], hs[:, u, 1:2], gd[:, 0:1], None, ALU.mult)

            def residual(n, u):
                dve.wait_ge(y_done, n + 1)
                xs = x_sb[:, ds(n, 1), :].rearrange("p o d -> p (o d)")
                dve.scalar_tensor_tensor(out=xs, in0=ps_y[u][:, :], scalar=ys[:, ds(n, 1)], in1=xs,
                                         op0=ALU.mult, op1=ALU.add).then_inc(y_used, 1)

            def step(n, u):
                if live(n + 1):
                    transposed(n + 1, 1 - u)
                if live(n):
                    hidden(n, u)
                if live(n - 3):
                    residual(n - 3, 1 - u)
                if isinstance(n, int) and 0 <= n < B - 1:
                    scales(n + 1)
            dve.tensor_scalar(gd[:, 0:1], wstat[:, 2:3], per["gates"][:, 3:4], 1.0 / 127.0, ALU.mult, ALU.mult)
            scales(0)
            transposed(0, 0)
            schedule(dve, step)

        @block.scalar
        def _(act):
            def silu(n, u):
                act.wait_ge(gate_done, n + 1)
                wait(act, t_ready, n - 1)
                act.activation(sg[:, u, :], ps_g[:, :], ACT.Silu, scale=amax[:, AG, ds(n, 1)]).then_inc(silu_done, 1)

            def rounding(n, u):
                act.wait_ge(f_ready, n + 1)
                wait(act, hq_ready, n - 1)
                act.activation(r[:, u, :], t[:, u, :], ACT.Copy, scale=hs[:, u, 3:4], bias=MAGIC).then_inc(r_ready, 1)

            def transposed(n, u):
                act.wait_ge(hT_done, n + 1)
                wait(act, y_done, n - 1)
                act.copy(hqT[:, u, :, :], ps_h[:, :, :]).then_inc(hT_ready, 1)

            def step(n, u):
                if live(n):
                    silu(n, u)
                if live(n - 1):
                    rounding(n - 1, 1 - u)
                if live(n - 2):
                    transposed(n - 2, u)
            schedule(act, step)

        @block.tensor
        def _(pe):
            def x_transposes(n, u):
                pe.wait_ge(xq_ready, n + 1)
                wait(pe, xT_ready, n)
                for c in range(DC):
                    last = pe.transpose(ps_x[:, c, :], xq[:, u, c * P:(c + 1) * P], id16)
                last.then_inc(xT_done, 1)

            def gate_up(n, u):
                pe.wait_ge(xT_ready, n + 1)
                for out_, w, used, done in ((ps_g, wg, silu_done, gate_done), (ps_u, wu, t_ready, up_done)):
                    wait(pe, used, n)
                    for half in range(2):
                        cols = slice(half * 512, half * 512 + 512)
                        for c in range(DC):
                            last = pe.matmul(out_[:, cols], xqT[:, u, c, :], w[:, c, cols], start=(c == 0),
                                             stop=(c == DC - 1))
                    last.then_inc(done, 1)

            def h_transposes(n, u):
                pe.wait_ge(hq_ready, n + 1)
                wait(pe, hT_ready, n)
                for c in range(IC):
                    last = pe.transpose(ps_h[:, c, :], hq[:, u, c * P:(c + 1) * P], id16)
                last.then_inc(hT_done, 1)

            def down(n, u):
                pe.wait_ge(hT_ready, n + 1)
                wait(pe, y_used, n - 1)
                for c in range(IC):
                    last = pe.matmul(ps_y[u][:, :], hqT[:, u, c, :], wd[:, c, :], start=(c == 0), stop=(c == IC - 1))
                last.then_inc(y_done, 1)

            def step(n, u):
                if live(n + 1):
                    x_transposes(n + 1, 1 - u)
                if live(n):
                    gate_up(n, u)
                if live(n - 3):
                    down(n - 3, 1 - u)
                if live(n - 2):
                    h_transposes(n - 2, u)
            x_transposes(0, 0)
            schedule(pe, step)


def build(nc, a, out, stop=99):
    outer = ExitStack()
    with outer:
        sb = lambda n, s, d: outer.enter_context(nc.sbuf_tensor(n, s, d))
        per = {
            "x": sb("x", [P, T, D], F32), "st": sb("st", [P, T, 6], F32),
            "c32": sb("c32", [P, C32], F32), "c16": sb("c16", [P, C16], BF16),
            "mask_u8": sb("mask_u8", [P, T], U8), "mask": sb("mask", [P, T], F32),
            "gates_raw": sb("gates_raw", [P, 4], F32), "gates": sb("gates", [P, 4], F32),
        }
        phase_load(nc, a, per)
        qs = sb("qs", [P, B * H, S], BF16)
        ks = sb("ks", [P, B * H, S], BF16)
        arrived = {n: outer.enter_context(nc.semaphore("arrived_" + n)) for n in ("experts", "context", "weights")}
        with ExitStack() as inner:
            va = inner.enter_context(nc.sbuf_tensor("va", [P, STEPS, QT * G * (HD + 1)], F32))
            phase_prepare(nc, a, per, qs, ks, va)
            phase_attend(nc, per, qs, ks, va)
        wabs = sb("wabs", [P, 3], F32)
        late = ks[:, :, :].rearrange("p h s -> p (h s)").bitcast(F32)
        cuts = [0, T * D, 2 * T * D, 2 * T * D + 4 * DC * D, 2 * T * D + 4 * DC * D + 6 * INNER]
        ctok, ctxT, wqv, w32 = (late[:, lo:hi] for lo, hi in zip(cuts, cuts[1:]))
        ctok = ctok.rearrange("p (t d) -> p t d", d=D)
        ctxT = ctxT.rearrange("p (c n) -> p c n", c=DC)
        wqv = wqv.rearrange("p (k c d) -> p k c d", k=4, c=DC)
        w32 = w32.rearrange("p (i n) -> p i n", i=3)
        with ExitStack() as ctx:
            sbb = lambda n, s, d: ctx.enter_context(nc.sbuf_tensor(n, s, d))
            up = sbb("up", [P, NX, 2, DC, P], F32)
            down = sbb("down", [P, NX, D], F32)
            loads = [(down[:, :, :], a["down"], arrived["experts"])]
            loads += [(up[:, e, :, :, :], a["up"][e], arrived["experts"]) for e in range(NX)]
            loads += [(ctxT, a["ctxTC"], arrived["context"]),
                      (ctok, a["ctx"].rearrange("b (q p) d -> p (b q) d", p=P), arrived["context"]),
                      (wqv, a["wqv"], arrived["context"])]
            loads += [(w32[:, i, :], a[n], arrived["weights"]) for i, n in enumerate(("wg", "wu", "wd"))]
            phase_project(nc, a, per, qs, loads)
            if stop > 1:
                xT_all, wjunk = carve(qs[:, :, :].rearrange("p h s -> p (h s)").bitcast(F32),
                                      [(DC, T * P), (2 * INNER,)])
                nselT = sbb("nselT", [P, T * P], BF16)
                phase_route(nc, a, per, xT_all, nselT, down, arrived["experts"])
                phase_experts(nc, a, per, xT_all, nselT, up, down, w32, wjunk, wabs, arrived["experts"],
                              arrived["weights"])
        if stop > 2:
            with ExitStack() as ctx:
                sbc = lambda n, s, d: ctx.enter_context(nc.sbuf_tensor(n, s, d))
                wq16 = sbc("wq16", [P, 3, 2 * INNER], BF16)
                wstat = sbc("wstat", [P, 6], F32)
                free = qs[:, :, :].rearrange("p h s -> p (h s)").bitcast(F32)
                ffn = {"xn": free[:, B * H * S // 2 - T * D:].rearrange("p (t d) -> p t d", d=D),
                       "tmp": sbc("ffn_tmp", [P, 9, T], F32), "power": sbc("ffn_power", [P, QT], F32)}
                ffn.update({n: ctx.enter_context(nc.semaphore("ffn_" + n))
                            for n in ("steps", "power_ready", "stats_done", "normed")})
                phase_coattend(nc, a, per, ffn, free, ctok, ctxT, wqv, w32, wabs, wq16, wstat, arrived["context"])
                if stop > 3:
                    phase_bitffn(nc, per, ffn, free, wq16, wstat, out)
        if stop <= 3:
            with ExitStack() as ctx:
                st = ctx.enter_context(nc.semaphore("st"))
                block = ctx.enter_context(nc.Block())

                @block.sync
                def _(sp):
                    sp.dma_start(out.rearrange("b (q p) d -> p (b q) d", p=P), per["x"][:, :, :]).then_inc(st, 16)
                    sp.wait_ge(st, 16)


def constants():
    import numpy as np

    c32 = np.zeros((P, C32), np.float32)
    c32[:, C_ID:C_ID + P] = np.eye(P)
    inv = (np.float32(1.0) / np.float32(10000.0) ** (np.arange(0, HD, 2, dtype=np.float32) / np.float32(HD)))
    f = np.outer(np.arange(S, dtype=np.float32), inv.astype(np.float32)).astype(np.float32)
    cos = np.cos(f.astype(np.float64)).astype(np.float32)
    sin = np.sin(f.astype(np.float64)).astype(np.float32)
    cos, sin = np.concatenate([cos, cos], -1), np.concatenate([-sin, sin], -1)
    c32[:, C_COS:C_SIN] = cos.reshape(QT, P, HD).transpose(1, 0, 2).reshape(P, -1)
    c32[:, C_SIN:C_TRI] = sin.reshape(QT, P, HD).transpose(1, 0, 2).reshape(P, -1)
    c32[:, C_TRI:C_TRI + E * E] = np.tril(np.ones((E, E)), -1).reshape(1, -1)
    c16 = np.zeros((P, C16), np.float32)
    c16[:, B_ID:B_ID + P] = np.eye(P)
    pre = np.zeros((2, H, XROWS), np.float32)
    pre[0, :, MASK_ROW] = 1.0
    for h in range(H):
        pre[1, h, 3 * (h % G):3 * (h % G) + 3] = 1.0
    c16[:, B_PRE:C16] = pre.reshape(1, -1)
    skip = np.zeros((P, E, P), np.float32)
    for e in range(E):
        skip[e, e, :] = -BIG
    bits = lambda v: (v.view(np.uint32) >> 16).astype(np.uint16)
    return c32, bits(c16), bits(skip)


def layout(inputs):
    import numpy as np

    i = {k: np.asarray(v) for k, v in inputs.items()}
    row = lambda v: np.ascontiguousarray(v).reshape(1, -1)
    chunks = lambda w: np.ascontiguousarray(w.reshape(-1, P, w.shape[-1]).transpose(1, 0, 2))
    a = {"x": i["x"], "ctx": i["ctx_1024"]}
    ctxT = i["ctx_1024"].reshape(T * P, D).T
    a["ctxTC"] = chunks(ctxT)
    a["ctxT"] = np.ascontiguousarray(ctxT.reshape(DC, P, T, P).transpose(2, 1, 0, 3))
    a["mask"] = np.ascontiguousarray(i["mask_BxS2_bf1"].reshape(T, P).T).view(np.uint8)
    a["gates"] = row(np.concatenate([i["g_xattn"], i["g_ffn"]]))
    a["wq"], a["wk"], a["wv"] = (chunks(i[f"L0_xattn_W{n}"].T) for n in "qkv")
    a["bqk"] = row(np.concatenate([i["L0_xattn_bq"], i["L0_xattn_bk"]]))
    a["bv"], a["bp"] = row(i["L0_xattn_bv"]), row(i["L0_xattn_bp"])
    a["wp"] = chunks(i["L0_xattn_Wp"].T)
    a["gate_w"] = chunks(i["L0_ffn_gate_w"].T)
    a["lb"] = row(i["L0_ffn_lb_bias"])
    gate = np.concatenate([i["L0_ffn_expert_gate_w"], i["L0_ffn_shared_gate_w"].reshape(SH, I, D)])
    up = np.concatenate([i["L0_ffn_expert_up_w"], i["L0_ffn_shared_up_w"].reshape(SH, I, D)])
    a["up"] = np.ascontiguousarray(np.stack([gate, up], 1).reshape(NX, 2, I, DC, P).transpose(0, 4, 1, 3, 2))
    down = np.concatenate([i["L0_ffn_expert_down_w"].transpose(2, 0, 1),
                           i["L0_ffn_shared_down_w"].T.reshape(SH, I, D).transpose(1, 0, 2)], 1)
    a["down"] = np.ascontiguousarray(down)
    ws = i["L1_xattn_w_sim"].reshape(3, DC, P)
    a["wsim"] = np.ascontiguousarray(ws[1:].transpose(2, 0, 1))
    a["w1"] = row(i["L1_xattn_w_sim"][:D])
    a["bsim"], a["bqv"] = row(i["L1_xattn_b_sim"]), row(i["L1_xattn_b_qv"])
    a["wqv"] = np.ascontiguousarray(i["L1_xattn_W_qv"].reshape(4, DC, P, D).transpose(2, 0, 1, 3))
    a["wg"], a["wu"], a["wd"] = (chunks(i[f"L1_ffn_w_{n}"].T).reshape(P, -1) for n in ("gate", "up", "down"))
    a["c32"], a["c16"], a["skip"] = constants()
    return a


def kernel(**inputs):
    import numpy as np
    import concourse.bacc as bacc
    from concourse.bass_utils import run_bass_kernel_spmd as run

    nc = bacc.Bacc("TRN2", target_bir_lowering=False, num_devices=1)
    arrays, args = {}, {}
    for name, v in layout(inputs).items():
        v = np.ascontiguousarray(v)
        arrays[f"in_{name}"] = v
        args[name] = nc.dram_tensor(f"in_{name}", v.shape, mybir.dt.from_np(v.dtype), kind="ExternalInput").ap()
    out = nc.dram_tensor("out", (B, S, D), F32, kind="ExternalOutput").ap()
    build(nc, args, out)
    return run(nc, [arrays], core_ids=[0]).results[0]["out"]
```

```python
from contextlib import ExitStack

import concourse.bass as bass
from concourse import mybir
from concourse.alu_op_type import AluOpType as ALU

ACT = mybir.ActivationFunctionType
F32 = mybir.dt.float32
BF16 = mybir.dt.bfloat16
F16 = mybir.dt.float16
U8 = mybir.dt.uint8
U16 = mybir.dt.uint16
AX_X = mybir.AxisListType.X
ds = bass.ds

P = 128
B = 4
S = 512
D = 256
DC = D // P
QT = S // P
T = B * QT
H = 16
HD = D // H
G = 4
NG = H // G
STEPS = B * NG
E = 8
I = 128
SH = 2
NX = E + SH
INNER = 1024
IC = INNER // P
EPS = 1e-5
BIG = 1e30
FAR = 1e38
XS = 2.0 ** 11
WS = 2.0 ** 14
HPAD = 32
XROWS = 32
MASK_ROW = 3 * G
SCALE = HD ** -0.5
MAGIC = 1.5 * 2.0 ** 23

C_ID, C_COS, C_SIN, C_TRI, C32 = 0, 128, 192, 256, 320
B_ID, B_PRE, C16 = 0, 128, 128 + 2 * H * XROWS

Q1, Q2, Q3 = slice(0, 3), slice(3, 5), slice(5, 6)
K1, K2, K3 = slice(1, 6, 2), slice(2, 5, 2), slice(0, 1)


def wait(eng, sem, value):
    if not isinstance(value, int) or value > 0:
        eng.wait_ge(sem, value)


def live(k):
    return not isinstance(k, int) or 0 <= k < T


def schedule(eng, step):
    for n in range(4):
        step(n, n % 2)
    with eng.Fori(2, (T - 2) // 2) as half_n0:
        for u in range(2):
            step(2 * half_n0 + u, u)
    for n in range(T - 2, T + 3):
        step(n, n % 2)


def carve(region, sizes):
    views, lo = [], 0
    for shape in sizes:
        size = 1
        for n in shape:
            size *= n
        v = region[:, lo:lo + size]
        lo += size
        if len(shape) == 2:
            v = v.rearrange("p (a b) -> p a b", a=shape[0])
        if len(shape) == 3:
            v = v.rearrange("p (a b c) -> p a b c", a=shape[0], b=shape[1])
        views.append(v)
    return views


def row_statistics(nc, sb, sem, per, tag):
    st, x_sb = per["st"], per["x"]
    tmp = sb("lntmp" + tag, [P, 4, T], F32)
    mean = sb("mean" + tag, [P, T], F32)
    rstd = sb("rstd" + tag, [P, T], F32)
    power = sb("power" + tag, [P, T], F32)
    chain = sem("ln_chain" + tag)
    var_ready = sem("var_ready" + tag)
    rstd_ready = sem("rstd_ready" + tag)

    def vector(dve, i, tiles):
        own = slice(*tiles)
        steps = 4 * i + 1
        for t in range(*tiles):
            last = dve.bn_stats(st[:, t, :], x_sb[:, t, :])
        last.then_inc(chain, 1)
        dve.wait_ge(chain, steps)
        dve.tensor_tensor(tmp[:, 0, own], st[:, own, 1], st[:, own, 4], ALU.subtract)
        dve.tensor_tensor(tmp[:, 1, own], st[:, own, 1], st[:, own, 4], ALU.add)
        dve.tensor_tensor(tmp[:, 2, own], st[:, own, 2], st[:, own, 5], ALU.add).then_inc(chain, 1)
        dve.wait_ge(chain, steps + 1)
        dve.tensor_tensor(tmp[:, 3, own], tmp[:, 0, own], tmp[:, 0, own], ALU.mult)
        dve.tensor_scalar(mean[:, own], tmp[:, 1, own], 0.5, None, ALU.mult).then_inc(chain, 1)
        dve.wait_ge(chain, steps + 2)
        dve.tensor_scalar(tmp[:, 0, own], tmp[:, 3, own], 0.25, EPS, ALU.mult, ALU.add).then_inc(chain, 1)
        dve.wait_ge(chain, steps + 3)
        dve.scalar_tensor_tensor(out=tmp[:, 1, own], in0=tmp[:, 2, own], scalar=1.0 / D, in1=tmp[:, 0, own],
                                 op0=ALU.mult, op1=ALU.add).then_inc(var_ready, 1)

    def pool(pool_, i, tiles):
        own = slice(*tiles)
        if i == 0:
            pool_.memset(power[:, :], -0.5).then_inc(rstd_ready, 1)
            pool_.wait_ge(rstd_ready, 1)
        pool_.wait_ge(var_ready, i + 1)
        pool_.tensor_tensor(rstd[:, own], tmp[:, 1, own], power[:, own], ALU.pow).then_inc(rstd_ready, 1)

    return mean, rstd, rstd_ready, vector, pool


def batch_norm_state(nc, ctx, tag, tile):
    norm = {"tile": tile, "tmp": ctx.enter_context(nc.sbuf_tensor("norm_tmp" + tag, [P, 9, T], F32)),
            "power": ctx.enter_context(nc.sbuf_tensor("norm_power" + tag, [P, QT], F32))}
    for n in ("steps", "power_ready", "stats_done", "centred", "normed"):
        norm[n] = ctx.enter_context(nc.semaphore(n + tag))
    return norm


def batch_statistics(pool, per, norm, b):
    st, tmp, steps = per["st"], norm["tmp"], norm["steps"]
    own = slice(b * QT, (b + 1) * QT)
    ready = 5 * b
    if b == 0:
        pool.memset(norm["power"][:, :], -0.5).then_inc(norm["power_ready"], 1)
        pool.wait_ge(norm["power_ready"], 1)
    pool.wait_ge(norm["stats_done"], (b + 1) * QT)
    pool.tensor_tensor(tmp[:, 0, own], st[:, own, 1], st[:, own, 4], ALU.subtract)
    pool.tensor_tensor(tmp[:, 1, own], st[:, own, 1], st[:, own, 4], ALU.add)
    pool.tensor_tensor(tmp[:, 2, own], st[:, own, 2], st[:, own, 5], ALU.add).then_inc(steps, 1)
    pool.wait_ge(steps, ready + 1)
    pool.tensor_tensor(tmp[:, 3, own], tmp[:, 0, own], tmp[:, 0, own], ALU.mult)
    pool.tensor_scalar(tmp[:, 4, own], tmp[:, 1, own], -0.5, None, ALU.mult)
    pool.tensor_scalar(tmp[:, 5, own], tmp[:, 2, own], 1.0 / D, None, ALU.mult).then_inc(steps, 1)
    pool.wait_ge(steps, ready + 2)
    pool.tensor_scalar(tmp[:, 6, own], tmp[:, 3, own], 0.25, EPS, ALU.mult, ALU.add).then_inc(steps, 1)
    pool.wait_ge(steps, ready + 3)
    pool.tensor_tensor(tmp[:, 7, own], tmp[:, 5, own], tmp[:, 6, own], ALU.add).then_inc(steps, 1)
    pool.wait_ge(steps, ready + 4)
    pool.tensor_tensor(tmp[:, 8, own], tmp[:, 7, own], norm["power"][:, 0:QT], ALU.pow).then_inc(steps, 1)
    pool.wait_ge(steps, ready + 5)


def normalise_batch(pool, per, norm, b):
    batch_statistics(pool, per, norm, b)
    x_sb, tmp = per["x"], norm["tmp"]
    tiles = range(b * QT, (b + 1) * QT)
    for t in tiles:
        last = pool.tensor_scalar(norm["tile"](t), x_sb[:, t, :], 1.0, tmp[:, 4, t:t + 1], ALU.mult, ALU.add)
    last.then_inc(norm["centred"], 1)
    pool.wait_ge(norm["centred"], b + 1)
    for t in tiles:
        last = pool.tensor_scalar(norm["tile"](t), norm["tile"](t), tmp[:, 8, t:t + 1], 0.0, ALU.mult, ALU.add)
    last.then_inc(norm["normed"], 1)


def phase_prepare(nc, a, per, qs, ks, va):
    x_sb, c32, c16 = per["x"], per["c32"], per["c16"]
    id32 = c32[:, C_ID:C_ID + P]
    id16 = c16[:, B_ID:B_ID + P]
    cos = c32[:, C_COS:C_SIN].rearrange("p (q d) -> p q d", q=QT)
    sin = c32[:, C_SIN:C_TRI].rearrange("p (q d) -> p q d", q=QT)
    preset = c16[:, B_PRE:C16].rearrange("p (h r) -> p h r", r=XROWS)
    with ExitStack() as ctx:
        sb = lambda n, s, d: ctx.enter_context(nc.sbuf_tensor(n, s, d))
        ps = lambda n, s, d: ctx.enter_context(nc.psum_tensor(n, s, d))
        sem = lambda n: ctx.enter_context(nc.semaphore(n))
        wq, wk, wv = (sb(n, [P, DC, D], F32) for n in ("wq", "wk", "wv"))
        bqk = sb("bqk", [P, 2 * D], F32)
        bv = sb("bv", [P, D], F32)
        ctxT = sb("ctxT", [P, 2, DC, P], F32)
        xn = sb("xn", [P, D], F32)
        xnT = sb("xnT", [P, 2, DC, P], F32)
        qkb = sb("qkb", [P, 2, 2 * H, HD], F32)
        rope2 = sb("rope2", [P, 2 * H, HD], F32)
        qkr = sb("qkr", [P, 2, 2 * H, HD], F32)
        rest = sb("rest", [P, 2 * H, HD], F32)
        stack = sb("stack", [P, 2, 2 * H, P], BF16)
        mbias = sb("mbias", [P, T], F32)
        mean, rstd, rstd_ready, ln_vector, ln_pool = row_statistics(nc, sb, sem, per, "A")
        ps_st = [ps(f"ps_st{i}", [P, 8, P], BF16) for i in range(4)]
        ps_T = ps("ps_T", [P, DC, P], F32)
        ps_qk = ps("ps_qk", [P, 2 * D], F32)
        ps_v = ps("ps_v", [P, D], F32)

        first_x_in, x_in, consts, masks, gates = (sem("first_x_in"), sem("x_in"), sem("consts"), sem("masks"),
                                                  sem("gates_in"))
        weights, ctx_in = sem("weights"), [sem("ctx_in0"), sem("ctx_in1")]
        xn_ready, xT_done, xT_copied = sem("xn_ready"), sem("xT_done"), sem("xT_copied")
        proj_done, qk_copied, v_copied = sem("proj_done"), sem("qk_copied"), sem("v_copied")
        vb_done, mask_done = sem("vb_done"), sem("mask_done")
        rope_half, rope_done, rest1_done = sem("rope_half"), sem("rope_done"), sem("rest1_done")
        part1_done, part2_done, part3_done = sem("part1_done"), sem("part2_done"), sem("part3_done")
        stackT_done, stackT_v, stackT_a = sem("stackT_done"), sem("stackT_v"), sem("stackT_a")
        block = ctx.enter_context(nc.Block())

        va_v = va[:, :, :].rearrange("p s (k j d) -> p s k j d", k=QT, j=G)
        parts = lambda u, first: stack[:, u, first:first + H, 0:96].rearrange("p h (s d) -> p h s d", d=HD)

        def stack_out(copy, dst, i, n):
            at = (n // QT) * H + 8 * (i % 2)
            return copy(dst[:, ds(at, 8), ds((n % QT) * P, P)], ps_st[i][:, :, :])

        @block.sync
        def _(sp):
            xv = a["x"].rearrange("b (q p) d -> p (b q) d", p=P)

            def load_x(b):
                sp.dma_start(x_sb[:, QT * b:QT * (b + 1), :], xv[:, QT * b:QT * (b + 1), :])\
                  .then_inc(x_in if b else first_x_in, 16)
            load_x(0)
            for w, n in ((wq, "wq"), (wk, "wk"), (wv, "wv")):
                sp.dma_start(w[:, :, :], a[n]).then_inc(weights, 16)

            def load(n, u):
                wait(sp, proj_done, n - 1)
                sp.dma_start(ctxT[:, u, :, :], a["ctxT"][ds(n, 1), :, :, :]).then_inc(ctx_in[u], 16)
            load(0, 0)
            load(1, 1)
            for b in range(1, B):
                load_x(b)
            with sp.Fori(1, T // 2) as half_n0:
                n0 = 2 * half_n0
                for u in range(2):
                    load(n0 + u, u)

        @block.vector
        def _(dve):
            dve.wait_ge(first_x_in, 16)
            ln_vector(dve, 0, (0, QT))
            dve.wait_ge(masks, 16)
            dve.tensor_copy(per["mask"][:, :], per["mask_u8"][:, :]).then_inc(mask_done, 1)
            dve.wait_ge(mask_done, 1)
            dve.tensor_scalar(mbias[:, :], per["mask"][:, :], BIG, -BIG, ALU.mult, ALU.add).then_inc(mask_done, 1)
            dve.wait_ge(mask_done, 2)
            dve.wait_ge(consts, 16 * 2)
            for u in range(2):
                dve.tensor_copy(stack[:, u, :, 96:128], preset)
            for k in range(QT):
                m = per["mask"][:, k:T:QT].rearrange("p (b g j) -> p b g j", g=1, j=1)
                vm = va_v[:, :, k, :, HD].rearrange("p (b g) j -> p b g j", b=B)
                dve.tensor_copy(vm, m.broadcast_to([P, B, NG, G]))

            def normalise(n):
                wait(dve, xT_done, n)
                dve.tensor_scalar(xn[:, :], x_sb[:, ds(n, 1), :], mean[:, ds(n, 1)], rstd[:, ds(n, 1)],
                                  ALU.subtract, ALU.mult).then_inc(xn_ready, 1)

            def third_part(n, u):
                dve.wait_ge(part2_done, n + 1)
                for first, slot, src in ((0, Q3, Q2), (H, K3, K2)):
                    last = dve.tensor_tensor(parts(u, first)[:, :, slot.start, :], rest[:, first:first + H, :],
                                             parts(u, first)[:, :, src.start, :], ALU.subtract)
                dve.tensor_copy(stack[:, u, H:2 * H, 96 + MASK_ROW],
                                mbias[:, ds(n, 1)].broadcast_to([P, H])).then_inc(part3_done, 1)

            def stack_copy(n):
                dve.wait_ge(stackT_done, 4 * n + 2)
                for i in (0, 1):
                    last = stack_out(dve.tensor_copy, qs, i, n)
                last.then_inc(stackT_v, 1)

            def projections(n, u):
                dve.wait_ge(proj_done, n + 1)
                wait(dve, rope_done, n - 1)
                dve.tensor_tensor(qkb[:, u, :, :], ps_qk[:, :].rearrange("p (h d) -> p h d", d=HD),
                                  bqk[:, :].rearrange("p (h d) -> p h d", d=HD), ALU.add).then_inc(qk_copied, 1)
                out = va_v[:, ds((n // QT) * NG, NG), ds(n % QT, 1), :, 0:HD].rearrange("p g k j d -> p (g k) j d")
                heads = lambda v: v[:, :].rearrange("p (g j d) -> p g j d", g=NG, j=G)
                dve.tensor_tensor(out, heads(ps_v), heads(bv), ALU.add).then_inc(vb_done, 1)
                dve.wait_ge(vb_done, n + 1)
                dve.tensor_scalar(out, out, per["mask"][:, ds(n, 1)], None, ALU.mult).then_inc(v_copied, 1)

            def transposed(n, u):
                dve.wait_ge(xT_done, n + 1)
                wait(dve, proj_done, n - 1)
                dve.tensor_copy(xnT[:, u, :, :], ps_T[:, :, :]).then_inc(xT_copied, 1)

            def step(n, u):
                if live(n):
                    projections(n, u)
                if live(n + 1):
                    transposed(n + 1, 1 - u)
                if live(n + 2):
                    normalise(n + 2)
                if live(n - 3):
                    stack_copy(n - 3)
                if live(n - 2):
                    third_part(n - 2, u)
                if isinstance(n, int) and n == 1:
                    dve.wait_ge(x_in, 16 * (B - 1))
                    ln_vector(dve, 1, (QT, T))
                    dve.wait_ge(rstd_ready, 3)
            dve.wait_ge(rstd_ready, 2)
            normalise(0)
            transposed(0, 0)
            normalise(1)
            dve.wait_ge(weights, 16 * 5)
            schedule(dve, step)

        @block.scalar
        def _(act):
            def first_part(n, u):
                act.wait_ge(rope_done, n + 1)
                wait(act, stackT_done, 4 * (n - 1))
                for first, slots in ((0, Q1), (H, K1)):
                    src = qkr[:, u, first:first + H, :].rearrange("p h (o d) -> p h o d", o=1)
                    last = act.copy(parts(u, first)[:, :, slots, :], src.broadcast_to([P, H, 3, HD]))
                last.then_inc(part1_done, 1)

            def second_part(n, u):
                act.wait_ge(rest1_done, n + 1)
                for first, slots in ((0, Q2), (H, K2)):
                    src = rest[:, first:first + H, :].rearrange("p h (o d) -> p h o d", o=1)
                    last = act.copy(parts(u, first)[:, :, slots, :], src.broadcast_to([P, H, 2, HD]))
                last.then_inc(part2_done, 1)

            def stack_copy(n):
                for i in (2, 3):
                    act.wait_ge(stackT_done, 4 * n + i + 1)
                    last = stack_out(act.copy, ks, i, n)
                last.then_inc(stackT_a, 1)

            def step(n, u):
                if live(n - 1):
                    second_part(n - 1, 1 - u)
                if live(n):
                    first_part(n, u)
                if live(n - 2):
                    stack_copy(n - 2)
            act.dma_start(per["gates_raw"][:, :], a["gates"].to_broadcast([P, 4])).then_inc(gates, 16)
            act.dma_start(c32[:, :], a["c32"]).then_inc(consts, 16)
            act.dma_start(c16[:, :].bitcast(U16), a["c16"]).then_inc(consts, 16)
            act.dma_start(per["mask_u8"][:, :], a["mask"]).then_inc(masks, 16)
            act.dma_start(bqk[:, :], a["bqk"].to_broadcast([P, 2 * D])).then_inc(weights, 16)
            act.dma_start(bv[:, :], a["bv"].to_broadcast([P, D])).then_inc(weights, 16)
            act.wait_ge(gates, 16)
            act.activation(per["gates"][:, :], per["gates_raw"][:, :], ACT.Tanh)
            schedule(act, step)

        @block.gpsimd
        def _(pool):
            ln_pool(pool, 0, (0, QT))
            pool.wait_ge(consts, 16 * 2)

            def rope(n, u):
                pool.wait_ge(qk_copied, n + 1)
                wait(pool, rope_done, n)
                wait(pool, rest1_done, n - 1)
                c = cos[:, ds(n % QT, 1), :].broadcast_to([P, 2 * H, HD])
                s = sin[:, ds(n % QT, 1), :]
                lo, hi = slice(0, HD // 2), slice(HD // 2, HD)
                pool.tensor_tensor(qkr[:, u, :, :], qkb[:, u, :, :], c, ALU.mult)
                pool.tensor_tensor(rope2[:, :, lo], qkb[:, u, :, hi], s[:, :, lo].broadcast_to([P, 2 * H, HD // 2]),
                                   ALU.mult)
                pool.tensor_tensor(rope2[:, :, hi], qkb[:, u, :, lo], s[:, :, hi].broadcast_to([P, 2 * H, HD // 2]),
                                   ALU.mult).then_inc(rope_half, 1)
                pool.wait_ge(rope_half, n + 1)
                pool.tensor_tensor(qkr[:, u, :, :], qkr[:, u, :, :], rope2[:, :, :], ALU.add).then_inc(rope_done, 1)

            def first_rest(n, u):
                pool.wait_ge(part1_done, n + 1)
                wait(pool, part3_done, n)
                for first, slot in ((0, Q1), (H, K1)):
                    last = pool.tensor_tensor(rest[:, first:first + H, :], qkr[:, u, first:first + H, :],
                                              parts(u, first)[:, :, slot.start, :], ALU.subtract)
                last.then_inc(rest1_done, 1)

            def step(n, u):
                if live(n):
                    rope(n, u)
                if live(n - 1):
                    first_rest(n - 1, 1 - u)
                if isinstance(n, int) and n == 1:
                    ln_pool(pool, 1, (QT, T))
            schedule(pool, step)

        @block.tensor
        def _(pe):
            def stack_transposes(n, u):
                pe.wait_ge(part3_done, n + 1)
                for i in range(4):
                    if i == 0:
                        wait(pe, stackT_v, n)
                    if i == 2:
                        wait(pe, stackT_a, n)
                    for h in range(8):
                        last = pe.transpose(ps_st[i][:, h, :], stack[:, u, 8 * i + h, :], id16)
                    last.then_inc(stackT_done, 1)

            def x_transposes(n, u):
                pe.wait_ge(xn_ready, n + 1)
                wait(pe, xT_copied, n)
                for c in range(DC):
                    last = pe.transpose(ps_T[:, c, :], xn[:, c * P:(c + 1) * P], id32)
                last.then_inc(xT_done, 1)

            def projections(n, u):
                pe.wait_ge(xT_copied, n + 1)
                wait(pe, v_copied, n)
                pe.wait_ge(ctx_in[u], (n // 2 + 1) * 16)
                for out, src, w in ((ps_qk[:, 0:D], xnT, wq), (ps_qk[:, D:2 * D], ctxT, wk), (ps_v[:, :], ctxT, wv)):
                    for c in range(DC):
                        last = pe.matmul(out, src[:, u, c, :], w[:, c, :], start=(c == 0), stop=(c == DC - 1))
                last.then_inc(proj_done, 1)

            def step(n, u):
                if live(n + 1):
                    x_transposes(n + 1, 1 - u)
                if live(n):
                    projections(n, u)
                if live(n - 3):
                    stack_transposes(n - 3, 1 - u)
            pe.wait_ge(consts, 16 * 2)
            x_transposes(0, 0)
            pe.wait_ge(weights, 16 * 5)
            schedule(pe, step)


def phase_attend(nc, a, per, qs, ks, va):
    id16 = per["c16"][:, B_ID:B_ID + P]
    with ExitStack() as ctx:
        sb = lambda n, s, d: ctx.enter_context(nc.sbuf_tensor(n, s, d))
        ps = lambda n, s, d: ctx.enter_context(nc.psum_tensor(n, s, d))
        sem = lambda n: ctx.enter_context(nc.semaphore(n))
        prob = sb("prob", [P, 2, G, S], F32)
        vst = sb("vst", [P, 2, QT, G * HPAD], F32)
        mx = sb("mx", [P, 2, QT, G], F32)
        minus = sb("minus", [P, QT, G], F32)
        mrest = sb("mrest", [P, 2, QT, G], F32)
        mparts = sb("mparts", [P, 2, QT, XROWS], BF16)
        ps_f = [ps(f"ps_f{i}", [P, S], F32) for i in range(2)]
        ps_s = [ps(f"ps_s{i}", [P, 2, S], F32) for i in range(2)]
        ps_o = ps("ps_o", [P, S], F32)
        ps_m = ps("ps_m", [P, QT, P], BF16)
        scored, max_done = sem("scored"), sem("max_done")
        mpreset, split1, split_done = sem("mpreset"), sem("split1"), sem("split_done")
        mT_done, m_ready = sem("mT_done"), sem("m_ready")
        v_ready = sem("v_ready")
        bp = sb("bp", [P, D], F32)
        coef = per["coef"]
        gated = sb("gated", [P, D], F32)
        bp_in, coef_done, gated_done = sem("bp_in"), sem("coef_done"), sem("gated_done")
        s_done, exp_done, pv_done, o_copied = sem("s_done"), sem("exp_done"), sem("pv_done"), sem("o_copied")
        block = ctx.enter_context(nc.Block())
        o32 = qs[:, :, :].rearrange("p h s -> p (h s)").bitcast(F32).rearrange("p (s c) -> p s c", s=STEPS)

        @block.sync
        def _(sp):
            sp.dma_start(bp[:, :], a["bp"].to_broadcast([P, D])).then_inc(bp_in, 16)

        @block.tensor
        def _(pe):
            def first_scores(f, idx):
                qt, j = divmod(idx, G)
                wait(pe, max_done, f * 16 + idx - 1)
                pe.matmul(ps_f[idx % 2][:, :], qs[:, ds(f * G + j, 1), qt * P:(qt + 1) * P],
                          ks[:, ds(f * G + j, 1), :], start=True, stop=True).then_inc(scored, 1)

            def scores(s, kt, half):
                wait(pe, exp_done, s * 8 + kt * 2 + half - 1)
                for j in (2 * half, 2 * half + 1):
                    last = pe.matmul(ps_s[half][:, j % 2, :], ks[:, ds(s * G + j, 1), kt * P:(kt + 1) * P],
                                     qs[:, ds(s * G + j, 1), :], start=True, stop=True)
                last.then_inc(s_done, 1)

            def values(s, u, kt, half):
                pe.wait_ge(exp_done, s * 8 + kt * 2 + 2)
                if kt == 0 and half == 0:
                    pe.wait_ge(v_ready, s + 1)
                    wait(pe, o_copied, s)
                for j in (2 * half, 2 * half + 1):
                    last = pe.matmul(ps_o[HPAD * j:HPAD * (j + 1), :], vst[:, u, kt, HPAD * j:HPAD * (j + 1)],
                                     prob[:, kt % 2, j, :], start=(kt == 0), stop=(kt == QT - 1))
                if half:
                    last.then_inc(pv_done, 1)

            def maxima(s, u):
                pe.wait_ge(split_done, s + 1)
                wait(pe, m_ready, 2 * s)
                for qt in range(QT):
                    last = pe.transpose(ps_m[96:128, qt, :], mparts[:, u, qt, :], id16)
                last.then_inc(mT_done, 1)

            def step(s, u, before, ahead, next_):
                for kt in range(QT):
                    for part in range(QT):
                        if ahead:
                            first_scores(s + 2, 4 * kt + part)
                        if kt == 0 and part == 0:
                            pe.wait_ge(m_ready, 2 * s + 2)
                        if part < 2:
                            scores(s, kt, part)
                        elif kt:
                            values(s, u, kt - 1, part - 2)
                        elif before:
                            values(s - 1, 1 - u, QT - 1, part - 2)
                    if kt == 0 and next_:
                        maxima(s + 1, 1 - u)

            for f in range(2):
                for idx in range(16):
                    first_scores(f, idx)
            maxima(0, 0)
            step(0, 0, False, True, True)
            step(1, 1, True, True, True)
            with pe.Fori(1, (STEPS - 2) // 2) as half_s0:
                s0 = 2 * half_s0
                for u in range(2):
                    step(s0 + u, u, True, True, True)
            step(STEPS - 2, 0, True, False, True)
            step(STEPS - 1, 1, True, False, False)
            for half in range(2):
                values(STEPS - 1, 1, QT - 1, half)

        @block.vector
        def _(dve):
            def maxima(f, u):
                wait(dve, split_done, f - 1)
                for idx in range(16):
                    dve.wait_ge(scored, f * 16 + idx + 1)
                    dve.tensor_reduce(mx[:, u, idx // G, idx % G:idx % G + 1], ps_f[idx % 2][:, :], AX_X,
                                      ALU.max).then_inc(max_done, 1)
            maxima(0, 0)
            maxima(1, 1)
            with dve.Fori(1, STEPS // 2) as half_f0:
                f0 = 2 * half_f0
                for u in range(2):
                    maxima(f0 + u, u)

        @block.gpsimd
        def _(pool):
            pool.memset(vst[:, :, :, :], 0.0)
            pool.memset(minus[:, :, :], -1.0)
            pool.memset(mparts[:, :, :, :], 0.0).then_inc(mpreset, 1)
            pool.wait_ge(mpreset, 1)
            pool.memset(mparts[:, :, :, MASK_ROW:MASK_ROW + 1], 1.0).then_inc(mpreset, 1)
            pool.wait_ge(mpreset, 2)

            def split(s, u):
                out = mparts[:, u, :, 0:3 * G].rearrange("p q (j i) -> p q j i", i=3)
                pool.wait_ge(max_done, 16 * (s + 1))
                wait(pool, mT_done, s - 1)
                pool.tensor_tensor(out[:, :, :, 0], mx[:, u, :, :], minus[:, :, :], ALU.mult).then_inc(split1, 1)
                pool.wait_ge(split1, s * 4 + 1)
                pool.tensor_tensor(mrest[:, 0, :, :], mx[:, u, :, :], out[:, :, :, 0], ALU.add).then_inc(split1, 1)
                pool.wait_ge(split1, s * 4 + 2)
                pool.tensor_tensor(out[:, :, :, 1], mrest[:, 0, :, :], minus[:, :, :], ALU.mult).then_inc(split1, 1)
                pool.wait_ge(split1, s * 4 + 3)
                pool.tensor_tensor(mrest[:, 1, :, :], mrest[:, 0, :, :], out[:, :, :, 1], ALU.add).then_inc(split1, 1)
                pool.wait_ge(split1, s * 4 + 4)
                pool.tensor_tensor(out[:, :, :, 2], mrest[:, 1, :, :], minus[:, :, :], ALU.mult)\
                    .then_inc(split_done, 1)

            def stage_values(s, u):
                wait(pool, pv_done, QT * (s - 1))
                pool.tensor_copy(vst[:, u, :, :].rearrange("p k (j c) -> p (k j) c", c=HPAD)[:, :, 0:HD + 1],
                                 va[:, ds(s, 1), :].rearrange("p o (k d) -> p (o k) d", d=HD + 1)).then_inc(v_ready, 1)

            def bias(t):
                wait(pool, gated_done, 2 * t)
                pool.tensor_tensor(gated[:, :], bp[:, :], coef[:, ds(t, 1)].broadcast_to([P, D]), ALU.mult)\
                    .then_inc(gated_done, 1)
                pool.wait_ge(gated_done, 2 * t + 1)
                xs = per["x"][:, ds(t, 1), :].rearrange("p o d -> p (o d)")
                pool.tensor_tensor(xs, xs, gated[:, :], ALU.add).then_inc(gated_done, 1)

            pool.tensor_tensor(coef[:, :], per["mask"][:, :], per["gates"][:, 0:1].broadcast_to([P, T]), ALU.mult)\
                .then_inc(coef_done, 1)
            pool.wait_ge(coef_done, 1)
            pool.wait_ge(bp_in, 16)
            for s in range(2):
                split(s, s)
                stage_values(s, s)
                bias(s)
            with pool.Fori(1, STEPS // 2) as half_s0:
                s0 = 2 * half_s0
                for u in range(2):
                    split(s0 + u, u)
                    stage_values(s0 + u, u)
                    bias(s0 + u)

        @block.scalar
        def _(act):
            def exps(s, kt):
                for half in range(2):
                    act.wait_ge(s_done, s * 8 + kt * 2 + half + 1)
                    if half == 0:
                        wait(act, pv_done, s * QT + kt - 1)
                    act.activation(prob[:, kt % 2, 2 * half:2 * half + 2, :], ps_s[half][:, :, :], ACT.Exp,
                                   scale=SCALE).then_inc(exp_done, 1)

            def spread_maxima(s, half):
                act.wait_ge(mT_done, s + 1)
                act.copy(qs[96:128, ds(s * G + 2 * half, 2), :],
                         ps_m[96:128, :, :].rearrange("p q (o c) -> p o (q c)", o=1).broadcast_to([32, 2, S]))\
                    .then_inc(m_ready, 1)

            def sums_out(s):
                act.wait_ge(pv_done, QT * (s + 1))
                act.copy(o32[:, ds(s, 1), 0:S], ps_o[:, :]).then_inc(o_copied, 1)

            def step(s, before, next_):
                for kt in range(QT):
                    exps(s, kt)
                    if kt == 0 and before:
                        sums_out(s - 1)
                    if kt in (1, 2) and next_:
                        spread_maxima(s + 1, kt - 1)
            for half in range(2):
                spread_maxima(0, half)
            step(0, False, True)
            with act.Fori(1, STEPS - 1) as s:
                step(s, True, True)
            step(STEPS - 1, True, False)
            sums_out(STEPS - 1)


def phase_project(nc, a, per, norm, qs, loads):
    x_sb, st = per["x"], per["st"]
    id32 = per["c32"][:, C_ID:C_ID + P]
    o32 = qs[:, :, :].rearrange("p h s -> p (h s)").bitcast(F32).rearrange("p (s c) -> p s c", s=STEPS)
    with ExitStack() as ctx:
        sb = lambda n, s, d: ctx.enter_context(nc.sbuf_tensor(n, s, d))
        ps = lambda n, s, d: ctx.enter_context(nc.psum_tensor(n, s, d))
        sem = lambda n: ctx.enter_context(nc.semaphore(n))
        wp = sb("wp", [P, DC, D], F32)
        stage = sb("stage", [P, 2, S], F32)
        recip = sb("recip", [P, NG, QT, G], F32)
        on = sb("on", [P, QT, D], F32)
        onT = sb("onT", [P, DC, S], F32)
        coef = per["coef"]
        ps_t = [ps(f"ps_t{i}", [P, QT, G, HPAD], F32) for i in range(2)]
        ps_o = [ps(f"ps_oT{i}", [P, DC, 2 * P], F32) for i in range(2)]
        ps_y = [ps(f"ps_y{i}", [P, 2, D], F32) for i in range(2)]
        wp_in, staged, t_done, r_done, on_done = (sem("wp_in"), sem("staged"), sem("t_done"),
                                                         sem("r_done"), sem("on_done"))
        oT_done, oT_ready, y_done, y_used = sem("oT_done"), sem("oT_ready"), sem("y_done"), sem("y_used")
        block = ctx.enter_context(nc.Block())

        @block.sync
        def _(sp):
            sp.dma_start(wp[:, :, :], a["wp"]).then_inc(wp_in, 16)
            for dst, src, arrived in loads:
                sp.dma_start(dst, src).then_inc(arrived, 16)

        @block.scalar
        def _(act):
            def stage_sums(s, u):
                wait(act, t_done, s - 1)
                act.copy(stage[:, u, :], o32[:, ds(s, 1), 0:S].rearrange("p o c -> p (o c)")).then_inc(staged, 1)

            def transposed(b):
                for i in range(2):
                    act.wait_ge(oT_done, b * 2 + i + 1)
                    last = act.copy(onT[:, :, i * 2 * P:(i + 1) * 2 * P], ps_o[i][:, :, :])
                last.then_inc(oT_ready, 1)
            for g in range(NG):
                stage_sums(g, g % 2)
            stage_sums(NG, 0)
            stage_sums(NG + 1, 1)
            transposed(0)
            with act.Fori(1, B - 1) as b:
                stage_sums(b * NG + 2, 0)
                stage_sums(b * NG + 3, 1)
                stage_sums(b * NG + 4, 0)
                stage_sums(b * NG + 5, 1)
                transposed(b)
            stage_sums(STEPS - 2, 0)
            stage_sums(STEPS - 1, 1)
            transposed(B - 1)

        @block.tensor
        def _(pe):
            def sums(b, g):
                s = b * NG + g
                pe.wait_ge(staged, s + 1)
                wait(pe, on_done, s - 1)
                for qt in range(QT):
                    last = pe.transpose(ps_t[g % 2][:, qt, :, :].rearrange("p j c -> p (j c)"),
                                        stage[:, g % 2, qt * P:(qt + 1) * P], id32)
                last.then_inc(t_done, 1)

            def transposes(b):
                pe.wait_ge(on_done, (b + 1) * NG)
                for qt in range(QT):
                    for c in range(DC):
                        last = pe.transpose(ps_o[qt // 2][:, c, (qt % 2) * P:(qt % 2 + 1) * P],
                                            on[:, qt, c * P:(c + 1) * P], id32)
                    if qt % 2:
                        last.then_inc(oT_done, 1)

            def project(b):
                pe.wait_ge(oT_ready, b + 1)
                for qt in range(QT):
                    wait(pe, y_used, b * 2 - 1 + qt // 2)
                    for c in range(DC):
                        last = pe.matmul(ps_y[qt // 2][:, qt % 2, :], onT[:, c, qt * P:(qt + 1) * P], wp[:, c, :],
                                         start=(c == 0), stop=(c == DC - 1))
                    if qt % 2:
                        last.then_inc(y_done, 1)
            pe.wait_ge(wp_in, 16)
            for g in range(NG):
                sums(0, g)
            transposes(0)
            for g in range(NG):
                sums(1, g)
            project(0)
            transposes(1)
            with pe.Fori(2, B) as b:
                for g in range(NG):
                    sums(b, g)
                project(b - 1)
                transposes(b)
            project(B - 1)

        @block.gpsimd
        def _(pool):
            for b in range(B - 1):
                normalise_batch(pool, per, norm, b)

        @block.vector
        def _(dve):
            def normalise(b, g):
                s = b * NG + g
                dve.wait_ge(t_done, s + 1)
                wait(dve, on_done, s - NG + 1)
                dve.reciprocal(recip[:, g, :, :], ps_t[g % 2][:, :, :, HD]).then_inc(r_done, 1)
                dve.wait_ge(r_done, s + 1)
                dve.tensor_tensor(on[:, :, g * G * HD:(g + 1) * G * HD].rearrange("p q (j d) -> p q j d", d=HD),
                                  ps_t[g % 2][:, :, :, 0:HD],
                                  recip[:, g, :, :].rearrange("p q (j o) -> p q j o", o=1)
                                  .broadcast_to([P, QT, G, HD]), ALU.mult).then_inc(on_done, 1)

            def residual(b):
                for h in range(2):
                    k = b * 2 + h
                    dve.wait_ge(y_done, k + 1)
                    for q in range(2):
                        xs = x_sb[:, ds(b * QT + 2 * h + q, 1), :].rearrange("p o d -> p (o d)")
                        last = dve.scalar_tensor_tensor(out=xs, in0=ps_y[h][:, q, :],
                                                        scalar=coef[:, ds(b * QT + 2 * h + q, 1)],
                                                        in1=xs, op0=ALU.mult, op1=ALU.add)
                    last.then_inc(y_used, 1)
                    dve.wait_ge(y_used, k + 1)
                    for q in range(2):
                        dve.bn_stats(st[:, ds(b * QT + 2 * h + q, 1), :].rearrange("p o d -> p (o d)"),
                                     x_sb[:, ds(b * QT + 2 * h + q, 1), :].rearrange("p o d -> p (o d)"))\
                           .then_inc(norm["stats_done"], 1)
            for g in range(NG):
                normalise(0, g)
            with dve.Fori(1, B) as b:
                for g in range(NG):
                    normalise(b, g)
                residual(b - 1)
            residual(B - 1)


def phase_experts(nc, a, per, norm, next_norm, xT_all, scratch, x_parts, w_parts, nselT, up, down, w32, wjunk,
                  wabs, up_in, w32_in):
    x_sb, c32, c16 = per["x"], per["c32"], per["c16"]
    id32 = c32[:, C_ID:C_ID + P]
    id16 = c16[:, B_ID:B_ID + P]
    order = list(range(E, NX)) + list(range(E))
    with ExitStack() as ctx:
        sb = lambda n, s, d: ctx.enter_context(nc.sbuf_tensor(n, s, d))
        ps = lambda n, s, d: ctx.enter_context(nc.psum_tensor(n, s, d))
        sem = lambda n: ctx.enter_context(nc.semaphore(n))
        sg, h = carve(scratch, [(2, S), (2, S)])
        lgT = sb("lgT", [P, S], F32)
        xp = x_parts.bitcast(F16).rearrange("p (c k d n) -> p c k d n", c=B, k=2, d=DC)
        shared_parts = sb("shared_parts", [P, SH * 2 * DC * P], F32)
        wp_of = lambda region: region.bitcast(F16).rearrange("p (e i k d n) -> p e i k d n", i=2, k=2, d=DC, n=P)
        shared_wp, expert_wp = wp_of(shared_parts[:, :]), wp_of(w_parts)
        wp = lambda e: expert_wp[:, e] if e < E else shared_wp[:, e - E]
        wmax = sb("wmax", [P, 4, NX, 2], F32)
        gw = sb("gw", [P, DC, HPAD], F32)
        lb = sb("lb", [P, E], F32)
        skip = sb("skip", [P, E, P], BF16)
        tri = sb("tri", [P, E, E], BF16)
        logits = sb("logits", [P, T, E], F32)
        score = sb("score", [P, T, E], F32)
        beats = sb("beats", [P, T, E, E], BF16)
        ties = sb("ties", [P, T, E, E], BF16)
        rank = sb("rank", [P, T, E], F32)
        total = sb("total", [P, 2, T], F32)
        both = sb("both", [P, 2, E, T], F32)
        sums = sb("sums", [P, 2, E], F32)
        ones = sb("ones", [P, P], F32)
        most = sb("most", [P, 3, E], F32)
        nsel = sb("nsel", [P, T, P], BF16)
        ps_g = [ps(f"ps_g{i}", [P, S], F32) for i in range(2)]
        ps_u = [ps(f"ps_u{i}", [P, S], F32) for i in range(2)]
        ps_y = [ps(f"ps_yE{i}", [P, 2, D], F32) for i in range(2)]
        ps_x = [ps(f"ps_xE{i}", [P, S], F32) for i in range(2)]
        ps_lgT = ps_y[0][:, :, :].rearrange("p a b -> p (a b)")
        ps_lg = ps_y[1][:, :, :].rearrange("p a b -> p (a b)").rearrange("p (q r) -> p q r", q=QT)
        ps_T = [x[:, :].rearrange("p (c n) -> p c n", c=DC) for x in ps_x]
        ps_n = [x[:, :].bitcast(BF16).rearrange("p (t c) -> p t c", c=P) for x in ps_x]
        ps_sum = ps_x[0][:, 0:2 * E]
        skip_in, small_in, pads = sem("skip_in"), sem("small_in"), sem("padsB")
        xT_done, kept, lgT_done, lgT_copied, lg_done = (sem("xT_doneB"), sem("kept"), sem("lgT_done"),
                                                        sem("lgT_copied"), sem("lg_done"))
        lg_copied, score_done, step_done = sem("lg_copied"), sem("score_done"), sem("step_done")
        sums_ready, sums_done, nsel_ready, nT_done = (sem("sums_ready"), sem("sums_done"), sem("nsel_ready"),
                                                      sem("nT_done"))
        nselT_ready, mean_ready, scaled = sem("nselT_ready"), sem("mean_ready"), sem("scaledB")
        gu_done, silu_done = sem("gu_done"), sem("silu_done")
        wmax_ready, wmax_all, wscale_step, wscale_ready = (sem("wmax_ready"), sem("wmax_all"), sem("wscale_step"),
                                                           sem("wscale_ready"))
        xhigh_done, xsplit, whigh_done, wsplit = sem("xhigh_done"), sem("xsplit"), sem("whigh_done"), sem("wsplit")
        halves = (slice(E, NX), slice(0, E))
        h_ready, h_used, y_used, abs_done = sem("h_ready"), sem("h_used"), sem("y_usedE"), sem("abs_done")
        block = ctx.enter_context(nc.Block())

        @block.sync
        def _(sp):
            sp.dma_start(lb[:, :], a["lb"].to_broadcast([P, E])).then_inc(small_in, 16)
            sp.dma_start(skip[:, :, :].bitcast(U16), a["skip"]).then_inc(skip_in, 16)
            sp.wait_ge(pads, 1)
            sp.dma_start(gw[:, :, 0:E], a["gate_w"]).then_inc(small_in, 16)

        @block.gpsimd
        def _(pool):
            pool.memset(gw[:, :, :], 0.0).then_inc(pads, 1)
            pool.memset(ones[:, :], 1.0).then_inc(pads, 1)

            def largest(i):
                pool.wait_ge(wmax_ready, i + 1)
                pool.partition_all_reduce(wmax[:, 1, halves[i], :].rearrange("p e i -> p (e i)"),
                                          wmax[:, 0, halves[i], :].rearrange("p e i -> p (e i)"), P,
                                          bass.bass_isa.ReduceOp.max).then_inc(wmax_all, 1)
            largest(0)
            normalise_batch(pool, per, norm, B - 1)
            largest(1)
            pool.memset(nsel[:, :, E:P], 0.0).then_inc(pads, 1)
            pool.wait_ge(mean_ready, 1)
            pool.wait_ge(up_in, 16 * (NX + 1))
            for e in range(E):
                pool.tensor_scalar(down[:, e, :], down[:, e, :], most[:, 2, e:e + 1], None, ALU.mult)\
                    .then_inc(scaled, 1)
            for b in range(B - 1):
                batch_statistics(pool, per, next_norm, b)

        @block.tensor
        def _(pe):
            def transposes(b):
                for i in range(2):
                    k = 2 * b + i
                    wait(pe, kept, k - 1)
                    for q in range(2):
                        for c in range(DC):
                            last = pe.transpose(ps_T[i][:, c, q * P:(q + 1) * P],
                                                norm["tile"](b * QT + 2 * i + q)[:, c * P:(c + 1) * P], id32)
                    last.then_inc(xT_done, 1)

            def gate_up(c, k):
                e, u = order[k], k % 2
                cols = ds(c * S, S)
                terms = [(kw, kx, d) for kw, kx in ((0, 0), (0, 1), (1, 0)) for d in range(DC)]
                for i, out in ((0, ps_g[u]), (1, ps_u[u])):
                    masked = i == 0 and e < E
                    for j, (kw, kx, d) in enumerate(terms):
                        last = pe.matmul(out[:, :], wp(e)[:, i, kw, d, :],
                                         xp[:, ds(c, 1), kx, d, :].rearrange("p o n -> p (o n)"), start=(j == 0),
                                         stop=(j == len(terms) - 1 and not masked))
                    if masked:
                        pe.matmul(out[:, :], skip[:, e, :], nselT[:, cols], start=False, stop=True)
                last.then_inc(gu_done, 1)

            def project(c, k):
                e, u = order[k], k % 2
                pe.wait_ge(h_ready, c * NX + k + 1)
                for q in range(QT):
                    last = pe.matmul(ps_y[q // 2][:, q % 2, :], h[:, u, q * P:(q + 1) * P], down[:, e, :],
                                     start=(k == 0 and q % 2 == 0), stop=(k == NX - 1), skip_group_check=True)
                last.then_inc(h_used, 1)

            for b in range(B - 1):
                pe.wait_ge(norm["normed"], b + 1)
                transposes(b)
            pe.wait_ge(xsplit, 1)
            pe.wait_ge(wsplit, 1)
            gate_up(0, 0)
            pe.wait_ge(norm["normed"], B)
            transposes(B - 1)
            pe.wait_ge(small_in, 32)
            pe.wait_ge(kept, 2 * B)
            for c in range(DC):
                for b in range(B):
                    last = pe.matmul(ps_lgT[HPAD * b:HPAD * (b + 1), :], gw[:, c, :], xT_all[:, c, b * S:(b + 1) * S],
                                     start=(c == 0), stop=(c == DC - 1))
            last.then_inc(lgT_done, 1)
            pe.wait_ge(lgT_copied, 1)
            for q in range(QT):
                last = pe.transpose(ps_lg[:, q, :], lgT[:, q * P:(q + 1) * P], id32)
            last.then_inc(lg_done, 1)
            pe.wait_ge(wsplit, 2)
            gate_up(0, 1)
            project(0, 0)
            pe.wait_ge(nsel_ready, 1)
            pe.wait_ge(pads, 3)
            for i in range(2):
                for t in range(8):
                    last = pe.transpose(ps_n[i][:, t, :], nsel[:, 8 * i + t, :], id16)
                last.then_inc(nT_done, 1)
            project(0, 1)
            pe.wait_ge(nselT_ready, 2)
            pe.wait_ge(skip_in, 16)
            pe.wait_ge(wsplit, SH + 1)
            gate_up(0, SH)
            pe.wait_ge(sums_ready, 1)
            pe.matmul(ps_sum, ones[:, :], sums[:, :, :].rearrange("p a e -> p (a e)"), start=True, stop=True)\
                .then_inc(sums_done, 1)
            for k in range(SH + 1, NX):
                pe.wait_ge(wsplit, k + 1)
                gate_up(0, k)
                pe.wait_ge(scaled, order[k - 1] + 1)
                project(0, k - 1)
            pe.wait_ge(scaled, E)
            pe.wait_ge(xsplit, B)
            gate_up(1, 0)
            project(0, NX - 1)

            def chunk(c, edge):
                for k in range(1, NX):
                    gate_up(c, k)
                    project(c, k - 1)
                if not edge:
                    gate_up(c + 1, 0)
                project(c, NX - 1)
            with pe.Fori(1, B - 1) as c:
                chunk(c, False)
            chunk(B - 1, True)

        @block.scalar
        def _(act):
            def keep(k):
                act.wait_ge(xT_done, k + 1)
                act.copy(xT_all[:, :, k * 2 * P:(k + 1) * 2 * P], ps_T[k % 2]).then_inc(kept, 1)

            def high_x(c):
                act.wait_ge(kept, 2 * c + 2)
                if c == 1:
                    act.wait_ge(xT_done, 2 * B)
                act.activation(xp[:, c, 0], xT_all[:, :, c * S:(c + 1) * S], ACT.Copy, scale=XS)\
                   .then_inc(xhigh_done, 1)

            def high_w(k):
                e = order[k]
                act.wait_ge(wscale_ready, 1 + int(e < E))
                for i in range(2):
                    last = act.activation(wp(e)[:, i, 0], up[:, e, i, :, :], ACT.Copy, scale=wmax[:, 2, e, i:i + 1])
                last.then_inc(whigh_done, 1)

            def silu(c, k):
                act.wait_ge(gu_done, c * NX + k + 1)
                act.activation(sg[:, k % 2, :], ps_g[k % 2][:, :], ACT.Silu, scale=wmax[:, 3, order[k], 0:1])\
                   .then_inc(silu_done, 1)
            for k in range(2):
                keep(k)
            high_x(0)
            high_w(0)
            for k in range(2, 2 * B - 2):
                keep(k)
            high_w(1)
            for k in range(2 * B - 2, 2 * B):
                keep(k)
            for k in range(SH, SH + 3):
                high_w(k)
            act.wait_ge(lg_copied, 1)
            act.activation(score[:, :, :], logits[:, :, :], ACT.Sigmoid).then_inc(score_done, 1)
            for k in range(NX):
                silu(0, k)
                if SH <= k + 3 < NX and k + 3 >= SH + 3:
                    high_w(k + 3)
                if SH <= k < SH + B - 1:
                    high_x(k - SH + 1)
            with act.Fori(1, B - 1) as c:
                for k in range(NX):
                    silu(c, k)
            act.wait_ge(w32_in, 16 * 3)
            for k in range(NX):
                silu(B - 1, k)
                if 1 <= k <= 3:
                    wait(act, abs_done, k - 1)
                    act.activation(wjunk, w32[:, k - 1, :], ACT.Abs, accum_out=wabs[:, k - 1:k]).then_inc(abs_done, 1)

        @block.vector
        def _(dve):
            def hidden(c, k, edge):
                dve.wait_ge(silu_done, c * NX + k + 1)
                if not edge:
                    dve.wait_ge(h_used, c * NX + k - 1)
                dve.scalar_tensor_tensor(out=h[:, k % 2, :], in0=ps_u[k % 2][:, :], scalar=wmax[:, 3, order[k], 1:2],
                                         in1=sg[:, k % 2, :], op0=ALU.mult, op1=ALU.mult).then_inc(h_ready, 1)

            def weight_maxima(i):
                dve.tensor_reduce(wmax[:, 0, halves[i], :],
                                  up[:, halves[i], :, :, :].rearrange("p e i d n -> p e i (d n)"), AX_X, ALU.max,
                                  apply_absolute_value=True).then_inc(wmax_ready, 1)

            def weight_scales(i):
                own = lambda row: wmax[:, row, halves[i], :]
                dve.wait_ge(wmax_all, i + 1)
                dve.tensor_scalar(own(1), own(1), 1e-20, None, ALU.max).then_inc(wscale_step, 1)
                dve.wait_ge(wscale_step, 2 * i + 1)
                dve.tensor_scalar(own(3), own(1), 1.0 / (WS * XS), None, ALU.mult)
                dve.reciprocal(own(2), own(1)).then_inc(wscale_step, 1)
                dve.wait_ge(wscale_step, 2 * i + 2)
                dve.tensor_scalar(own(2), own(2), WS, None, ALU.mult).then_inc(wscale_ready, 1)
                dve.wait_ge(wscale_ready, i + 1)

            def low_w(k):
                e = order[k]
                dve.wait_ge(whigh_done, k + 1)
                for i in range(2):
                    last = dve.scalar_tensor_tensor(out=wp(e)[:, i, 1], in0=up[:, e, i, :, :],
                                                    scalar=wmax[:, 2, e, i:i + 1], in1=wp(e)[:, i, 0],
                                                    op0=ALU.mult, op1=ALU.subtract)
                last.then_inc(wsplit, 1)

            def low_x(c):
                dve.wait_ge(xhigh_done, c + 1)
                dve.scalar_tensor_tensor(out=xp[:, c, 1], in0=xT_all[:, :, c * S:(c + 1) * S], scalar=XS,
                                         in1=xp[:, c, 0], op0=ALU.mult, op1=ALU.subtract).then_inc(xsplit, 1)

            def residual(c):
                dve.wait_ge(h_used, (c + 1) * NX)
                for i in range(2):
                    xs = x_sb[:, ds(c * QT + 2 * i, 2), :]
                    dve.scalar_tensor_tensor(out=xs, in0=ps_y[i][:, :, :], scalar=per["gates"][:, 2:3], in1=xs,
                                             op0=ALU.mult, op1=ALU.add).then_inc(y_used, 1)
                dve.wait_ge(y_used, 2 * c + 2)
                for i in range(QT):
                    dve.bn_stats(per["st"][:, ds(c * QT + i, 1), :].rearrange("p o d -> p (o d)"),
                                 x_sb[:, ds(c * QT + i, 1), :].rearrange("p o d -> p (o d)"))\
                       .then_inc(next_norm["stats_done"], 1)

            count = [0]

            def link(ins):
                count[0] += 1
                ins.then_inc(step_done, 1)
                dve.wait_ge(step_done, count[0])
            dve.wait_ge(up_in, 16 * (NX + 1))
            weight_maxima(0)
            weight_scales(0)
            low_x(0)
            low_w(0)
            weight_maxima(1)
            low_w(1)
            weight_scales(1)
            dve.tensor_copy(tri[:, :, :], c32[:, C_TRI:C_TRI + E * E].rearrange("p (e f) -> p e f", f=E))
            dve.wait_ge(small_in, 32)
            dve.wait_ge(lgT_done, 1)
            dve.tensor_copy(lgT[:, :], ps_lgT).then_inc(lgT_copied, 1)
            dve.wait_ge(lg_done, 1)
            for b in range(B):
                last = dve.tensor_tensor(logits[:, b * QT:(b + 1) * QT, :], ps_lg[:, :, HPAD * b:HPAD * b + E],
                                         lb[:, :].rearrange("p (o e) -> p o e", o=1).broadcast_to([P, QT, E]), ALU.add)
            last.then_inc(lg_copied, 1)
            dve.wait_ge(score_done, 1)
            other = score[:, :, :].rearrange("p t (o f) -> p t o f", o=1).broadcast_to([P, T, E, E])
            own = score[:, :, :].rearrange("p t (e o) -> p t e o", o=1).broadcast_to([P, T, E, E])
            before = tri[:, :, :].rearrange("p (o e) f -> p o e f", o=1).broadcast_to([P, T, E, E])
            dve.tensor_tensor(beats[:, :, :, :], other, own, ALU.is_gt)
            link(dve.tensor_tensor(ties[:, :, :, :], other, own, ALU.is_equal))
            link(dve.tensor_tensor(ties[:, :, :, :], ties[:, :, :, :], before, ALU.mult))
            link(dve.tensor_tensor(beats[:, :, :, :], beats[:, :, :, :], ties[:, :, :, :], ALU.add))
            hidden(0, 0, True)
            low_w(SH)
            link(dve.tensor_reduce(rank[:, :, :], beats[:, :, :, :], AX_X, ALU.add))
            dve.tensor_scalar(nsel[:, :, 0:E], rank[:, :, :], 1.5, None, ALU.is_gt).then_inc(nsel_ready, 1)
            chosen = both[:, 1, :, :].rearrange("p e t -> p t e")
            weight = both[:, 0, :, :].rearrange("p e t -> p t e")
            link(dve.tensor_scalar(chosen, rank[:, :, :], 1.5, None, ALU.is_lt))
            link(dve.tensor_tensor(weight, score[:, :, :], chosen, ALU.mult))
            link(dve.tensor_reduce(total[:, 0, :], weight, AX_X, ALU.add))
            link(dve.tensor_scalar(total[:, 1, :], total[:, 0, :], 1e-8, None, ALU.add))
            hidden(0, 1, True)
            for i in range(2):
                dve.wait_ge(nT_done, i + 1)
                dve.tensor_copy(nselT[:, i * 8 * P:(i + 1) * 8 * P].rearrange("p (t c) -> p t c", c=P), ps_n[i])\
                   .then_inc(nselT_ready, 1)
            link(dve.reciprocal(total[:, 0, :], total[:, 1, :]))
            link(dve.tensor_tensor(both[:, 0, :, :], both[:, 0, :, :],
                                   total[:, 0, :].rearrange("p (o t) -> p o t", o=1).broadcast_to([P, E, T]),
                                   ALU.mult))
            dve.tensor_reduce(sums[:, :, :], both[:, :, :, :], AX_X, ALU.add).then_inc(sums_ready, 1)
            low_w(SH + 1)
            hidden(0, SH, False)
            low_w(SH + 2)
            dve.wait_ge(sums_done, 1)
            link(dve.tensor_scalar(most[:, 0, :], ps_sum[:, E:2 * E], 1.0, None, ALU.max))
            link(dve.reciprocal(most[:, 1, :], most[:, 0, :]))
            dve.tensor_tensor(most[:, 2, :], ps_sum[:, 0:E], most[:, 1, :], ALU.mult).then_inc(mean_ready, 1)
            for k in range(SH + 1, NX):
                if k + 2 < NX:
                    low_w(k + 2)
                if k - SH < B:
                    low_x(k - SH)
                hidden(0, k, False)
            with dve.Fori(1, B) as c:
                residual(c - 1)
                for k in range(NX):
                    hidden(c, k, False)
            residual(B - 1)


def phase_coattend(nc, a, per, norm, ffn, free, ctok, ctxT, wqv, w32, wabs, wq16, wstat, ctx_in):
    x_sb, c32 = per["x"], per["c32"]
    id32 = c32[:, C_ID:C_ID + P]
    with ExitStack() as ctx:
        sb = lambda n, s, d: ctx.enter_context(nc.sbuf_tensor(n, s, d))
        ps = lambda n, s, d: ctx.enter_context(nc.psum_tensor(n, s, d))
        sem = lambda n: ctx.enter_context(nc.semaphore(n))
        wsim = sb("wsim", [P, 2, DC], F32)
        w1 = sb("w1", [P, D], F32)
        bsim = sb("bsim", [P, 1], F32)
        bqv = sb("bqv", [P, D], F32)
        e, eT, sT, junk, att, attT = carve(free, [(2, QT, D), (2, DC, S), (DC, S), (QT, D), (QT, S), (2, QT, P)])
        hqT = sb("hqT", [P, 2, DC, S], F32)
        ehT = sb("ehT", [P, 2, DC, S], F32)
        hq = sb("hq", [P, 2, D], F32)
        wx = sb("wx", [P, DC, D], F32)
        yb = sb("ybC", [P, 2, D], F32)
        nmax = sb("nmax", [P, QT], F32)
        lsum = sb("lsum", [P, QT], F32)
        lrec = sb("lrec", [P, QT], F32)
        own = sb("own", [P, QT], F32)
        z = sb("z", [P, 3, QT], F32)
        nz = sb("nz", [P, 1], F32)
        ez = sb("ez", [P, QT], F32)
        ezs = sb("ezs", [P, 1], F32)
        rz = sb("rz", [P, 1], F32)
        hc = sb("hc", [P, DC], F32)
        ones = sb("onesC", [P, P], F32)
        less_mean, rstd = norm["tmp"][:, 4, :], norm["tmp"][:, 8, :]
        ps_T = [ps(f"ps_TC{i}", [P, DC, 2 * P], F32) for i in range(2)]
        ps_S = [ps(f"ps_SC{i}", [P, S], F32) for i in range(2)]
        ps_A = ps("ps_A", [P, QT, P], F32)
        ps_q = ps("ps_q", [P, D], F32)
        ps_qT = ps("ps_qT", [P, DC, P], F32)
        ps_h = ps("ps_h", [P, 8], F32)
        w_in = sem("w_inC")
        e_ready, eT_done, eT_ready, sT_ready = sem("e_readyC"), sem("eT_done"), sem("eT_ready"), sem("sT_ready")
        S_done, max_ready, exp_done = sem("S_doneC"), sem("max_readyC"), sem("exp_doneC")
        own_done, z_half, z_ready, zmax_ready, nz_ready = (sem("own_done"), sem("z_half"), sem("z_ready"),
                                                           sem("zmax_ready"), sem("nz_ready"))
        ez_ready, hc_done, hc_step, wx_ready = sem("ez_ready"), sem("hc_done"), sem("hc_step"), sem("wx_ready")
        attT_done, attT_ready, q_done, q_ready = sem("attT_done"), sem("attT_ready"), sem("q_done"), sem("q_ready")
        l_ready = sem("l_ready")
        qT_done, qT_ready, eh_ready = sem("qT_done"), sem("qT_ready"), sem("eh_ready")
        out_done, biased, out_used = sem("out_doneC"), sem("biasedC"), sem("out_usedC")
        ones_ready, wsum_done, wstat_step, quant = sem("ones_ready"), sem("wsum_done"), sem("wstat_step"), sem("quant")
        block = ctx.enter_context(nc.Block())

        @block.sync
        def _(sp):
            sp.dma_start(wsim[:, :, :], a["wsim"]).then_inc(w_in, 16)
            sp.dma_start(w1[:, :], a["w1"].to_broadcast([P, D])).then_inc(w_in, 16)
            sp.dma_start(bsim[:, :], a["bsim"].to_broadcast([P, 1])).then_inc(w_in, 16)
            sp.dma_start(bqv[:, :], a["bqv"].to_broadcast([P, D])).then_inc(w_in, 16)

        def batches(eng, batch):
            batch(0, 0, False, False)
            with eng.Fori(0, (B - 2) // 2) as pair:
                for v in range(2):
                    batch(2 * pair + v + 1, (v + 1) % 2, True, False)
            batch(B - 1, (B - 1) % 2, True, True)

        @block.tensor
        def _(pe):
            def transposes(b, v):
                for i in range(2):
                    pe.wait_ge(e_ready, b * QT + 2 * i + 2)
                    for q in range(2):
                        for c in range(DC):
                            last = pe.transpose(ps_T[i][:, c, q * P:(q + 1) * P],
                                                e[:, v, 2 * i + q, c * P:(c + 1) * P], id32)
                    last.then_inc(eT_done, 1)

            def similarity(b, q):
                n = b * QT + q
                if q == 0:
                    pe.wait_ge(sT_ready, b + 1)
                if q > 1:
                    pe.wait_ge(exp_done, n - 1)
                for c in range(DC):
                    last = pe.matmul(ps_S[q % 2][:, :], sT[:, c, q * P:(q + 1) * P], ctxT[:, c, ds(b * S, S)],
                                     start=(c == 0), stop=(c == DC - 1))
                last.then_inc(S_done, 1)

            def attended(b, q):
                n = b * QT + q
                pe.wait_ge(exp_done, n + 1)
                if q:
                    pe.wait_ge(attT_ready, n)
                for k in range(QT):
                    last = pe.transpose(ps_A[:, k, :], att[:, q, k * P:(k + 1) * P], id32)
                last.then_inc(attT_done, 1)

            def context(b, q):
                n = b * QT + q
                pe.wait_ge(attT_ready, n + 1)
                wait(pe, q_ready, n)
                for k in range(QT):
                    last = pe.matmul(ps_q[:, :], attT[:, q % 2, k, :], ctok[:, ds(b * QT + k, 1), :],
                                     start=(k == 0), stop=(k == QT - 1))
                last.then_inc(q_done, 1)

            def context_transposes(b, q):
                n = b * QT + q
                pe.wait_ge(q_ready, n + 1)
                wait(pe, qT_ready, n)
                for c in range(DC):
                    last = pe.transpose(ps_qT[:, c, :], hq[:, q % 2, c * P:(c + 1) * P], id32)
                last.then_inc(qT_done, 1)

            def pooled(b, v):
                pe.wait_ge(ez_ready, b + 1)
                pe.matmul(ps_h[:, 2:3], ones[:, :], ezs[:, :], start=True, stop=True)
                for c in range(DC):
                    for q in range(QT):
                        last = pe.matmul(ps_h[:, c:c + 1], e[:, v, q, c * P:(c + 1) * P], ez[:, q:q + 1],
                                         start=(q == 0), stop=(q == QT - 1))
                last.then_inc(hc_done, 1)

            def features(b, v, q):
                n = b * QT + q
                if q == 0:
                    pe.wait_ge(wx_ready, b + 1)
                pe.wait_ge(eh_ready, n + 1)
                wait(pe, out_used, n - 1)
                cols = slice(q * P, (q + 1) * P)
                terms = [(eT[:, v, c, cols], wx[:, c, :]) for c in range(DC)]
                terms += [(hqT[:, v, c, cols], wqv[:, 1, c, :]) for c in range(DC)]
                terms += [(ehT[:, v, c, cols], wqv[:, 2, c, :]) for c in range(DC)]
                for i, (l, r) in enumerate(terms):
                    last = pe.matmul(ps_T[q % 2][:, 0, :], l, r, start=(i == 0), stop=(i == len(terms) - 1))
                last.then_inc(out_done, 1)

            def batch(b, v, before, last):
                feature = lambda q: features(b - 1, 1 - v, q) if before else None
                transposes(b, v)
                if before:
                    pe.wait_ge(eT_ready, 2 * b + 1)
                feature(0)
                for q in range(QT):
                    similarity(b, q)
                attended(b, 0)
                feature(1)
                attended(b, 1)
                context(b, 0)
                attended(b, 2)
                context(b, 1)
                context_transposes(b, 0)
                attended(b, 3)
                context(b, 2)
                context_transposes(b, 1)
                feature(2)
                context(b, 3)
                context_transposes(b, 2)
                feature(3)
                pooled(b, v)
                context_transposes(b, 3)

            pe.wait_ge(w_in, 16 * 4)
            pe.wait_ge(ctx_in, 16 * 3)
            pe.wait_ge(ones_ready, 1)
            pe.matmul(ps_h[:, 4:7], ones[:, :], wabs[:, :], start=True, stop=True).then_inc(wsum_done, 1)
            pe.wait_ge(wstat_step, 1)
            batches(pe, batch)
            for q in range(QT):
                features(B - 1, (B - 1) % 2, q)

        @block.vector
        def _(dve):
            def normalise(b, v):
                for q in range(QT):
                    n = b * QT + q
                    dve.tensor_scalar(e[:, v, q, :], x_sb[:, ds(n, 1), :].rearrange("p o d -> p (o d)"),
                                      less_mean[:, ds(n, 1)], rstd[:, ds(n, 1)], ALU.add, ALU.mult)\
                       .then_inc(e_ready, 1)

            def transposed(b, v):
                for i in range(2):
                    dve.wait_ge(eT_done, b * 2 + i + 1)
                    dve.tensor_copy(eT[:, v, :, i * 2 * P:(i + 1) * 2 * P], ps_T[i][:, :, :]).then_inc(eT_ready, 1)
                dve.wait_ge(eT_ready, 2 * b + 2)
                for c in range(DC):
                    last = dve.tensor_scalar(sT[:, c, :], eT[:, v, c, :], wsim[:, 1, c:c + 1],
                                             wsim[:, 0, c:c + 1], ALU.mult, ALU.add)
                last.then_inc(sT_ready, 1)

            def maximum(b, q):
                dve.wait_ge(S_done, b * QT + q + 1)
                dve.tensor_reduce(nmax[:, q:q + 1], ps_S[q % 2][:, :], AX_X, ALU.max, negate=True)\
                   .then_inc(max_ready, 1)

            def own_part(b, v):
                for q in range(QT):
                    last = dve.tensor_tensor_reduce(out=junk[:, q, :], in0=e[:, v, q, :], in1=w1[:, :], scale=1.0,
                                                    scalar=0.0, op0=ALU.mult, op1=ALU.add,
                                                    accum_out=own[:, q:q + 1])
                last.then_inc(own_done, 1)

            def sim_maxima(b):
                dve.wait_ge(max_ready, (b + 1) * QT)
                dve.wait_ge(own_done, b + 1)
                dve.tensor_tensor(z[:, 0, :], own[:, :], nmax[:, :], ALU.subtract).then_inc(z_half, 1)
                dve.wait_ge(z_half, b + 1)
                dve.tensor_scalar(z[:, 1, :], z[:, 0, :], bsim[:, 0:1], None, ALU.add).then_inc(z_ready, 1)

            def sum_inverses(b):
                dve.wait_ge(exp_done, (b + 1) * QT)
                dve.reciprocal(lrec[:, :], lsum[:, :]).then_inc(l_ready, 1)
                dve.wait_ge(l_ready, b + 1)

            def batch_maximum(b):
                dve.wait_ge(zmax_ready, b + 1)
                dve.tensor_reduce(nz[:, :], z[:, 2, :], AX_X, ALU.max, negate=True).then_inc(nz_ready, 1)

            def context(b, q):
                dve.wait_ge(q_done, b * QT + q + 1)
                dve.tensor_scalar(hq[:, q % 2, :], ps_q[:, :], lrec[:, q:q + 1], None, ALU.mult).then_inc(q_ready, 1)

            def context_transposed(b, v, q):
                dve.wait_ge(qT_done, b * QT + q + 1)
                dve.tensor_copy(hqT[:, v, :, q * P:(q + 1) * P], ps_qT[:, :, :]).then_inc(qT_ready, 1)

            def pooled_weights(b):
                dve.wait_ge(hc_done, b + 1)
                dve.reciprocal(rz[:, :], ps_h[:, 2:3]).then_inc(hc_step, 1)
                dve.wait_ge(hc_step, b * 2 + 1)
                dve.tensor_scalar(hc[:, :], ps_h[:, 0:2], rz[:, 0:1], None, ALU.mult).then_inc(hc_step, 1)
                dve.wait_ge(hc_step, b * 2 + 2)
                for c in range(DC):
                    last = dve.scalar_tensor_tensor(out=wx[:, c, :], in0=wqv[:, 3, c, :], scalar=hc[:, c:c + 1],
                                                    in1=wqv[:, 0, c, :], op0=ALU.mult, op1=ALU.add)
                last.then_inc(wx_ready, 1)

            def residual(b, q):
                n = b * QT + q
                dve.wait_ge(out_done, n + 1)
                dve.tensor_tensor(yb[:, q % 2, :], ps_T[q % 2][:, 0, :], bqv[:, :], ALU.add).then_inc(biased, 1)
                dve.wait_ge(biased, n + 1)
                xs = x_sb[:, ds(n, 1), :].rearrange("p o d -> p (o d)")
                dve.scalar_tensor_tensor(out=xs, in0=yb[:, q % 2, :], scalar=per["gates"][:, 1:2], in1=xs,
                                         op0=ALU.mult, op1=ALU.add).then_inc(out_used, 1)
                dve.wait_ge(out_used, n + 1)
                dve.bn_stats(per["st"][:, ds(n, 1), :].rearrange("p o d -> p (o d)"), xs)\
                   .then_inc(ffn["stats_done"], 1)

            def batch(b, v, before, last):
                updated = lambda q: residual(b - 1, q) if before else None
                transposed(b, v)
                own_part(b, v)
                maximum(b, 0)
                updated(0)
                for q in range(1, QT):
                    maximum(b, q)
                sim_maxima(b)
                sum_inverses(b)
                updated(1)
                context(b, 0)
                context(b, 1)
                batch_maximum(b)
                context_transposed(b, v, 0)
                context(b, 2)
                context_transposed(b, v, 1)
                updated(2)
                context(b, 3)
                context_transposed(b, v, 2)
                updated(3)
                if not last:
                    normalise(b + 1, 1 - v)
                pooled_weights(b)
                context_transposed(b, v, 3)
            dve.wait_ge(norm["steps"], 5)
            normalise(0, 0)
            dve.wait_ge(w_in, 16 * 4)
            dve.wait_ge(ctx_in, 16 * 3)
            dve.wait_ge(wsum_done, 1)
            dve.tensor_scalar(wstat[:, 0:3], ps_h[:, 4:7], 1.0 / (D * INNER), 1e-5, ALU.mult, ALU.max)\
               .then_inc(wstat_step, 1)
            dve.wait_ge(wstat_step, 1)
            dve.reciprocal(wstat[:, 3:6], wstat[:, 0:3]).then_inc(wstat_step, 1)
            dve.wait_ge(norm["steps"], 5 * B)
            batches(dve, batch)
            for q in range(QT):
                residual(B - 1, q)

        @block.scalar
        def _(act):
            with act.Fori(0, B) as b:
                for q in range(QT):
                    n = b * QT + q
                    act.wait_ge(max_ready, n + 1)
                    act.activation(att[:, q, :], ps_S[q % 2][:, :], ACT.Exp, bias=nmax[:, q:q + 1],
                                   accum_out=lsum[:, q:q + 1]).then_inc(exp_done, 1)
                for q in range(QT):
                    n = b * QT + q
                    act.wait_ge(attT_done, n + 1)
                    if q > 1:
                        act.wait_ge(q_done, n - 1)
                    act.copy(attT[:, q % 2, :, :], ps_A[:, :, :]).then_inc(attT_ready, 1)
                act.wait_ge(nz_ready, b + 1)
                act.activation(ez[:, :], z[:, 1, :], ACT.Exp, bias=nz[:, 0:1], accum_out=ezs[:, 0:1])\
                   .then_inc(ez_ready, 1)

        @block.gpsimd
        def _(pool):
            pool.memset(ones[:, :], 1.0).then_inc(ones_ready, 1)
            batch_statistics(pool, per, norm, B - 1)

            def quantise_weights(i):
                pool.tensor_scalar(w32[:, i, :], w32[:, i, :], wstat[:, 3 + i:4 + i], MAGIC, ALU.mult, ALU.add)\
                    .then_inc(quant, 1)
                pool.wait_ge(quant, 3 * i + 1)
                pool.tensor_scalar(w32[:, i, :], w32[:, i, :], MAGIC + 1.0, MAGIC - 1.0, ALU.min, ALU.max)\
                    .then_inc(quant, 1)
                pool.wait_ge(quant, 3 * i + 2)
                pool.tensor_scalar(wq16[:, i, :], w32[:, i, :], 1.0, -MAGIC, ALU.mult, ALU.add).then_inc(quant, 1)
            for b in range(B):
                pool.wait_ge(z_ready, b + 1)
                pool.partition_all_reduce(z[:, 2, :], z[:, 1, :], P, bass.bass_isa.ReduceOp.max)\
                    .then_inc(zmax_ready, 1)
                for q in range(QT):
                    pool.wait_ge(qT_ready, b * QT + q + 1)
                    cols = slice(q * P, (q + 1) * P)
                    pool.tensor_tensor(ehT[:, b % 2, :, cols], eT[:, b % 2, :, cols], hqT[:, b % 2, :, cols],
                                       ALU.mult).then_inc(eh_ready, 1)
                if b:
                    normalise_batch(pool, per, ffn, b - 1)
                if b == 0:
                    pool.wait_ge(wstat_step, 2)
                if b < 3:
                    quantise_weights(b)


def phase_bitffn(nc, per, ffn, xn, free, wq16, wstat, out):
    x_sb, c16 = per["x"], per["c16"]
    id16 = c16[:, B_ID:B_ID + P]
    wg, wu = (wq16[:, i, :].rearrange("p (c n) -> p c n", c=DC) for i in range(2))
    wd = wq16[:, 2, :].rearrange("p (c n) -> p c n", c=IC)
    with ExitStack() as ctx:
        sb = lambda n, s, d: ctx.enter_context(nc.sbuf_tensor(n, s, d))
        ps = lambda n, s, d: ctx.enter_context(nc.psum_tensor(n, s, d))
        sem = lambda n: ctx.enter_context(nc.semaphore(n))
        sg, t, r = carve(free, [(2, INNER), (2, INNER), (2, INNER)])
        amax = sb("amax", [P, 6, T], F32)
        gd = sb("gd", [P, 2], F32)
        xr = sb("xr", [P, 2, D], F32)
        xq = sb("xq", [P, 2, D], BF16)
        xqT = sb("xqT", [P, 2, DC, P], BF16)
        hq = sb("hqD", [P, 2, INNER], BF16)
        hqT = sb("hqTD", [P, 2, IC, P], BF16)
        hs = sb("hs", [P, 2, 4], F32)
        yg = sb("yg", [P, 2, D], F32)
        ys = sb("ys", [P, T], F32)
        ps_x = ps("ps_x", [P, DC, P], BF16)
        ps_g = ps("ps_gD", [P, INNER], F32)
        ps_u = ps("ps_uD", [P, INNER], F32)
        ps_h = ps("ps_hD", [P, IC, P], BF16)
        ps_y = [ps(f"ps_yD{i}", [P, D], F32) for i in range(2)]
        scale_step, scales_ready, added, ys_ready = (sem("scale_step"), sem("scales_ready"), sem("added"),
                                                      sem("ys_ready"))
        xr_done, xq_ready, xT_done, xT_ready = sem("xr_done"), sem("xq_readyD"), sem("xT_doneD"), sem("xT_readyD")
        gate_done, up_done, silu_done, t_ready = sem("gate_done"), sem("up_done"), sem("silu_doneD"), sem("t_ready")
        hstep, f_ready, r_ready, hq_ready = sem("hstep"), sem("f_ready"), sem("r_ready"), sem("hq_readyD")
        hT_done, hT_ready, y_done, y_used, stored = (sem("hT_done"), sem("hT_readyD"), sem("y_doneD"), sem("y_usedD"),
                                                     sem("stored"))
        block = ctx.enter_context(nc.Block())
        ABS, AMAX, INV, SX, AG, AU = range(6)

        @block.sync
        def _(sp):
            ov = out.rearrange("b (q p) d -> p (b q) d", p=P)
            with sp.Fori(0, T) as n:
                sp.wait_ge(added, n + 1)
                sp.dma_start(ov[:, ds(n, 1), :], x_sb[:, ds(n, 1), :]).then_inc(stored, 16)
            sp.wait_ge(stored, 16 * T)

        @block.gpsimd
        def _(pool):
            def quantise(n, u):
                if n % QT == 0:
                    pool.wait_ge(scales_ready, n // QT + 1)
                pool.tensor_scalar(xr[:, u, :], xn[:, n, :], amax[:, SX, n:n + 1], MAGIC, ALU.mult, ALU.add)\
                    .then_inc(xr_done, 1)
                pool.wait_ge(xr_done, n + 1)
                wait(pool, xT_done, n - 1)
                pool.tensor_scalar(xq[:, u, :], xr[:, u, :], 1.0, -MAGIC, ALU.mult, ALU.add).then_inc(xq_ready, 1)

            def rounded(n, u):
                pool.wait_ge(f_ready, n + 1)
                pool.tensor_scalar(r[:, u, :], t[:, u, :], hs[:, u, 3:4], MAGIC, ALU.mult, ALU.add).then_inc(r_ready, 1)
                pool.wait_ge(r_ready, n + 1)
                wait(pool, hT_done, n - 1)
                pool.tensor_scalar(hq[:, u, :], r[:, u, :], 1.0, -MAGIC, ALU.mult, ALU.add).then_inc(hq_ready, 1)

            def residual(n, u):
                pool.wait_ge(y_used, n + 1)
                pool.tensor_tensor(x_sb[:, n, :], x_sb[:, n, :], yg[:, u, :], ALU.add).then_inc(added, 1)
            quantise(0, 0)
            quantise(1, 1)
            normalise_batch(pool, per, ffn, B - 1)
            for n in range(T + 3):
                if live(n + 2):
                    quantise(n + 2, n % 2)
                if live(n - 1):
                    rounded(n - 1, 1 - n % 2)
                if live(n - 3):
                    residual(n - 3, 1 - n % 2)

        @block.vector
        def _(dve):
            def scales(b):
                own = slice(b * QT, (b + 1) * QT)
                dve.wait_ge(ffn["normed"], b + 1)
                dve.tensor_reduce(amax[:, ABS, own], xn[:, own, :], AX_X, ALU.max, apply_absolute_value=True)\
                   .then_inc(scale_step, 1)
                dve.wait_ge(scale_step, 3 * b + 1)
                dve.tensor_scalar(amax[:, AMAX, own], amax[:, ABS, own], 1e-5, None, ALU.max).then_inc(scale_step, 1)
                dve.wait_ge(scale_step, 3 * b + 2)
                dve.reciprocal(amax[:, INV, own], amax[:, AMAX, own])
                dve.tensor_scalar(amax[:, AG, own], amax[:, AMAX, own], wstat[:, 0:1], 1.0 / 127.0, ALU.mult, ALU.mult)
                dve.tensor_scalar(amax[:, AU, own], amax[:, AMAX, own], wstat[:, 1:2], 1.0 / 127.0, ALU.mult, ALU.mult)\
                   .then_inc(scale_step, 1)
                dve.wait_ge(scale_step, 3 * b + 3)
                dve.tensor_scalar(amax[:, SX, own], amax[:, INV, own], 127.0, None, ALU.mult).then_inc(scales_ready, 1)

            def transposed(n, u):
                dve.wait_ge(xT_done, n + 1)
                wait(dve, up_done, n - 1)
                dve.tensor_copy(xqT[:, u, :, :], ps_x[:, :, :]).then_inc(xT_ready, 1)

            def hidden(n, u):
                dve.wait_ge(up_done, n + 1)
                dve.wait_ge(silu_done, n + 1)
                wait(dve, r_ready, n - 1)
                dve.tensor_tensor(t[:, u, :], sg[:, u, :], ps_u[:, :], ALU.mult).then_inc(t_ready, 1)
                dve.wait_ge(t_ready, n + 1)
                dve.tensor_reduce(hs[:, u, 0:1], t[:, u, :], AX_X, ALU.max, apply_absolute_value=True)\
                   .then_inc(hstep, 1)
                dve.wait_ge(hstep, 3 * n + 1)
                dve.tensor_scalar(hs[:, u, 1:2], hs[:, u, 0:1], amax[:, AU, ds(n, 1)], 1e-5, ALU.mult, ALU.max)\
                   .then_inc(hstep, 1)
                dve.wait_ge(hstep, 3 * n + 2)
                dve.reciprocal(hs[:, u, 2:3], hs[:, u, 1:2]).then_inc(hstep, 1)
                dve.wait_ge(hstep, 3 * n + 3)
                dve.tensor_scalar(hs[:, u, 3:4], hs[:, u, 2:3], amax[:, AU, ds(n, 1)], 127.0, ALU.mult, ALU.mult)\
                   .then_inc(f_ready, 1)
                dve.tensor_scalar(ys[:, ds(n, 1)], hs[:, u, 1:2], gd[:, 0:1], None, ALU.mult).then_inc(ys_ready, 1)

            def step(n, u):
                if live(n + 1):
                    transposed(n + 1, 1 - u)
                if live(n):
                    hidden(n, u)
                if isinstance(n, int) and 0 <= n < B - 1:
                    scales(n + 1)
            dve.tensor_scalar(gd[:, 0:1], wstat[:, 2:3], per["gates"][:, 3:4], 1.0 / 127.0, ALU.mult, ALU.mult)
            scales(0)
            transposed(0, 0)
            schedule(dve, step)

        @block.scalar
        def _(act):
            def silu(n, u):
                act.wait_ge(gate_done, n + 1)
                wait(act, t_ready, n - 1)
                act.activation(sg[:, u, :], ps_g[:, :], ACT.Silu, scale=amax[:, AG, ds(n, 1)]).then_inc(silu_done, 1)

            def transposed(n, u):
                act.wait_ge(hT_done, n + 1)
                wait(act, y_done, n - 1)
                act.copy(hqT[:, u, :, :], ps_h[:, :, :]).then_inc(hT_ready, 1)

            def scaled(n, u):
                act.wait_ge(y_done, n + 1)
                act.wait_ge(ys_ready, n + 1)
                wait(act, added, n - 1)
                act.activation(yg[:, u, :], ps_y[u][:, :], ACT.Copy, scale=ys[:, ds(n, 1)]).then_inc(y_used, 1)

            def step(n, u):
                if live(n):
                    silu(n, u)
                if live(n - 3):
                    scaled(n - 3, 1 - u)
                if live(n - 2):
                    transposed(n - 2, u)
            schedule(act, step)

        @block.tensor
        def _(pe):
            def x_transposes(n, u):
                pe.wait_ge(xq_ready, n + 1)
                wait(pe, xT_ready, n)
                for c in range(DC):
                    last = pe.transpose(ps_x[:, c, :], xq[:, u, c * P:(c + 1) * P], id16)
                last.then_inc(xT_done, 1)

            def gate_up(n, u):
                pe.wait_ge(xT_ready, n + 1)
                for out_, w, used, done in ((ps_g, wg, silu_done, gate_done), (ps_u, wu, t_ready, up_done)):
                    wait(pe, used, n)
                    for half in range(2):
                        cols = slice(half * 512, half * 512 + 512)
                        for c in range(DC):
                            last = pe.matmul(out_[:, cols], xqT[:, u, c, :], w[:, c, cols], start=(c == 0),
                                             stop=(c == DC - 1))
                    last.then_inc(done, 1)

            def h_transposes(n, u):
                pe.wait_ge(hq_ready, n + 1)
                wait(pe, hT_ready, n)
                for c in range(IC):
                    last = pe.transpose(ps_h[:, c, :], hq[:, u, c * P:(c + 1) * P], id16)
                last.then_inc(hT_done, 1)

            def down(n, u):
                pe.wait_ge(hT_ready, n + 1)
                wait(pe, y_used, n - 1)
                for c in range(IC):
                    last = pe.matmul(ps_y[u][:, :], hqT[:, u, c, :], wd[:, c, :], start=(c == 0), stop=(c == IC - 1))
                last.then_inc(y_done, 1)

            def step(n, u):
                if live(n + 1):
                    x_transposes(n + 1, 1 - u)
                if live(n):
                    gate_up(n, u)
                if live(n - 3):
                    down(n - 3, 1 - u)
                if live(n - 2):
                    h_transposes(n - 2, u)
            x_transposes(0, 0)
            schedule(pe, step)


def build(nc, a, out, stop=99):
    outer = ExitStack()
    with outer:
        sb = lambda n, s, d: outer.enter_context(nc.sbuf_tensor(n, s, d))
        per = {
            "x": sb("x", [P, T, D], F32), "st": sb("st", [P, T, 6], F32),
            "c32": sb("c32", [P, C32], F32), "c16": sb("c16", [P, C16], BF16),
            "mask_u8": sb("mask_u8", [P, T], U8), "mask": sb("mask", [P, T], F32),
            "coef": sb("coef", [P, T], F32),
            "gates_raw": sb("gates_raw", [P, 4], F32), "gates": sb("gates", [P, 4], F32),
        }
        qs = sb("qs", [P, B * H, S], BF16)
        ks = sb("ks", [P, B * H, S], BF16)
        arrived = {n: outer.enter_context(nc.semaphore("arrived_" + n)) for n in ("experts", "context", "weights")}
        with ExitStack() as inner:
            va = inner.enter_context(nc.sbuf_tensor("va", [P, STEPS, QT * G * (HD + 1)], F32))
            phase_prepare(nc, a, per, qs, ks, va)
            phase_attend(nc, a, per, qs, ks, va)
        att_norm = batch_norm_state(nc, outer, "_att", None)
        wabs = sb("wabs", [P, 3], F32)
        late = ks[:, :, :].rearrange("p h s -> p (h s)").bitcast(F32)
        cuts = [0, T * D, 2 * T * D, 2 * T * D + 4 * DC * D, 2 * T * D + 4 * DC * D + 6 * INNER]
        ctok, ctxT, wqv, w32 = (late[:, lo:hi] for lo, hi in zip(cuts, cuts[1:]))
        ctok = ctok.rearrange("p (t d) -> p t d", d=D)
        ctxT = ctxT.rearrange("p (c n) -> p c n", c=DC)
        wqv = wqv.rearrange("p (k c d) -> p k c d", k=4, c=DC)
        w32 = w32.rearrange("p (i n) -> p i n", i=3)
        with ExitStack() as ctx:
            sbb = lambda n, s, d: ctx.enter_context(nc.sbuf_tensor(n, s, d))
            up = sbb("up", [P, NX, 2, DC, P], F32)
            down = sbb("down", [P, NX, D], F32)
            loads = [(down[:, :, :], a["down"], arrived["experts"])]
            loads += [(up[:, e, :, :, :], a["up"][e], arrived["experts"]) for e in range(NX)]
            loads += [(ctxT, a["ctxTC"], arrived["context"]),
                      (ctok, a["ctx"].rearrange("b (q p) d -> p (b q) d", p=P), arrived["context"]),
                      (wqv, a["wqv"], arrived["context"])]
            loads += [(w32[:, i, :], a[n], arrived["weights"]) for i, n in enumerate(("wg", "wu", "wd"))]
            queries = qs[:, :, :].rearrange("p h s -> p (h s)").bitcast(F32)
            halves = queries.rearrange("p (s a d) -> p s a d", s=STEPS, d=D)
            moe = batch_norm_state(nc, ctx, "_moe", lambda t: halves[:, T // 2 + t // 2, 2 + t % 2, :])
            phase_project(nc, a, per, moe, qs, loads)
            if stop > 1:
                xT_all, scratch, x_parts, w_parts = carve(queries, [(DC, T * P), (4 * S,), (DC * T * P,),
                                                                    (E * 2 * DC * P,)])
                wjunk = queries[:, B * H * S // 2 - 2 * INNER:]
                nselT = sbb("nselT", [P, T * P], BF16)
                phase_experts(nc, a, per, moe, att_norm, xT_all, scratch, x_parts, w_parts, nselT, up, down,
                              w32, wjunk, wabs, arrived["experts"],
                              arrived["weights"])
        if stop > 2:
            with ExitStack() as ctx:
                sbc = lambda n, s, d: ctx.enter_context(nc.sbuf_tensor(n, s, d))
                wq16 = sbc("wq16", [P, 3, 2 * INNER], BF16)
                wstat = sbc("wstat", [P, 6], F32)
                free = qs[:, :, :].rearrange("p h s -> p (h s)").bitcast(F32)
                xn = free[:, B * H * S // 2 - T * D:].rearrange("p (t d) -> p t d", d=D)
                ffn = batch_norm_state(nc, ctx, "_ffn", lambda t: xn[:, t, :])
                phase_coattend(nc, a, per, att_norm, ffn, free, ctok, ctxT, wqv, w32, wabs, wq16, wstat,
                               arrived["context"])
                if stop > 3:
                    phase_bitffn(nc, per, ffn, xn, free, wq16, wstat, out)
        if stop <= 3:
            with ExitStack() as ctx:
                st = ctx.enter_context(nc.semaphore("st"))
                block = ctx.enter_context(nc.Block())

                @block.sync
                def _(sp):
                    sp.dma_start(out.rearrange("b (q p) d -> p (b q) d", p=P), per["x"][:, :, :]).then_inc(st, 16)
                    sp.wait_ge(st, 16)


def constants():
    import numpy as np

    c32 = np.zeros((P, C32), np.float32)
    c32[:, C_ID:C_ID + P] = np.eye(P)
    inv = (np.float32(1.0) / np.float32(10000.0) ** (np.arange(0, HD, 2, dtype=np.float32) / np.float32(HD)))
    f = np.outer(np.arange(S, dtype=np.float32), inv.astype(np.float32)).astype(np.float32)
    cos = np.cos(f.astype(np.float64)).astype(np.float32)
    sin = np.sin(f.astype(np.float64)).astype(np.float32)
    cos, sin = np.concatenate([cos, cos], -1), np.concatenate([-sin, sin], -1)
    c32[:, C_COS:C_SIN] = cos.reshape(QT, P, HD).transpose(1, 0, 2).reshape(P, -1)
    c32[:, C_SIN:C_TRI] = sin.reshape(QT, P, HD).transpose(1, 0, 2).reshape(P, -1)
    c32[:, C_TRI:C_TRI + E * E] = np.tril(np.ones((E, E)), -1).reshape(1, -1)
    c16 = np.zeros((P, C16), np.float32)
    c16[:, B_ID:B_ID + P] = np.eye(P)
    pre = np.zeros((2, H, XROWS), np.float32)
    pre[0, :, MASK_ROW] = 1.0
    for h in range(H):
        pre[1, h, 3 * (h % G):3 * (h % G) + 3] = 1.0
    c16[:, B_PRE:C16] = pre.reshape(1, -1)
    skip = np.zeros((P, E, P), np.float32)
    for e in range(E):
        skip[e, e, :] = -FAR
    bits = lambda v: (v.view(np.uint32) >> 16).astype(np.uint16)
    return c32, bits(c16), bits(skip)


def layout(inputs):
    import numpy as np

    i = {k: np.asarray(v) for k, v in inputs.items()}
    row = lambda v: np.ascontiguousarray(v).reshape(1, -1)
    chunks = lambda w: np.ascontiguousarray(w.reshape(-1, P, w.shape[-1]).transpose(1, 0, 2))
    a = {"x": i["x"], "ctx": i["ctx_1024"]}
    ctxT = i["ctx_1024"].reshape(T * P, D).T
    a["ctxTC"] = chunks(ctxT)
    a["ctxT"] = np.ascontiguousarray(ctxT.reshape(DC, P, T, P).transpose(2, 1, 0, 3))
    a["mask"] = np.ascontiguousarray(i["mask_BxS2_bf1"].reshape(T, P).T).view(np.uint8)
    a["gates"] = row(np.concatenate([i["g_xattn"], i["g_ffn"]]))
    a["wq"], a["wk"], a["wv"] = (chunks(i[f"L0_xattn_W{n}"].T) for n in "qkv")
    a["bqk"] = row(np.concatenate([i["L0_xattn_bq"], i["L0_xattn_bk"]]))
    a["bv"], a["bp"] = row(i["L0_xattn_bv"]), row(i["L0_xattn_bp"])
    a["wp"] = chunks(i["L0_xattn_Wp"].T)
    a["gate_w"] = chunks(i["L0_ffn_gate_w"].T)
    a["lb"] = row(i["L0_ffn_lb_bias"])
    gate = np.concatenate([i["L0_ffn_expert_gate_w"], i["L0_ffn_shared_gate_w"].reshape(SH, I, D)])
    up = np.concatenate([i["L0_ffn_expert_up_w"], i["L0_ffn_shared_up_w"].reshape(SH, I, D)])
    a["up"] = np.ascontiguousarray(np.stack([gate, up], 1).reshape(NX, 2, I, DC, P).transpose(0, 4, 1, 3, 2))
    down = np.concatenate([i["L0_ffn_expert_down_w"].transpose(2, 0, 1),
                           i["L0_ffn_shared_down_w"].T.reshape(SH, I, D).transpose(1, 0, 2)], 1)
    a["down"] = np.ascontiguousarray(down)
    ws = i["L1_xattn_w_sim"].reshape(3, DC, P)
    a["wsim"] = np.ascontiguousarray(ws[1:].transpose(2, 0, 1))
    a["w1"] = row(i["L1_xattn_w_sim"][:D])
    a["bsim"], a["bqv"] = row(i["L1_xattn_b_sim"]), row(i["L1_xattn_b_qv"])
    a["wqv"] = np.ascontiguousarray(i["L1_xattn_W_qv"].reshape(4, DC, P, D).transpose(2, 0, 1, 3))
    a["wg"], a["wu"], a["wd"] = (chunks(i[f"L1_ffn_w_{n}"].T).reshape(P, -1) for n in ("gate", "up", "down"))
    a["c32"], a["c16"], a["skip"] = constants()
    return a


def kernel(**inputs):
    import numpy as np
    import concourse.bacc as bacc
    from concourse.bass_utils import run_bass_kernel_spmd as run

    nc = bacc.Bacc("TRN2", target_bir_lowering=False, num_devices=1)
    arrays, args = {}, {}
    for name, v in layout(inputs).items():
        v = np.ascontiguousarray(v)
        arrays[f"in_{name}"] = v
        args[name] = nc.dram_tensor(f"in_{name}", v.shape, mybir.dt.from_np(v.dtype), kind="ExternalInput").ap()
    out = nc.dram_tensor("out", (B, S, D), F32, kind="ExternalOutput").ap()
    build(nc, args, out)
    return run(nc, [arrays], core_ids=[0]).results[0]["out"]
```
